# Optimizing a Trainium2 kernel written in Bass

```python
import numpy as np
import jax
import jax.numpy as jnp

def _softmax(x, axis=-1):
    return jax.nn.softmax(x, axis=axis)

def _gelu(x):
    return jax.nn.gelu(x, approximate=True)

def _silu(x):
    return jax.nn.silu(x)

def _sigmoid(x):
    return jax.nn.sigmoid(x)

def _layernorm(x, axis=-1, eps=1e-05):
    m = jnp.mean(x, axis=axis, keepdims=True)
    v = jnp.var(x, axis=axis, keepdims=True)
    return (x - m) / jnp.sqrt(v + eps)

def _scatter_add(tgt, idx, src, axis=0):
    return tgt.at[idx].add(src)

def _segment_sum(src, seg, n):
    return jax.ops.segment_sum(src, seg, n)
kernel_name = 'mk_flamingo_gated_d2_seqx_r8_ba0e2f'

def setup_inputs(seed: int=0):
    np.random.seed(seed)
    _w = jnp.asarray

    def _rec_inputs():
        import jax
        import jax.numpy as jnp
        _rk = jax.random.key(seed)
        x = 6.313e-05 + 0.9998 * jax.random.normal(jax.random.fold_in(_rk, 1), (8, 56, 128), jnp.float32)
        _lenS = 56 - jax.random.randint(jax.random.fold_in(_rk, 7), (8,), 0, max(1, 56 // 4) + 1, jnp.int32)
        _lenS2 = 1500 - jax.random.randint(jax.random.fold_in(_rk, 8), (8,), 0, max(1, 1500 // 4) + 1, jnp.int32)
        _ctx_1024P = jax.random.normal(jax.random.fold_in(_rk, 11), (8, 16, 128), jnp.float32)
        _ctx_1024c = jax.random.dirichlet(jax.random.fold_in(_rk, 511), 0.3 * jnp.ones((16,), jnp.float32), (8, 1500))
        _ctx_1024t = jnp.einsum('bsk,bkd->bsd', _ctx_1024c, _ctx_1024P)
        _ctx_1024t = _ctx_1024t * jax.lax.rsqrt(jnp.mean(jnp.square(_ctx_1024t)) + 1e-12) * 0.953939
        ctx_1024 = -0.000214406 + 1.00034 * (_ctx_1024t + 0.3 * jax.random.normal(jax.random.fold_in(_rk, 611), (8, 1500, 128), jnp.float32))
        _g = jax.random.normal(jax.random.fold_in(_rk, 9001), (2, 2), jnp.float32)
        _g = jnp.sign(_g) * jnp.maximum(jnp.abs(_g), 1.0) + (_g == 0) * 1.0
        g_xattn = _g[0]
        g_ffn = _g[1]
        return (x, ctx_1024, g_xattn, g_ffn)
    x, ctx_1024, g_xattn, g_ffn = _rec_inputs()

    def _L0_xattn_setup():
        import jax, jax.numpy as jnp
        import numpy as np
        from jax import lax
        BIG = jnp.float32(1e+30)

        def _pairwise_euclidean(a, b):
            aa = jnp.sum(a * a, axis=-1)[:, None]
            bb = jnp.sum(b * b, axis=-1)[None, :]
            ab = a @ b.T
            return jnp.sqrt(jnp.maximum(aa + bb - 2.0 * ab, 0.0))

        def _dtw_cost(D):
            row0 = jnp.cumsum(D[0])

            def row_step(prev_row, d_row):
                first = d_row[0] + prev_row[0]

                def col_step(left, inp):
                    d_ij, up, diag = inp
                    r = d_ij + jnp.minimum(jnp.minimum(up, left), diag)
                    return (r, r)
                _, rest = lax.scan(col_step, first, (d_row[1:], prev_row[1:], prev_row[:-1]))
                row = jnp.concatenate([first[None], rest])
                return (row, row)
            _, rows = lax.scan(row_step, row0, D[1:])
            return jnp.concatenate([row0[None], rows], axis=0)

        def _backtrack(R, T1, T2):
            L = T1 + T2 - 1

            def step(carry, _):
                i, j, done = carry
                valid = jnp.logical_not(done)
                cd = jnp.where((i > 0) & (j > 0), R[jnp.maximum(i - 1, 0), jnp.maximum(j - 1, 0)], BIG)
                cu = jnp.where(i > 0, R[jnp.maximum(i - 1, 0), j], BIG)
                cl = jnp.where(j > 0, R[i, jnp.maximum(j - 1, 0)], BIG)
                choice = jnp.argmin(jnp.stack([cd, cu, cl]))
                ni = jnp.where(choice <= 1, i - 1, i)
                nj = jnp.where((choice == 0) | (choice == 2), j - 1, j)
                at_origin = (i == 0) & (j == 0)
                ni = jnp.where(at_origin, 0, ni)
                nj = jnp.where(at_origin, 0, nj)
                return ((ni, nj, done | at_origin), (i, j, valid))
            init = (jnp.int32(T1 - 1), jnp.int32(T2 - 1), jnp.bool_(False))
            _, (i_idx, j_idx, valid) = lax.scan(step, init, None, length=L)
            return (i_idx, j_idx, valid)

        def _align_one(small, large):
            T_small, d = small.shape
            T_large = large.shape[0]
            D = _pairwise_euclidean(small, large)
            R = _dtw_cost(D)
            i_idx, j_idx, valid = _backtrack(R, T_small, T_large)
            contrib = small[i_idx] * valid[:, None].astype(small.dtype)
            expanded = jnp.zeros((T_large, d), dtype=small.dtype).at[j_idx].add(contrib)
            return expanded
        key = jax.random.key(seed)
        k1, k2 = jax.random.split(key)
        teacher = jax.random.normal(k1, (16, 50, 128), dtype=jnp.float32)
        student = jax.random.normal(k2, (16, 75, 128), dtype=jnp.float32)
        return {'teacher_features': teacher, 'student_features': student}
    _L0_xattn_all = _L0_xattn_setup()
    _L0_xattn_in = {k: v for k, v in _L0_xattn_all.items() if k in ()}
    del _L0_xattn_all

    def _L0_ffn_setup():
        import jax, jax.numpy as jnp
        import numpy as np
        DIM = 128
        HEADS = 8
        NUM_EXPERTS = 8192
        NUM_KEYS = 32
        DIM_KEY = 64
        PK_TOPK = 16
        FINAL_TOPK = 1
        BATCH, SEQ = (4, 256)
        key = jax.random.key(seed)
        k1, k2, k3, k4, k5 = jax.random.split(key, 5)
        x = jax.random.normal(k1, (BATCH, SEQ, DIM), jnp.float32)
        w_q = jax.random.normal(k2, (DIM, 2 * HEADS * DIM_KEY), jnp.float32) * 0.02
        keys = jax.random.normal(k3, (HEADS, NUM_KEYS, 2, DIM_KEY), jnp.float32) * 0.02
        w_down = jax.random.normal(k4, (NUM_EXPERTS, DIM), jnp.float32) * 0.02
        w_up = jax.random.normal(k5, (NUM_EXPERTS, DIM), jnp.float32) * 0.02
        return {'x': x, 'w_q': w_q, 'keys': keys, 'w_down': w_down, 'w_up': w_up}
    _L0_ffn_all = _L0_ffn_setup()
    _L0_ffn_in = {k: v for k, v in _L0_ffn_all.items() if k in ('w_q', 'keys', 'w_down', 'w_up')}
    del _L0_ffn_all

    def _L1_xattn_setup():
        import jax, jax.numpy as jnp
        import numpy as np
        NUM_HEADS = 16
        D_MODEL = 128
        HEAD_DIM = D_MODEL // NUM_HEADS
        B, S = (2, 256)
        key = jax.random.key(seed)
        ks = jax.random.split(key, 11)
        scale = 1.0 / np.sqrt(D_MODEL)
        inp = {'query': jax.random.normal(ks[0], (B, S, D_MODEL), jnp.float32), 'key': jax.random.normal(ks[1], (B, S, D_MODEL), jnp.float32), 'value': jax.random.normal(ks[2], (B, S, D_MODEL), jnp.float32), 'Wq': jax.random.normal(ks[3], (D_MODEL, D_MODEL), jnp.float32) * scale, 'bq': jnp.zeros((D_MODEL,), jnp.float32), 'Wk': jax.random.normal(ks[4], (D_MODEL, D_MODEL), jnp.float32) * scale, 'bk': jnp.zeros((D_MODEL,), jnp.float32), 'Wv': jax.random.normal(ks[5], (D_MODEL, D_MODEL), jnp.float32) * scale, 'bv': jnp.zeros((D_MODEL,), jnp.float32), 'Wo': jax.random.normal(ks[6], (D_MODEL, D_MODEL), jnp.float32) * scale, 'bo': jnp.zeros((D_MODEL,), jnp.float32)}
        return inp
    _L1_xattn_all = _L1_xattn_setup()
    _L1_xattn_in = {k: v for k, v in _L1_xattn_all.items() if k in ('Wq', 'bq', 'Wk', 'bk', 'Wv', 'bv', 'Wo', 'bo')}
    del _L1_xattn_all

    def _L1_ffn_setup():
        import jax, jax.numpy as jnp
        import numpy as np
        N_EMBD = 128
        NUM_EXPERTS = 8
        TOP_K = 2
        D_FF = 4 * N_EMBD
        B, S = (4, 256)
        key = jax.random.key(seed)
        ks = jax.random.split(key, 7)
        scale = lambda fan_in: 1.0 / np.sqrt(fan_in)
        x = jax.random.normal(ks[0], (B, S, N_EMBD), dtype=jnp.float32)
        W_router = jax.random.normal(ks[1], (N_EMBD, NUM_EXPERTS), dtype=jnp.float32) * scale(N_EMBD)
        b_router = jnp.zeros((NUM_EXPERTS,), dtype=jnp.float32)
        W1 = jax.random.normal(ks[2], (NUM_EXPERTS, N_EMBD, D_FF), dtype=jnp.float32) * scale(N_EMBD)
        b1 = jnp.zeros((NUM_EXPERTS, D_FF), dtype=jnp.float32)
        W2 = jax.random.normal(ks[3], (NUM_EXPERTS, D_FF, N_EMBD), dtype=jnp.float32) * scale(D_FF)
        b2 = jnpp = jnp.zeros((NUM_EXPERTS, N_EMBD), dtype=jnp.float32)
        return {'x': x, 'W_router': W_router, 'b_router': b_router, 'W1': W1, 'b1': b1, 'W2': W2, 'b2': b2}
    _L1_ffn_all = _L1_ffn_setup()
    _L1_ffn_in = {k: v for k, v in _L1_ffn_all.items() if k in ('W_router', 'b_router', 'W1', 'b1', 'W2', 'b2')}
    del _L1_ffn_all
    return {'x': x, 'ctx_1024': ctx_1024, 'g_xattn': g_xattn, 'g_ffn': g_ffn, 'L0_ffn_w_q': _L0_ffn_in['w_q'], 'L0_ffn_keys': _L0_ffn_in['keys'], 'L0_ffn_w_down': _L0_ffn_in['w_down'], 'L0_ffn_w_up': _L0_ffn_in['w_up'], 'L1_xattn_Wq': _L1_xattn_in['Wq'], 'L1_xattn_bq': _L1_xattn_in['bq'], 'L1_xattn_Wk': _L1_xattn_in['Wk'], 'L1_xattn_bk': _L1_xattn_in['bk'], 'L1_xattn_Wv': _L1_xattn_in['Wv'], 'L1_xattn_bv': _L1_xattn_in['bv'], 'L1_xattn_Wo': _L1_xattn_in['Wo'], 'L1_xattn_bo': _L1_xattn_in['bo'], 'L1_ffn_W_router': _L1_ffn_in['W_router'], 'L1_ffn_b_router': _L1_ffn_in['b_router'], 'L1_ffn_W1': _L1_ffn_in['W1'], 'L1_ffn_b1': _L1_ffn_in['b1'], 'L1_ffn_W2': _L1_ffn_in['W2'], 'L1_ffn_b2': _L1_ffn_in['b2']}

def reference(x, ctx_1024, g_xattn, g_ffn, L0_ffn_w_q, L0_ffn_keys, L0_ffn_w_down, L0_ffn_w_up, L1_xattn_Wq, L1_xattn_bq, L1_xattn_Wk, L1_xattn_bk, L1_xattn_Wv, L1_xattn_bv, L1_xattn_Wo, L1_xattn_bo, L1_ffn_W_router, L1_ffn_b_router, L1_ffn_W1, L1_ffn_b1, L1_ffn_W2, L1_ffn_b2):
    import jax
    import jax.numpy as jnp

    def _L0_xattn_ref(teacher_features, student_features):
        import jax, jax.numpy as jnp
        import numpy as np
        from jax import lax
        BIG = jnp.float32(1e+30)

        def _pairwise_euclidean(a, b):
            aa = jnp.sum(a * a, axis=-1)[:, None]
            bb = jnp.sum(b * b, axis=-1)[None, :]
            ab = a @ b.T
            return jnp.sqrt(jnp.maximum(aa + bb - 2.0 * ab, 0.0))

        def _dtw_cost(D):
            row0 = jnp.cumsum(D[0])

            def row_step(prev_row, d_row):
                first = d_row[0] + prev_row[0]

                def col_step(left, inp):
                    d_ij, up, diag = inp
                    r = d_ij + jnp.minimum(jnp.minimum(up, left), diag)
                    return (r, r)
                _, rest = lax.scan(col_step, first, (d_row[1:], prev_row[1:], prev_row[:-1]))
                row = jnp.concatenate([first[None], rest])
                return (row, row)
            _, rows = lax.scan(row_step, row0, D[1:])
            return jnp.concatenate([row0[None], rows], axis=0)

        def _backtrack(R, T1, T2):
            L = T1 + T2 - 1

            def step(carry, _):
                i, j, done = carry
                valid = jnp.logical_not(done)
                cd = jnp.where((i > 0) & (j > 0), R[jnp.maximum(i - 1, 0), jnp.maximum(j - 1, 0)], BIG)
                cu = jnp.where(i > 0, R[jnp.maximum(i - 1, 0), j], BIG)
                cl = jnp.where(j > 0, R[i, jnp.maximum(j - 1, 0)], BIG)
                choice = jnp.argmin(jnp.stack([cd, cu, cl]))
                ni = jnp.where(choice <= 1, i - 1, i)
                nj = jnp.where((choice == 0) | (choice == 2), j - 1, j)
                at_origin = (i == 0) & (j == 0)
                ni = jnp.where(at_origin, 0, ni)
                nj = jnp.where(at_origin, 0, nj)
                return ((ni, nj, done | at_origin), (i, j, valid))
            init = (jnp.int32(T1 - 1), jnp.int32(T2 - 1), jnp.bool_(False))
            _, (i_idx, j_idx, valid) = lax.scan(step, init, None, length=L)
            return (i_idx, j_idx, valid)

        def _align_one(small, large):
            T_small, d = small.shape
            T_large = large.shape[0]
            D = _pairwise_euclidean(small, large)
            R = _dtw_cost(D)
            i_idx, j_idx, valid = _backtrack(R, T_small, T_large)
            contrib = small[i_idx] * valid[:, None].astype(small.dtype)
            expanded = jnp.zeros((T_large, d), dtype=small.dtype).at[j_idx].add(contrib)
            return expanded
        return jax.vmap(_align_one)(teacher_features, student_features)

    def _L0_ffn_ref(x, w_q, keys, w_down, w_up):
        import jax, jax.numpy as jnp
        import numpy as np
        DIM = 128
        HEADS = 8
        NUM_EXPERTS = 8192
        NUM_KEYS = 32
        DIM_KEY = 64
        PK_TOPK = 16
        FINAL_TOPK = 1
        BATCH, SEQ = (4, 256)
        b, n, d = x.shape
        q = (x @ w_q).reshape(b, n, 2, HEADS, DIM_KEY).transpose(2, 0, 1, 3, 4)
        sim = jnp.einsum('pbnhd,hkpd->pbnhk', q, keys)
        vals, idx = jax.lax.top_k(sim, PK_TOPK)
        sx, sy = (vals[0], vals[1])
        ix, iy = (idx[0], idx[1])
        all_scores = (sx[..., :, None] + sy[..., None, :]).reshape(b, n, HEADS, PK_TOPK * PK_TOPK)
        all_indices = (ix[..., :, None] * NUM_KEYS + iy[..., None, :]).reshape(b, n, HEADS, PK_TOPK * PK_TOPK)
        scores, pk_indices = jax.lax.top_k(all_scores, FINAL_TOPK)
        indices = jnp.take_along_axis(all_indices, pk_indices, axis=-1)
        weights_down = w_down[indices]
        weights_up = w_up[indices]
        h = jnp.einsum('bnd,bnhkd->bnhk', x, weights_down)
        h = jax.nn.gelu(h, approximate=False)
        h = h * jax.nn.relu(scores)
        return jnp.einsum('bnhk,bnhkd->bnd', h, weights_up)

    def _L1_xattn_ref(query, key, value, Wq, bq, Wk, bk, Wv, bv, Wo, bo):
        import jax, jax.numpy as jnp
        import numpy as np
        NUM_HEADS = 16
        D_MODEL = 128
        HEAD_DIM = D_MODEL // NUM_HEADS
        B, S = (2, 256)
        b, s, _ = query.shape
        Q = query @ Wq + bq
        K = key @ Wk + bk
        V = value @ Wv + bv
        Q = Q.reshape(b, s, NUM_HEADS, HEAD_DIM).transpose(0, 2, 1, 3)
        K = K.reshape(b, -1, NUM_HEADS, HEAD_DIM).transpose(0, 2, 1, 3)
        V = V.reshape(b, -1, NUM_HEADS, HEAD_DIM).transpose(0, 2, 1, 3)
        scores = jnp.einsum('bhqd,bhkd->bhqk', Q, K) / jnp.sqrt(jnp.float32(HEAD_DIM)).astype(Q.dtype)
        attn = jax.nn.softmax(scores, axis=-1)
        ctx = jnp.einsum('bhqk,bhkd->bhqd', attn, V)
        ctx = ctx.transpose(0, 2, 1, 3).reshape(b, s, D_MODEL)
        return ctx @ Wo + bo

    def _L1_ffn_ref(x, W_router, b_router, W1, b1, W2, b2):
        import jax, jax.numpy as jnp
        import numpy as np
        N_EMBD = 128
        NUM_EXPERTS = 8
        TOP_K = 2
        D_FF = 4 * N_EMBD
        B, S = (4, 256)
        Bv, Sv, D = x.shape
        flat_x = x.reshape(-1, D)
        T = flat_x.shape[0]
        logits = flat_x @ W_router + b_router
        top_vals, top_idx = jax.lax.top_k(logits, TOP_K)
        neg_inf = jnp.full_like(logits, -jnp.inf)
        sparse_logits = neg_inf.at[jnp.arange(T)[:, None], top_idx].set(top_vals)
        router_weights = jax.nn.softmax(sparse_logits, axis=-1)
        final_output = jnp.zeros_like(flat_x)
        for e in range(NUM_EXPERTS):
            expert_mask = jnp.any(top_idx == e, axis=-1)
            h = jax.nn.relu(flat_x @ W1[e] + b1[e])
            y = h @ W2[e] + b2[e]
            w = router_weights[:, e] * expert_mask.astype(x.dtype)
            final_output = final_output + y * w[:, None]
        return final_output.reshape(Bv, Sv, D)
    x = x + jnp.tanh(g_xattn[0]) * _L0_xattn_ref(ctx_1024, _layernorm(x, axis=-1))
    x = x + jnp.tanh(g_ffn[0]) * _L0_ffn_ref(_layernorm(x, axis=-1), L0_ffn_w_q, L0_ffn_keys, L0_ffn_w_down, L0_ffn_w_up)
    x = x + jnp.tanh(g_xattn[1]) * _L1_xattn_ref(_layernorm(x, axis=-1), ctx_1024, ctx_1024, L1_xattn_Wq, L1_xattn_bq, L1_xattn_Wk, L1_xattn_bk, L1_xattn_Wv, L1_xattn_bv, L1_xattn_Wo, L1_xattn_bo)
    x = x + jnp.tanh(g_ffn[1]) * _L1_ffn_ref(_layernorm(x, axis=-1), L1_ffn_W_router, L1_ffn_b_router, L1_ffn_W1, L1_ffn_b1, L1_ffn_W2, L1_ffn_b2)
    return x

_drawn_inputs = setup_inputs


def setup_inputs(seed=0):
    import zlib

    import numpy as np

    out = dict(_drawn_inputs(seed))
    spreads = {'g_ffn': (-1.0, 0.6),
     'L1_xattn_bq': (0.0, 0.8),
     'L1_xattn_bk': (0.0, 2.0),
     'L1_xattn_bv': (0.0, 0.8),
     'L1_xattn_bo': (0.0, 2.0),
     'L1_ffn_b_router': (0.0, 0.8),
     'L1_ffn_b1': (0.0, 0.8),
     'L1_ffn_b2': (0.0, 2.0)}
    factors = {'L0_ffn_w_q': 8.0,
     'L0_ffn_keys': 8.0,
     'L0_ffn_w_down': 8.0,
     'L0_ffn_w_up': 8.0,
     'L1_xattn_Wq': 8.0,
     'L1_xattn_Wk': 8.0,
     'L1_xattn_Wv': 6.353,
     'L1_xattn_Wo': 6.01,
     'L1_ffn_W_router': 8.0,
     'L1_ffn_W1': 8.0,
     'L1_ffn_W2': 8.0}
    for name, (base, spread) in spreads.items():
        noise = np.random.default_rng([zlib.crc32(name.encode()), seed]).standard_normal(out[name].shape)
        drawn = base * np.exp(spread * noise) if base else spread * noise
        out[name] = jnp.asarray(drawn.astype(out[name].dtype))
    for name, factor in factors.items():
        out[name] = (out[name] * factor).astype(out[name].dtype)
    return out
```

```python
from contextlib import ExitStack

import concourse.bass as bass
from concourse import mybir

ALU = mybir.AluOpType
ACT = mybir.ActivationFunctionType
AX_X = mybir.AxisListType.X
F32 = mybir.dt.float32
BF16 = mybir.dt.bfloat16
I32 = mybir.dt.int32
U32 = mybir.dt.uint32

P = 128
BIG = 1.0e20
EPS = 1.0e-5


def view(ap, dims, offset=0):
    return bass.AP(tensor=ap.tensor, offset=ap.offset + offset, ap=[list(ap.ap[0])] + dims)


def build_gated_layers(nc, x, ctx_in, g_xattn, g_ffn, w_q, keys, w_tab, Wq, bq, Wk, bk, Wv, bv, Wo, bo,
                       W_router, b_router, W1, b1, W2, b2, out, stage=9):
    NB, NJ, D = x.shape
    NI = ctx_in.shape[1]
    TOK = NB * NJ
    LB = P // NB
    C = 100
    NS = NI // C
    assert NS * C == NI and NS < LB and D == P
    BS = LB * (NJ + NS - 2)
    STEPS = NJ + NS - 1
    PADJ = NS - 1
    JW = NJ + PADJ
    SLOT = C + 1
    PIECE = 500
    NPIECE = NI // PIECE
    SPP = PIECE // C
    TB = 5
    NTB = STEPS // TB
    assert NTB * TB == STEPS
    RING = 4
    DT_STEPS = PIECE // C
    JQ = NS * D + 3 * NS * NJ
    NHK, NK = keys.shape[0], keys.shape[1]
    FOLD = w_q.shape[1]
    NH = 16
    DH = D // NH
    HQ = NH * NJ
    NCH = -(-NI // P)
    VW = 6 * (3 * DH + 1)
    UNITS = NH // 2 * NPIECE
    MAXROW_AT = 9
    NE, F = W1.shape[0], W1.shape[2]
    TT = TOK // 4

    with ExitStack() as ctx:
        def sb(name, shape, dt=F32):
            return ctx.enter_context(nc.sbuf_tensor(name, shape, dt))

        def sem(name):
            return ctx.enter_context(nc.semaphore(name))

        banks = ctx.enter_context(nc.psum_tensor("banks", [P, 8, 512], F32))
        ps = [banks[:, i, :] for i in range(8)]

        ctxT = sb("ctxT", [P, NB * NI])
        N_DIST, N_NAT, N_JUMP, N_R = NB * BS + P, RING * NS * D, NJ * C, (STEPS + 1) * SLOT
        arena = sb("arena", [P, N_DIST + N_NAT + N_JUMP + N_R])
        o_nat, o_jump, o_R = N_DIST, N_DIST + N_NAT, N_DIST + N_NAT + N_JUMP
        dist = arena[0:C, 0:N_DIST]
        nat = arena[0:C, o_nat:o_jump].rearrange("c (r s d) -> c r s d", r=RING, s=NS)
        jump = arena[:, o_jump:o_R]
        R = arena[:, o_R:]
        N_B = TB * C
        work = sb("work", [P, 10 * N_B + TB * SLOT])
        mring = work[:, 0:2 * N_B]
        dts = work[:, 2 * N_B:4 * N_B]
        wk = [[work[:, (4 + 3 * a + i) * N_B:(5 + 3 * a + i) * N_B] for i in range(3)] for a in range(2)]
        gate = work[:, 10 * N_B:]
        taken = 0

        def later(rows, n, dt=F32):
            nonlocal taken
            words = n if dt == F32 else -(-n // 2)
            ap = work[0:rows, taken:taken + words]
            taken += words
            assert taken <= 10 * N_B + TB * SLOT
            return ap if dt == F32 else ap.bitcast(dt)

        twice1 = sb("twice1", [P, C])
        sq = jump[0:C, 0:NS * D]
        absum = jump[0:C, NS * D:NS * D + 2 * NS * NJ].rearrange("c (a n) -> c a n", a=2)
        dtmp = jump[0:C, NS * D + 2 * NS * NJ:NS * D + 3 * NS * NJ]
        aa = sb("aa", [C, NB, NS])
        bbB = jump[0:C, JQ:JQ + TOK]

        ident = sb("ident", [P, P])
        meanw = sb("meanw", [P, P])
        ones = sb("ones", [P, P])
        blk = sb("blk", [P, P])
        first = sb("first", [P, NB])
        pidx = sb("pidx", [P, 1], I32)
        lane_i = sb("lane_i", [P, 1], I32)
        lane = sb("lane", [P, 1])
        lmask = sb("lmask", [P, 4])
        twice = sb("twice", [P, C * 2])
        rowc2 = sb("rowc2", [C, NS])
        acc = sb("acc", [P, NJ])
        e_last = sb("e_last", [P, 1])
        hops = sb("hops", [P, 2, STEPS + 1])
        shf = sb("shf", [P, STEPS + 1])
        zt = mring[:, 0:NB * (NJ + 1)].rearrange("p (b j) -> p b j", b=NB)
        EB = work[0:C, 6 * N_B:6 * N_B + NB * (NJ + 1)].rearrange("c (b j) -> c b j", b=NB)
        Am = work[0:C, 5 * N_B:5 * N_B + NB * NJ].rearrange("c (a n) -> c a n", a=2)
        Pm = R[0:C, 0:NS * NB // 2 * NJ].rearrange("c (s n) -> c s n", s=NS)
        U = work[:, 8 * N_B:8 * N_B + NB // 2 * D].rearrange("p (t d) -> p t d", d=D)
        g4 = sb("g4", [P, 4])
        gt = sb("gt", [P, 4])
        x_tok = sb("x_tok", [TT, 4, D])
        xT = sb("xT", [P, TOK])
        xc = sb("xc", [P, TOK])
        xsq = sb("xsq", [P, TOK])
        rstd = sb("rstd", [P, TOK])
        xnT = sb("xnT", [P, TOK])
        xm2 = jump[:, JQ + TOK:JQ + 2 * TOK]
        epsc = sb("epsc", [P, 1])
        pad0 = sb("pad0", [P, 1])

        o_fold = N_R - 3 * FOLD
        wq_sb = R[:, o_fold:o_fold + FOLD]
        keyn = R[0:2 * NK, o_fold + FOLD:o_fold + 2 * FOLD].rearrange("k (c f) -> k c f", f=P)
        wqT = R[:, o_fold + 2 * FOLD:o_fold + 3 * FOLD]
        keyT = sb("keyT", [P, FOLD // 2])
        fold = sb("fold", [P, FOLD // 2])
        kiota = later(TT, 2 * NHK * NK)
        mxs = sb("mxs", [TT, 4, 2 * NHK])
        ixs = sb("ixs", [TT, 4, 2 * NHK])
        score = sb("score", [TT, 4, NHK])
        idxf = sb("idxf", [TT, 4, NHK])
        idx = sb("idx", [TT, 4 * NHK], U32)
        hcol = sb("hcol", [TT, 4, NHK])
        gath = arena[0:TT, 0:4 * NHK * 2 * D].rearrange("p (t h d) -> p t h d", t=4, h=NHK)
        prod = later(P, NHK * D)
        vals = arena[:, o_nat:o_nat + NCH * NB * VW + 32]
        o_att = o_nat + NCH * NB * VW + 32
        Pt = arena[:, o_att:o_att + 2 * HQ].rearrange("p (r n) -> p r n", r=2)
        Qb = arena[:, o_att + 2 * HQ:o_att + 4 * HQ].rearrange("p (r n) -> p r n", r=2)
        Wq_sb, Wk_sb, Wv_sb = later(P, D), later(P, D), later(P, D)
        WoAB = later(P, 2 * D).rearrange("p (a d) -> p a d", a=2)
        bvAB = sb("bvAB", [P, 2])
        cols = sb("cols", [P, 3])
        hm = sb("hm", [P, NH])
        QT = later(P, TOK)
        mx3 = sb("mx3", [2 * NJ, 2, NH // 2, NPIECE])
        nmx = sb("nmx", [2 * NJ, NH // 2])
        npart = sb("npart", [2 * NJ, NH // 2, 3], BF16)
        identb = later(P, P, BF16)
        NM = later(P, 2 * HQ, BF16).rearrange("p (r n) -> p r n", r=2)
        ones3 = later(P, P, BF16)
        Osb = arena[:, o_att + 4 * HQ:o_att + 4 * HQ + 6 * NJ]
        num = arena[:, o_att + 4 * HQ + 6 * NJ:o_att + 4 * HQ + 12 * NJ]
        OAB = arena[:, o_att + 4 * HQ + 12 * NJ:o_att + 4 * HQ + 12 * NJ + 2 * TOK].rearrange(
            "p (a n) -> p a n", a=2)
        assert o_att + 4 * HQ + 12 * NJ + 2 * TOK <= N_DIST + N_NAT + N_JUMP + N_R
        nd = later(P, 4 * NJ).rearrange("p (a n) -> p a n", a=2)
        mk = sb("mk", [P, 6])
        mku = sb("mku", [P, 2])
        sel = later(P, P)
        mk2 = sb("mk2", [P, 6])
        l32 = sb("l32", [P, 1])
        W1s = arena[:, 0:NE * F].rearrange("p (e f) -> p e f", e=NE)
        W2s = arena[:, NE * F:2 * NE * F].rearrange("p (u d) -> p u d", d=D)
        assert 2 * NE * F <= N_DIST
        Wr = sb("Wr", [P, NE])
        brB = sb("brB", [TT, NE])
        b1s = sb("b1s", [P, NE * F // P])
        b2s = sb("b2s", [P, NE])
        eiota = sb("eiota", [TT, 4, NE])
        lg = later(TT, 6 * 4 * NE).rearrange("p (i n) -> p i n", i=6)
        rs = sb("rs", [TT, 8, 4])
        wT = later(NE, TOK)
        sele = prod[0:NE, :].rearrange("p (e n) -> p e n", n=P)
        hT = arena[:, o_nat:o_nat + 4 * TOK].rearrange("p (r n) -> p r n", r=4)
        wBs = arena[:, o_nat + 4 * TOK:o_nat + 6 * TOK].rearrange("p (r n) -> p r n", r=2)

        s_x = sem("x_loaded")
        s_small = sem("small_loaded")
        s_nat = [sem(f"nat_loaded{r}") for r in range(NB)]
        s_nat2 = [sem(f"nat_again{b}") for b in range(NB)]
        s_pool = sem("pool_done")
        s_const = sem("constants_done")
        s_dve = sem("dve_done")
        s_act = sem("act_done")
        s_xT = sem("xT_transposed")
        s_xTe = sem("xT_copied")
        s_mean = sem("mean_ready")
        s_cen = sem("centred_squares_ready")
        s_var = sem("variance_ready")
        s_std = sem("deviation_ready")
        s_xn = sem("normalized_ready")
        s_bb = sem("query_norms_ready")
        s_bbe = sem("query_norms_copied")
        s_ct = sem("context_transposed")
        s_ctA = sem("context_copied_by_act")
        s_ctV = sem("context_copied_by_dve")
        s_sq = sem("context_squared")
        s_aa = sem("context_norms_ready")
        s_ab = sem("norm_sums_ready")
        s_dot = sem("dots_ready")
        s_d2 = sem("squared_distances_ready")
        s_dist = sem("distances_ready")
        s_dt = sem("distances_by_lane")
        s_dtc = sem("distances_by_lane_copied")
        s_scan = sem("column_scanned")
        s_jin = sem("jump_inputs_ready")
        s_sgn = sem("left_below_diagonal_ready")
        s_where = sem("where_to_ready")
        s_jump = sem("jumps_ready")
        s_carry = sem("carries_ready")
        s_desk = sem("jumps_deskewed")
        s_hit = sem("hit_ready")
        s_hop = sem("hop_ready")
        s_z = sem("hops_placed")
        s_eb = sem("hops_spread")
        s_pm = sem("path_masks_ready")
        s_ex = sem("rows_summed")
        s_u = sem("sums_copied")
        s_uT = sem("sums_transposed")
        s_gate = sem("gates_ready")
        s_natfree = sem("nat_used")
        s_out = sem("out_stored")

        s_tabs = sem("attention_tables_step")
        s_lane32 = sem("row_of_quarter_ready")
        s_et = sem("expert_tables_step")
        s_keyz = sem("key_tiles_zeroed")
        s_keys = sem("keys_loaded")
        s_foldT = sem("fold_inputs_transposed")
        s_foldc = sem("fold_inputs_copied")
        s_fold = sem("keys_folded")
        s_fold_sb = sem("folded_keys_copied")
        s_xr = sem("hidden_state_updated")
        s_xnk = sem("tokens_transposed")
        s_xnc = sem("tokens_copied")
        s_sim = sem("similarities_ready")
        s_picked = sem("similarities_used")
        s_idx = sem("experts_chosen")
        s_gath = [sem(f"rows_gathered{t}") for t in range(4)]
        s_hcol = sem("expert_dots_ready")
        s_gelu = sem("expert_gelu_ready")
        s_otok = sem("memory_output_ready")
        s_oT = sem("memory_output_transposed")
        s_wz = sem("weight_tiles_zeroed")
        s_w = sem("attention_weights_loaded")
        s_w12 = sem("expert_weights_loaded")
        s_tab = sem("attention_tables_ready")
        s_vp = sem("values_projected")
        s_vc = sem("values_copied")
        s_kp = sem("keys_projected")
        s_kc = sem("keys_copied")
        s_q = sem("queries_projected")
        s_qt = sem("queries_biased")
        s_qb = sem("query_blocks_ready")
        s_s1 = sem("row_scores_ready")
        s_mx = sem("row_scores_reduced")
        s_np = sem("negative_maxima_split")
        s_nmt = sem("negative_maxima_in_rows")
        s_nmc = sem("negative_maxima_copied")
        s_s2 = sem("column_scores_ready")
        s_exp = sem("probabilities_ready")
        s_pv = sem("values_weighted")
        s_oc = sem("head_sums_copied")
        s_den = sem("denominators_spread")
        s_ob = sem("heads_normalized")
        s_wo = sem("attention_output_ready")
        s_lg = sem("router_logits_ready")
        s_lgd = sem("logit_gap_ready")
        s_lge = sem("logit_gap_exponential")
        s_rw = sem("router_weights_ready")
        s_wtT = sem("router_weights_transposed")
        s_wtc = sem("router_weights_copied")
        s_wb = sem("router_weights_spread")
        s_wbc = sem("router_weights_spread_copied")
        s_h = sem("hidden_ready")
        s_hc = sem("hidden_copied")
        s_yu = sem("hidden_used")
        s_yc = sem("expert_output_added")
        s_fT = sem("output_transposed")
        s_fc = sem("output_copied")

        R_slot = lambda k, n, lo, cnt: view(R[:, :], [[SLOT, n], [1, cnt]], k * SLOT + lo)
        block = ctx.enter_context(nc.Block())

        @block.sync
        def _(sp):
            sp.dma_start(x_tok[:, :, :], x.rearrange("b j d -> (b j) d").rearrange("(t p) d -> p t d", t=4)
                         ).then_inc(s_x, 16)
            for b in range(NB):
                if b >= RING:
                    sp.wait_ge(s_ct, NPIECE * (b - RING + 1))
                    sp.wait_ge(s_sq, b - RING + 1)
                sp.dma_start(nat[:, b % RING, :, :], ctx_in[b].rearrange("(s c) d -> c s d", c=C)
                             ).then_inc(s_nat[b], 16)
            for b in range(RING):
                sp.wait_ge(s_ct, NPIECE * (b + RING + 1))
                sp.wait_ge(s_sq, b + RING + 1)
                sp.dma_start(nat[:, b, :, :], ctx_in[b].rearrange("(s c) d -> c s d", c=C)
                             ).then_inc(s_nat2[b], 16)
            sp.wait_ge(s_dt, NTB * TB // DT_STEPS)
            for b in range(RING, NB):
                o = (b - RING) * NS * D
                sp.dma_start(dist[:, o:o + NS * D].rearrange("c (s d) -> c s d", d=D),
                             ctx_in[b].rearrange("(s c) d -> c s d", c=C)).then_inc(s_nat2[b], 16)
            sp.wait_ge(s_carry, 1)
            for s in range(LB):
                sp.dma_start(view(jump[s:P - LB + s + 1:LB, :], [[1, NJ * C]]).rearrange("p (j c) -> p j c", c=C),
                             view(R[s:P - LB + s + 1:LB, :], [[SLOT, NJ], [1, C]], s * SLOT + 1)
                             ).then_inc(s_desk, 16)
            sp.wait_ge(s_keyz, 1)
            sp.dma_start(wq_sb[:, :], w_q[:, :]).then_inc(s_keys, 16)
            kv = keys.rearrange("(m a) k p f -> a p k m f", a=2)
            for a in range(2):
                for p in range(2):
                    sp.dma_start(keyn[NK * a:NK * (a + 1), 4 * p:4 * p + 4, 64 * a:64 * a + 64], kv[a, p]
                                 ).then_inc(s_keys, 16)
            sp.wait_ge(s_wz, 1)
            for dst, src in ((Wq_sb, Wq), (Wk_sb, Wk), (Wv_sb, Wv)):
                sp.dma_start(dst, src[:, :]).then_inc(s_w, 16)
            for i, src in enumerate((bq, bk, bo)):
                sp.dma_start(cols[:, i:i + 1], src.rearrange("(d a) -> d a", a=1)).then_inc(s_w, 16)
            G = 3 * DH
            for g in range(6):
                r = min(G, D - G * g)
                q, half = 32 * (g % 4), g // 4
                sp.dma_start(WoAB[q:q + r, half, :], Wo[G * g:G * g + r, :]).then_inc(s_w, 16)
                sp.dma_start(bvAB[q:q + r, half:half + 1], bv[G * g:G * g + r].rearrange("(d a) -> d a", a=1)
                             ).then_inc(s_w, 16)
            sp.dma_start(Wr[:, :], W_router[:, :]).then_inc(s_w, 16)
            sp.dma_start(brB[:, :], bass.AP(tensor=b_router.tensor, offset=0, ap=[[0, TT], [1, NE]])
                         ).then_inc(s_w, 16)
            sp.dma_start(b2s[:, :], b2.rearrange("e d -> d e"), allow_slow_non_contiguous=True).then_inc(s_w, 16)
            sp.dma_start(b1s[:, :], b1.rearrange("e (c p) -> p (e c)", p=P), allow_slow_non_contiguous=True
                         ).then_inc(s_w, 16)
            sp.wait_ge(s_otok, 4)
            sp.dma_start(W1s, W1.rearrange("e d f -> d e f")).then_inc(s_w12, 16)
            sp.dma_start(W2s, W2.rearrange("e (c p) d -> p (e c) d", p=P)).then_inc(s_w12, 16)
            sp.wait_ge(s_fc, 1)
            sp.dma_start(out.rearrange("b j d -> (b j) d").rearrange("(t p) d -> p t d", t=4),
                         x_tok[:, :, :]).then_inc(s_out, 16)
            sp.wait_ge(s_out, 16)

        @block.gpsimd
        def _(pool):
            n = 0

            def done(ins):
                nonlocal n
                n += 1
                ins.then_inc(s_pool, 1)

            done(nc.gpsimd.memset(ident[:, :], 0.0))
            done(nc.gpsimd.iota(pidx[:, :], [[1, 1]], base=0, channel_multiplier=1))
            done(nc.gpsimd.memset(first[:, :], 0.0))
            done(nc.gpsimd.memset(blk[:, :], 1.0))
            done(nc.gpsimd.iota(twice[:, :], [[1, 2 * C]], base=0, channel_multiplier=0,
                                allow_small_or_imprecise_dtypes=True))
            done(nc.gpsimd.iota(rowc2[:, :], [[2 * C, NS]], base=0, channel_multiplier=2,
                                allow_small_or_imprecise_dtypes=True))
            pool.wait_ge(s_pool, n)
            done(nc.gpsimd.affine_select(out=ident[:, :], in_=ident[:, :], compare_op=ALU.not_equal, fill=1.0,
                                         base=0, pattern=[[-1, P]], channel_multiplier=1))
            done(nc.gpsimd.affine_select(out=first[:, :], in_=first[:, :], compare_op=ALU.not_equal, fill=1.0,
                                         base=0, pattern=[[-LB, NB]], channel_multiplier=1))
            bv_ = blk[:, :].rearrange("p (b s) -> p b s", s=LB)
            done(nc.gpsimd.affine_select(out=bv_, in_=bv_, compare_op=ALU.is_ge, fill=0.0,
                                         base=0, pattern=[[-LB, NB], [0, LB]], channel_multiplier=1))
            pool.wait_ge(s_pool, n)
            nc.gpsimd.affine_select(out=bv_, in_=bv_, compare_op=ALU.is_ge, fill=0.0,
                                    base=LB - 1, pattern=[[LB, NB], [0, LB]], channel_multiplier=-1
                                    ).then_inc(s_const, 1)
            pool.wait_ge(s_bbe, 1)
            for b in range(NB):
                pool.wait_ge(s_aa, b + 1)
                if b >= 2:
                    pool.wait_ge(s_d2, b - 1)
                nc.gpsimd.tensor_tensor(
                    absum[:, b % 2, :].rearrange("c (s j) -> c s j", j=NJ),
                    aa[:, b, :].unsqueeze(2).broadcast_to([C, NS, NJ]),
                    bbB[:, b * NJ:(b + 1) * NJ].unsqueeze(1).broadcast_to([C, NS, NJ]), ALU.add).then_inc(s_ab, 1)
            pool.wait_ge(s_const, 3)
            three = lambda a: a.rearrange("p (t c) -> p t c", c=C)

            def where_to(k):
                pool.wait_ge(s_sgn, k + 1)
                nc.gpsimd.tensor_tensor(three(wk[k % 2][2][:, :]), view(twice1[:, :], [[0, TB], [1, C]]),
                                        three(wk[k % 2][0][:, :]), ALU.add).then_inc(s_where, 1)

            for k in range(NTB):
                pool.wait_ge(s_scan, TB * (k + 1))
                if k >= 2:
                    pool.wait_ge(s_jump, k - 1)
                t = k * TB
                nc.gpsimd.tensor_tensor(three(wk[k % 2][0][:, :]), R_slot(t, TB, 1, C), R_slot(t, TB, 0, C),
                                        ALU.subtract).then_inc(s_jin, 1)
                nc.gpsimd.tensor_tensor(
                    three(wk[k % 2][1][:, :]), R_slot(t + 1, TB, 0, C),
                    three(mring[:, (k % 2) * TB * C:(k % 2 + 1) * TB * C]), ALU.subtract).then_inc(s_jin, 1)
                if k >= 1:
                    where_to(k - 1)
            where_to(NTB - 1)
            pool.wait_ge(s_desk, 16 * LB)
            nc.gpsimd.memset(keyn, 0.0).then_inc(s_keyz, 1)
            pool.wait_ge(s_uT, 1)
            nc.gpsimd.iota(kiota, [[0, 2 * NHK], [1, NK]], base=-NK, channel_multiplier=0,
                           allow_small_or_imprecise_dtypes=True)
            nc.gpsimd.memset(bvAB[:, :], 0.0)
            nc.gpsimd.memset(WoAB, 0.0).then_inc(s_wz, 1)
            for t in range(4):
                pool.wait_ge(s_idx, 1)
                for h in range(NHK):
                    c = t * NHK + h
                    nc.gpsimd.indirect_dma_start(
                        out=gath[:, t, h, :], out_offset=None, in_=w_tab[:, :],
                        in_offset=bass.IndirectOffsetOnAxis(ap=idx[:, c:c + 1], axis=0)).then_inc(s_gath[t], 16)
            n = 0
            s_t = s_tabs
            done2 = lambda ins: ins.then_inc(s_t, 1)
            done2(nc.gpsimd.memset(hm[:, :], 1.0))
            done2(nc.gpsimd.memset(mk[:, :], 1.0))
            done2(nc.gpsimd.memset(sel, 0.0))
            done2(nc.gpsimd.memset(ones3, 0.0))
            done2(nc.gpsimd.memset(NM, 0.0))
            done2(nc.gpsimd.memset(identb, 0.0))
            pool.wait_ge(s_t, 6)
            done2(nc.gpsimd.affine_select(out=hm[:, :], in_=hm[:, :], compare_op=ALU.is_ge, fill=0.0, base=0,
                                          pattern=[[-DH, NH]], channel_multiplier=1))
            selv = sel.rearrange("p (t m) -> p t m", m=32)
            done2(nc.gpsimd.affine_select(out=selv, in_=selv, compare_op=ALU.not_equal, fill=1.0, base=-3 * DH,
                                          pattern=[[-32, 4], [0, 32]], channel_multiplier=1))
            done2(nc.gpsimd.affine_select(out=identb, in_=identb, compare_op=ALU.not_equal, fill=1.0, base=0,
                                          pattern=[[-1, P]], channel_multiplier=1))
            done2(nc.gpsimd.memset(ones3[0:3, :], 1.0))
            pool.wait_ge(s_t, 10)
            done2(nc.gpsimd.affine_select(out=hm[:, :], in_=hm[:, :], compare_op=ALU.is_ge, fill=0.0, base=DH - 1,
                                          pattern=[[DH, NH]], channel_multiplier=-1))
            pool.wait_ge(s_t, 11)
            pool.wait_ge(s_lane32, 1)
            for i in range(3):
                for half in range(2):
                    done2(nc.gpsimd.tensor_scalar(mk[:, 3 * half + i:3 * half + i + 1], l32[:, :], float(DH * i), None,
                                                  ALU.is_ge))
                    done2(nc.gpsimd.tensor_scalar(mk2[:, 3 * half + i:3 * half + i + 1], l32[:, :],
                                                  float(DH * (i + 1)), None, ALU.is_lt))
            pool.wait_ge(s_t, 23)
            done2(nc.gpsimd.tensor_tensor(mk[:, :], mk[:, :], mk2[:, :], ALU.mult))
            pool.wait_ge(s_t, 24)
            done2(nc.gpsimd.memset(mk[32:64, 4:6], 0.0))
            done2(nc.gpsimd.memset(mk[64:P, 3:6], 0.0))
            pool.wait_ge(s_t, 26)
            done2(nc.gpsimd.tensor_tensor(mku[:, :], mk[:, 0:6:3], mk[:, 1:6:3], ALU.add))
            pool.wait_ge(s_t, 27)
            done2(nc.gpsimd.tensor_tensor(mku[:, :], mku[:, :], mk[:, 2:6:3], ALU.add))
            pool.wait_ge(s_t, 28)
            done2(nc.gpsimd.tensor_scalar(mku[:, :], mku[:, :], -1.0, 1.0, ALU.mult, ALU.add))
            pool.wait_ge(s_ex, 2)
            vt = vals[:, 0:NCH * NB * VW].rearrange("p (c g w) -> p c g w", g=6, w=3 * DH + 1)
            done2(nc.gpsimd.memset(vt[:, :, 5, DH:3 * DH], 0.0))
            done2(nc.gpsimd.memset(vt[:, :, :, 3 * DH], 1.0))
            done2(nc.gpsimd.memset(vals[:, NCH * NB * VW:], 0.0))
            done2(nc.gpsimd.memset(Osb, 0.0))
            done2(nc.gpsimd.memset(vt[:, NCH - 1::NCH, 0, 0:7], 0.0))
            pool.wait_ge(s_t, 34)
            for b in range(NB):
                pool.wait_ge(s_qt, 1)
                if b >= 2:
                    pool.wait_ge(s_s2, NCH * (b - 1))
                nc.gpsimd.tensor_tensor(
                    Qb[:, b % 2, :].rearrange("p (h q) -> p h q", q=NJ),
                    QT[:, b * NJ:(b + 1) * NJ].unsqueeze(1).broadcast_to([P, NH, NJ]),
                    hm[:, :].unsqueeze(2).broadcast_to([P, NH, NJ]), ALU.mult).then_inc(s_qb, 1)
            pool.wait_ge(s_otok, 4)
            nc.gpsimd.iota(eiota[:, :, :], [[0, 4], [1, NE]], base=-NE, channel_multiplier=0,
                           allow_small_or_imprecise_dtypes=True).then_inc(s_et, 1)
            nc.gpsimd.memset(prod[0:NE, :], 0.0).then_inc(s_et, 1)
            pool.wait_ge(s_et, 2)
            nc.gpsimd.affine_select(out=sele, in_=sele, compare_op=ALU.not_equal, fill=1.0, base=0,
                                    pattern=[[-1, NE], [0, P]], channel_multiplier=1).then_inc(s_et, 1)

        @block.scalar
        def _(act):
            act.dma_start(g4[:, 0:2], bass.AP(tensor=g_xattn.tensor, offset=0, ap=[[0, P], [1, 2]])
                          ).then_inc(s_small, 16)
            act.dma_start(g4[:, 2:4], bass.AP(tensor=g_ffn.tensor, offset=0, ap=[[0, P], [1, 2]])
                          ).then_inc(s_small, 16)
            act.wait_ge(s_small, 32)
            nc.scalar.activation(gt[:, :], g4[:, :], ACT.Tanh).then_inc(s_gate, 1)
            act.wait_ge(s_xT, 1)
            nc.scalar.activation(xT[:, :], ps[0][:, 0:TOK], ACT.Copy).then_inc(s_xTe, 1)
            act.wait_ge(s_var, 1)
            act.wait_ge(s_const, 3)
            nc.scalar.activation(rstd[:, :], ps[0][:, 0:TOK], ACT.Sqrt, bias=epsc[:, 0:1]).then_inc(s_std, 1)

            def dist_of(b):
                act.wait_ge(s_d2, b + 1)
                nc.scalar.activation(view(dist[:, :], [[JW, NS], [1, NJ]], b * BS + PADJ),
                                     dtmp[:, :].rearrange("c (s j) -> c s j", j=NJ), ACT.Sqrt
                                     ).then_inc(s_dist, 1)

            for b in range(NB):
                act.wait_ge(s_nat[b], 16)
                if b >= 1:
                    act.wait_ge(s_aa, b)
                nc.scalar.activation(sq[:, :], nat[:, b % RING, :, :].rearrange("c s d -> c (s d)"), ACT.Square
                                     ).then_inc(s_sq, 1)
                for n in range(NPIECE - 1):
                    act.wait_ge(s_ct, NPIECE * b + n + 1)
                    nc.scalar.activation(ctxT[:, b * NI + n * PIECE:b * NI + (n + 1) * PIECE],
                                         ps[1 + n][:, 0:PIECE], ACT.Copy).then_inc(s_ctA, 1)
                if b >= 1:
                    dist_of(b - 1)
            dist_of(NB - 1)

            def lane_distances(q):
                act.wait_ge(s_dt, q + 1)
                if q >= 2:
                    act.wait_ge(s_scan, DT_STEPS * (q - 1))
                nc.scalar.activation(dts[:, (q % 2) * PIECE:(q % 2 + 1) * PIECE], ps[q % 2][:, 0:PIECE],
                                     ACT.Copy).then_inc(s_dtc, 1)

            lane_distances(0)
            lane_distances(1)
            for k in range(NTB):
                if k + 2 < NTB:
                    lane_distances(k + 2)
                h, g = wk[k % 2][0], wk[k % 2][1]
                act.wait_ge(s_jin, 2 * k + 1)
                nc.scalar.activation(h[:, :], h[:, :], ACT.Sign, scale=-1.0).then_inc(s_act, 1)
                act.wait_ge(s_act, 2 * k + 1)
                nc.scalar.activation(h[:, :], h[:, :], ACT.Relu).then_inc(s_sgn, 1)
                act.wait_ge(s_jin, 2 * k + 2)
                nc.scalar.activation(g[:, :], g[:, :], ACT.Copy, scale=1.0e14, bias=1.0).then_inc(s_act, 1)
            act.wait_ge(s_foldT, 1)
            nc.scalar.activation(wqT[:, 0:FOLD // 2], ps[1], ACT.Copy)
            nc.scalar.activation(wqT[:, FOLD // 2:], ps[2], ACT.Copy)
            nc.scalar.activation(keyT[:, :], ps[7], ACT.Copy).then_inc(s_foldc, 1)
            for half in range(2):
                act.wait_ge(s_ex, half + 1)
                for par in range(2):
                    nc.scalar.activation(U[64 * par:64 * par + NJ, 2 * half:2 * half + 2, :],
                                         ps[6 + half][64 * par:64 * par + NJ, 0:2 * D].rearrange(
                                             "p (t d) -> p t d", d=D), ACT.Copy).then_inc(s_u, 1)
                if half == 0:
                    act.wait_ge(s_fold, 1)
                    nc.scalar.activation(fold[:, :], ps[1], ACT.Copy).then_inc(s_fold_sb, 1)

            def deviation(k):
                act.wait_ge(s_var, k + 1)
                nc.scalar.activation(rstd[:, :], ps[0][:, 0:TOK], ACT.Sqrt, bias=epsc[:, 0:1]).then_inc(s_std, 1)

            deviation(1)
            act.wait_ge(s_xnk, 1)
            nc.scalar.activation(x_tok[:, :, :], ps[4][0:TT, :].rearrange("p (t d) -> p t d", d=D), ACT.Copy
                                 ).then_inc(s_xnc, 1)
            if stage >= 3:
                act.wait_ge(s_tabs, 34)
                for b in range(NB):
                    for i in range(NCH // 4):
                        n = b * (NCH // 4) + i
                        act.wait_ge(s_vp, n + 1)
                        tail = NI - (NCH - 1) * P if i == NCH // 4 - 1 else P
                        for r, c0, c1 in ((P, 0, 4),) if tail == P else ((P, 0, 3), (tail, 3, 4)):
                            dst = vals[0:r, (b * NCH + 4 * i + c0) * VW:(b * NCH + 4 * i + c1) * VW].rearrange(
                                "p (c g w) -> p c g w", g=6, w=3 * DH + 1)
                            src = ps[4 + n % 2][0:r, c0 * D:c1 * D].rearrange("p (c d) -> p c d", d=D)
                            for k in range(c1 - c0):
                                nc.scalar.activation(dst[:, k, 0:5, 0:3 * DH],
                                                     src[:, k, 0:15 * DH].rearrange("p (g w) -> p g w", g=5),
                                                     ACT.Copy)
                            last = nc.scalar.activation(dst[:, :, 5, 0:DH], src[:, :, 15 * DH:], ACT.Copy)
                        last.then_inc(s_vc, 1)
                    for i in range(NPIECE):
                        n = b * NPIECE + i
                        act.wait_ge(s_kp, n + 1)
                        nc.scalar.activation(ctxT[:, b * NI + i * PIECE:b * NI + (i + 1) * PIECE],
                                             ps[6 + n % 2][:, 0:PIECE], ACT.Identity, bias=cols[:, 1:2]
                                             ).then_inc(s_kc, 1)
            for t in range(4):
                act.wait_ge(s_hcol, t + 1)
                nc.scalar.activation(hcol[:, t, :], hcol[:, t, :], ACT.Gelu).then_inc(s_gelu, 1)
            if stage >= 3:
                deviation(2)

                def maxima_rows(b):
                    for half in range(2):
                        act.wait_ge(s_nmt, b + 1)
                        last = nc.scalar.activation(NM[0:3, b % 2, half * HQ // 2:(half + 1) * HQ // 2],
                                                    ps[7][32 * half:32 * half + 3, 0:HQ // 2], ACT.Copy)
                    last.then_inc(s_nmc, 1)

                def head_sums(b):
                    act.wait_ge(s_pv, NCH * (b + 1))
                    if b >= 1:
                        act.wait_ge(s_ob, b)
                    nc.scalar.activation(Osb[:, 0:3 * NJ], ps[6][:, 0:3 * NJ], ACT.Copy)
                    nc.scalar.activation(Osb[0:32, 3 * NJ:6 * NJ], ps[6][0:32, 3 * NJ:6 * NJ], ACT.Copy)
                    nc.scalar.activation(Osb[32:64, 3 * NJ:4 * NJ], ps[6][32:64, 3 * NJ:4 * NJ], ACT.Copy
                                         ).then_inc(s_oc, 1)

                maxima_rows(0)
                for b in range(NB):
                    for c in range(NCH):
                        g = b * NCH + c
                        rows = min(P, NI - c * P)
                        act.wait_ge(s_s2, g + 1)
                        if g >= 2:
                            act.wait_ge(s_pv, g - 1)
                        nc.scalar.activation(
                            Pt[0:rows, g % 2, :].rearrange("p (a n) -> p a n", a=2),
                            banks[0:rows, 2 + 2 * (g % 2):4 + 2 * (g % 2), 0:HQ // 2], ACT.Exp,
                            scale=float(DH) ** -0.5).then_inc(s_exp, 1)
                        if c == 1 and b >= 1:
                            head_sums(b - 1)
                        if c == MAXROW_AT + 1 and b + 1 < NB:
                            maxima_rows(b + 1)
                head_sums(NB - 1)
            if stage >= 4:
                deviation(3)
                act.wait_ge(s_lgd, 1)
                nc.scalar.activation(rs[:, 5, :], rs[:, 4, :], ACT.Exp).then_inc(s_lge, 1)
                act.wait_ge(s_wtT, 1)
                nc.scalar.activation(wT, ps[2][0:NE, 0:TOK], ACT.Copy).then_inc(s_wtc, 1)

                def hidden(i):
                    act.wait_ge(s_h, i + 1)
                    if i >= 4:
                        act.wait_ge(s_yu, i - 3)
                    nc.scalar.activation(hT[:, i % 4, :], ps[5 + i % 2][:, 0:TOK], ACT.Relu, bias=b1s[:, i:i + 1]
                                         ).then_inc(s_hc, 1)

                FC = F // P
                for e in range(NE):
                    hidden(FC * e)
                    hidden(FC * e + 1)
                    act.wait_ge(s_wb, e + 1)
                    if e >= 2:
                        act.wait_ge(s_yc, e - 1)
                    nc.scalar.activation(wBs[:, e % 2, :], ps[3 + e % 2][:, 0:TOK], ACT.Copy).then_inc(s_wbc, 1)
                    for i in range(2, FC):
                        hidden(FC * e + i)
            act.wait_ge(s_fT, 1)
            nc.scalar.activation(x_tok[:, :, :], ps[1][0:TT, :].rearrange("p (t d) -> p t d", d=D), ACT.Copy
                                 ).then_inc(s_fc, 1)

        @block.vector
        def _(ve):
            n = 0

            def link(ins):
                nonlocal n
                n += 1
                ins.then_inc(s_dve, 1)
                ve.wait_ge(s_dve, n)

            nc.vector.memset(meanw[:, :], 1.0 / D)
            nc.vector.memset(ones[:, :], 1.0)
            nc.vector.memset(epsc[:, :], EPS)
            nc.vector.memset(e_last[:, :], 2.0 * (NI - 1))
            nc.vector.memset(view(dist[:, :], [[BS, NB], [JW, NS], [1, PADJ]]), BIG)
            nc.vector.memset(view(dist[:, :], [[BS, NB], [1, BS - NS * JW]], NS * JW), BIG)
            nc.vector.memset(dist[:, NB * BS:NB * BS + P], BIG)
            link(nc.vector.memset(gate[:, :], 1.0))
            nc.vector.memset(pad0[:, :], 0.0).then_inc(s_const, 1)
            ve.wait_ge(s_pool, 6)
            link(nc.vector.tensor_scalar(lane_i[:, :], pidx[:, :], LB - 1, None, ALU.bitwise_and))
            link(nc.vector.tensor_copy(lane[:, :], lane_i[:, :]))
            link(nc.vector.tensor_scalar(lane_i[:, :], pidx[:, :], 31, None, ALU.bitwise_and))
            nc.vector.tensor_copy(l32[:, :], lane_i[:, :]).then_inc(s_lane32, 1)
            for i in range(4):
                nc.vector.tensor_scalar(lmask[:, i:i + 1], lane[:, :], float(1 << i), None, ALU.is_ge)
            nc.vector.memset(view(gate[:, :], [[SLOT, TB], [1, 1]]), 0.0)
            link(nc.vector.memset(R[:, 0:SLOT], BIG))
            link(nc.vector.tensor_scalar(R[:, 0:1], lane[:, :], 0.0, BIG, ALU.is_gt, ALU.mult))
            nc.vector.scalar_tensor_tensor(out=twice[:, :], in0=lane[:, 0:1].broadcast_to([P, 2 * C]),
                                           scalar=2.0 * C, in1=twice[:, :], op0=ALU.mult, op1=ALU.add
                                           ).then_inc(s_dve, 1)
            n += 1
            ve.wait_ge(s_dve, n)
            nc.vector.tensor_scalar(twice1[:, :], view(twice[:, :], [[2, C]]), -1.0, None, ALU.add
                                    ).then_inc(s_const, 1)

            def layernorm(k):
                ve.wait_ge(s_mean, k + 1)
                link(nc.vector.tensor_tensor(xc[:, :], xT[:, :], ps[0][:, 0:TOK], ALU.subtract))
                nc.vector.tensor_tensor(xsq[:, :], xc[:, :], xc[:, :], ALU.mult).then_inc(s_cen, 1)
                ve.wait_ge(s_std, k + 1)
                link(nc.vector.reciprocal(rstd[:, :], rstd[:, :]))
                nc.vector.tensor_tensor(xnT[:, :], xc[:, :], rstd[:, :], ALU.mult).then_inc(s_xn, 1)
                ve.wait_ge(s_xn, k + 1)

            layernorm(0)
            nc.vector.tensor_scalar(xm2[:, :], xnT[:, :], -2.0, None, ALU.mult)
            nc.vector.tensor_tensor(xsq[:, :], xnT[:, :], xnT[:, :], ALU.mult).then_inc(s_cen, 1)
            ve.wait_ge(s_bb, 1)
            nc.vector.tensor_copy(bbB[:, :], ps[0][0:C, 0:TOK]).then_inc(s_bbe, 1)

            def d2_of(b):
                ve.wait_ge(s_dot, b + 1)
                ve.wait_ge(s_ab, b + 1)
                if b >= 1:
                    ve.wait_ge(s_dist, b)
                for part, (lo, hi) in enumerate(((0, 8), (8, NS))):
                    bank = ps[4 + 2 * (b % 2) + part]
                    last = nc.vector.tensor_tensor(dtmp[:, lo * NJ:hi * NJ], bank[0:C, 0:(hi - lo) * NJ],
                                                   absum[:, b % 2, lo * NJ:hi * NJ], ALU.add)
                link(last)
                nc.vector.tensor_scalar(dtmp[:, :], dtmp[:, :], 0.0, None, ALU.max).then_inc(s_d2, 1)

            for b in range(NB):
                ve.wait_ge(s_sq, b + 1)
                nc.vector.tensor_reduce(aa[:, b, :], sq[:, :].rearrange("c (s d) -> c s d", d=D), AX_X, ALU.add
                                        ).then_inc(s_aa, 1)
                ve.wait_ge(s_ct, NPIECE * (b + 1))
                nc.vector.tensor_copy(ctxT[:, b * NI + 2 * PIECE:(b + 1) * NI], ps[3][:, 0:PIECE]
                                      ).then_inc(s_ctV, 1)
                if b >= 1:
                    d2_of(b - 1)
            d2_of(NB - 1)

            def memory_layer():
                layernorm(1)
                ve.wait_ge(s_wz, 1)
                for t in range(4):
                    ve.wait_ge(s_sim, t + 1)
                    sims = ps[t][0:TT, :].rearrange("p (g k) -> p g k", k=NK)
                    eq = prod[0:TT, 0:2 * NHK * NK]
                    eq3 = eq.rearrange("p (g k) -> p g k", k=NK)
                    link(nc.vector.tensor_reduce(mxs[:, t, :], sims, AX_X, ALU.max))
                    link(nc.vector.tensor_tensor(eq3, sims, mxs[:, t, :].unsqueeze(2).broadcast_to(
                        [TT, 2 * NHK, NK]), ALU.is_equal))
                    link(nc.vector.tensor_tensor(eq, eq, kiota, ALU.mult))
                    link(nc.vector.tensor_reduce(ixs[:, t, :], eq3, AX_X, ALU.min))
                nc.vector.tensor_tensor(score[:, :, :], mxs[:, :, 0:NHK], mxs[:, :, NHK:], ALU.add)
                link(nc.vector.scalar_tensor_tensor(out=idxf[:, :, :], in0=ixs[:, :, 0:NHK], scalar=float(NK),
                                                    in1=ixs[:, :, NHK:], op0=ALU.mult, op1=ALU.add))
                nc.vector.tensor_scalar(idx[:, :], idxf[:, :, :].rearrange("p t h -> p (t h)"),
                                        float(NK * NK + NK), None, ALU.add).then_inc(s_idx, 1)
                link(nc.vector.tensor_scalar(score[:, :, :], score[:, :, :], 0.0, None, ALU.max))
                ve.wait_ge(s_xnc, 1)
                pr = prod[0:TT, :].rearrange("p (h d) -> p h d", d=D)

                def down(t):
                    ve.wait_ge(s_gath[t], 16 * NHK)
                    link(nc.vector.tensor_tensor(pr, gath[:, t, :, 0:D], x_tok[:, t, :].unsqueeze(1).broadcast_to(
                        [TT, NHK, D]), ALU.mult))
                    nc.vector.tensor_reduce(hcol[:, t, :], pr, AX_X, ALU.add).then_inc(s_hcol, 1)
                    ve.wait_ge(s_hcol, t + 1)

                def up(t):
                    ve.wait_ge(s_gelu, t + 1)
                    link(nc.vector.tensor_tensor(hcol[:, t, :], hcol[:, t, :], score[:, t, :], ALU.mult))
                    link(nc.vector.tensor_tensor(pr, gath[:, t, :, D:], hcol[:, t, :].unsqueeze(2).broadcast_to(
                        [TT, NHK, D]), ALU.mult))
                    nc.vector.tensor_reduce(x_tok[:, t, :], view(prod[0:TT, :], [[1, D], [D, NHK]]), AX_X, ALU.add
                                            ).then_inc(s_otok, 1)
                    ve.wait_ge(s_otok, t + 1)

                down(0)
                for t in range(1, 4):
                    down(t)
                    up(t - 1)
                up(3)
                ve.wait_ge(s_oT, 1)
                nc.vector.scalar_tensor_tensor(out=xT[:, :], in0=ps[0][:, 0:TOK], scalar=gt[:, 2:3],
                                               in1=xT[:, :], op0=ALU.mult, op1=ALU.add).then_inc(s_xr, 1)
                ve.wait_ge(s_xr, 2)

            def attention_layer():
                layernorm(2)
                ve.wait_ge(s_q, 1)
                nc.vector.tensor_scalar(QT, ps[1][:, 0:TOK], cols[:, 0:1], None, ALU.add).then_inc(s_qt, 1)

                def reduce_scores(b, u):
                    k = b * UNITS + u
                    ve.wait_ge(s_s1, k + 1)
                    nc.vector.tensor_reduce(mx3[:, b % 2, u // NPIECE, u % NPIECE:u % NPIECE + 1],
                                            ps[k % 2][0:2 * NJ, 0:PIECE], AX_X, ALU.max).then_inc(s_mx, 1)

                def split_maxima(b):
                    ve.wait_ge(s_mx, UNITS * (b + 1))
                    if b >= 1:
                        ve.wait_ge(s_nmt, b)
                    link(nc.vector.tensor_reduce(nmx[:, :], mx3[:, b % 2, :, :], AX_X, ALU.max))
                    link(nc.vector.tensor_scalar(nmx[:, :], nmx[:, :], -1.0, None, ALU.mult))
                    for i in range(3):
                        link(nc.vector.tensor_copy(npart[:, :, i], nmx[:, :]))
                        if i < 2:
                            link(nc.vector.tensor_tensor(nmx[:, :], nmx[:, :], npart[:, :, i], ALU.subtract))
                    nc.vector.memset(pad0[:, :], 0.0).then_inc(s_np, 1)
                    ve.wait_ge(s_np, b + 1)

                def normalize(b):
                    ve.wait_ge(s_den, b + 1)
                    O3 = Osb.rearrange("p (m q) -> p m q", q=NJ)
                    n3 = num.rearrange("p (m q) -> p m q", q=NJ)
                    mkb = mk[:, :].unsqueeze(2).broadcast_to([P, 6, NJ])
                    pick = view(num, [[3 * NJ, 2], [1, NJ], [NJ, 3]])
                    two = lambda i: nd[:, i, :].rearrange("p (a q) -> p a q", a=2)
                    link(nc.vector.tensor_tensor(n3, O3, mkb, ALU.mult))
                    link(nc.vector.tensor_reduce(two(0), pick, AX_X, ALU.add))
                    link(nc.vector.tensor_tensor(n3, ps[7][:, 0:6 * NJ].rearrange("p (m q) -> p m q", q=NJ), mkb,
                                                 ALU.mult))
                    link(nc.vector.tensor_reduce(two(1), pick, AX_X, ALU.add))
                    link(nc.vector.tensor_tensor(two(1), two(1), mku[:, :].unsqueeze(2).broadcast_to([P, 2, NJ]),
                                                 ALU.add))
                    link(nc.vector.reciprocal(nd[:, 1, :], nd[:, 1, :]))
                    link(nc.vector.tensor_tensor(two(0), two(0), two(1), ALU.mult))
                    nc.vector.tensor_tensor(OAB[:, :, b * NJ:(b + 1) * NJ], two(0),
                                            bvAB[:, :].unsqueeze(2).broadcast_to([P, 2, NJ]), ALU.add
                                            ).then_inc(s_ob, 1)

                for u in range(UNITS):
                    reduce_scores(0, u)
                split_maxima(0)
                for b in range(NB):
                    if b + 1 < NB:
                        for u in range(UNITS):
                            reduce_scores(b + 1, u)
                            if u == 10 and b >= 1:
                                normalize(b - 1)
                        split_maxima(b + 1)
                normalize(NB - 2)
                normalize(NB - 1)
                ve.wait_ge(s_wo, 1)
                link(nc.vector.tensor_scalar(xc[:, :], ps[0][:, 0:TOK], cols[:, 2:3], None, ALU.add))
                nc.vector.scalar_tensor_tensor(out=xT[:, :], in0=xc[:, :], scalar=gt[:, 1:2], in1=xT[:, :],
                                               op0=ALU.mult, op1=ALU.add).then_inc(s_xr, 1)
                ve.wait_ge(s_xr, 3)

            def expert_layer():
                layernorm(3)
                ve.wait_ge(s_lg, 1)
                ve.wait_ge(s_et, 1)
                e4 = lambda i: lg[:, i, :].rearrange("p (t e) -> p t e", e=NE)
                wide = lambda a: a.unsqueeze(2).broadcast_to([TT, 4, NE])
                link(nc.vector.tensor_tensor(e4(0), ps[1][0:TT, 0:4 * NE].rearrange("p (t e) -> p t e", e=NE),
                                             brB[:, :].unsqueeze(1).broadcast_to([TT, 4, NE]), ALU.add))
                for i in range(2):
                    link(nc.vector.tensor_reduce(rs[:, i, :], e4(0), AX_X, ALU.max))
                    link(nc.vector.tensor_tensor(e4(3), e4(0), wide(rs[:, i, :]), ALU.is_equal))
                    link(nc.vector.tensor_tensor(e4(3), e4(3), eiota[:, :, :], ALU.mult))
                    link(nc.vector.tensor_reduce(rs[:, 2 + i, :], e4(3), AX_X, ALU.min))
                    link(nc.vector.tensor_tensor(e4(1 + i), eiota[:, :, :], wide(rs[:, 2 + i, :]), ALU.is_equal))
                    if i == 0:
                        link(nc.vector.scalar_tensor_tensor(out=lg[:, 0, :], in0=lg[:, 1, :], scalar=-3.0e38,
                                                            in1=lg[:, 0, :], op0=ALU.mult, op1=ALU.add))
                nc.vector.tensor_tensor(rs[:, 4, :], rs[:, 1, :], rs[:, 0, :], ALU.subtract).then_inc(s_lgd, 1)
                ve.wait_ge(s_lge, 1)
                link(nc.vector.tensor_scalar(rs[:, 6, :], rs[:, 5, :], 1.0, None, ALU.add))
                link(nc.vector.reciprocal(rs[:, 7, :], rs[:, 6, :]))
                link(nc.vector.tensor_tensor(e4(2), e4(2), wide(rs[:, 5, :]), ALU.mult))
                link(nc.vector.tensor_tensor(lg[:, 1, :], lg[:, 1, :], lg[:, 2, :], ALU.add))
                nc.vector.tensor_tensor(e4(4), e4(1), wide(rs[:, 7, :]), ALU.mult).then_inc(s_rw, 1)
                for e in range(NE):
                    ve.wait_ge(s_yu, F // P * (e + 1))
                    ve.wait_ge(s_wbc, e + 1)
                    dst = xsq if e == 0 else xc
                    ins = nc.vector.scalar_tensor_tensor(
                        out=dst[:, :], in0=ps[7 if e % 2 else 0][:, 0:TOK], scalar=b2s[:, e:e + 1],
                        in1=wBs[:, e % 2, :], op0=ALU.add, op1=ALU.mult)
                    ins.then_inc(s_yc, 1)
                    ve.wait_ge(s_yc, e + 1)
                    if e:
                        link(nc.vector.tensor_tensor(xsq[:, :], xsq[:, :], xc[:, :], ALU.add))
                nc.vector.scalar_tensor_tensor(out=xT[:, :], in0=xsq[:, :], scalar=gt[:, 3:4], in1=xT[:, :],
                                               op0=ALU.mult, op1=ALU.add).then_inc(s_xr, 1)

            shift = [LB - 1] + list(range(LB - 1)) + [2 * LB - 1] + list(range(LB, 2 * LB - 1))

            def jumps(k):
                t = k * TB
                h, g, w = wk[k % 2]
                ve.wait_ge(s_act, 2 * k + 2)
                link(nc.vector.tensor_tensor(g[:, :], g[:, :], h[:, :], ALU.is_gt))
                ve.wait_ge(s_where, k + 1)
                nc.vector.tensor_tensor(R_slot(t, TB, 1, C), g[:, :].rearrange("p (t c) -> p t c", c=C),
                                        w[:, :].rearrange("p (t c) -> p t c", c=C), ALU.mult).then_inc(s_jump, 1)

            for t in range(STEPS):
                if t % TB == 0 and t // TB >= 2:
                    jumps(t // TB - 2)
                m = mring[:, (t % (2 * TB)) * C:(t % (2 * TB) + 1) * C]
                if t >= 1:
                    ve.wait_ge(s_scan, t)
                nc.vector.tensor_tensor(m, R_slot(t, 1, 1, C), R_slot(t, 1, 0, C), ALU.min)
                link(nc.vector.stream_shuffle(R_slot(t + 1, 1, 0, 1), R_slot(t, 1, C, 1), shift))
                if t % DT_STEPS == 0:
                    ve.wait_ge(s_dtc, t // DT_STEPS + 1)
                d = dts[:, (t % (2 * DT_STEPS)) * C:(t % (2 * DT_STEPS) + 1) * C]
                nc.vector.tensor_tensor_scan(view(R, [[1, C]], (t + 1) * SLOT + 1), m, d,
                                             R[:, (t + 1) * SLOT:(t + 1) * SLOT + 1], ALU.min, ALU.add
                                             ).then_inc(s_scan, 1)
            jumps(NTB - 2)
            jumps(NTB - 1)
            ve.wait_ge(s_jump, NTB)
            link(nc.vector.tensor_reduce(hops[:, 0, 0:STEPS], R_slot(0, STEPS, 1, C), AX_X, ALU.max))
            for i in range(4):
                k = 1 << i
                a, b_ = hops[:, i % 2, :], hops[:, (i + 1) % 2, :]
                mask = list(range(32))
                for h in range(2):
                    for s in range(LB):
                        mask[h * LB + s] = h * LB + (s - k if s >= k else s)
                nc.vector.tensor_copy(b_[:, 0:k], a[:, 0:k])
                link(nc.vector.stream_shuffle(shf[:, 0:STEPS - k], a[:, 0:STEPS - k], mask))
                link(nc.vector.scalar_tensor_tensor(out=b_[:, k:STEPS], in0=shf[:, 0:STEPS - k],
                                                    scalar=lmask[:, i:i + 1], in1=a[:, k:STEPS],
                                                    op0=ALU.mult, op1=ALU.max))
            mask = [LB - 1] + list(range(LB - 1)) + [2 * LB - 1] + list(range(LB, 2 * LB - 1))
            nc.vector.memset(R[:, 0:1], 0.0)
            link(nc.vector.stream_shuffle(shf[:, 0:STEPS - 1], hops[:, 0, 0:STEPS - 1], mask))
            link(nc.vector.tensor_scalar(view(R[:, :], [[SLOT, STEPS - 1], [1, 1]], SLOT),
                                         shf[:, 0:STEPS - 1].unsqueeze(2), lmask[:, 0:1], None, ALU.mult))
            for k in range(NTB):
                v = R[:, k * TB * SLOT:(k + 1) * TB * SLOT]
                last = nc.vector.tensor_tensor_scan(v, gate[:, :], v, 0.0, ALU.mult, ALU.max)
            last.then_inc(s_carry, 1)

            nc.vector.memset(zt, 0.0)
            nc.vector.memset(U, 0.0)
            ve.wait_ge(s_desk, 16 * LB)
            for j in range(NJ - 1, 0, -1):
                if j < NJ - 1:
                    ve.wait_ge(s_hop, NJ - 1 - j)
                e = e_last[:, 0:1] if j == NJ - 1 else ps[4][:, j + 1:j + 2]
                nc.vector.scalar_tensor_tensor(
                    out=wk[0][0][:, 0:2 * C].rearrange("p (c k) -> p c k", k=2),
                    in0=twice[:, :].rearrange("p (c k) -> p c k", k=2), scalar=e,
                    in1=view(jump[:, :], [[1, C], [0, 2]], j * C),
                    op0=ALU.is_equal, op1=ALU.mult, accum_out=acc[:, j:j + 1]).then_inc(s_hit, 1)
            ve.wait_ge(s_hop, NJ - 1)
            nc.vector.tensor_tensor(zt[:, :, 1:NJ], ps[4][:, 1:NJ].unsqueeze(1).broadcast_to([P, NB, NJ - 1]),
                                    first[:, :].unsqueeze(2).broadcast_to([P, NB, NJ - 1]), ALU.mult)
            nc.vector.tensor_scalar(zt[:, :, NJ:NJ + 1], first[:, :].unsqueeze(2), 2.0 * (NI - 1), None, ALU.mult
                                    ).then_inc(s_z, 1)
            ve.wait_ge(s_eb, 1)
            link(nc.vector.tensor_copy(EB[:, :, :], ps[5][0:C, 0:NB * (NJ + 1)].rearrange(
                "c (b j) -> c b j", b=NB)))
            for half in range(2):
                if half:
                    ve.wait_ge(s_ex, 1)
                for s in range(NS):
                    eb = EB[:, half * NB // 2:(half + 1) * NB // 2, :]
                    if s >= 2:
                        pass
                    a = Am[:, s % 2, :].rearrange("c (b j) -> c b j", j=NJ)
                    link(nc.vector.tensor_scalar(a, eb[:, :, 0:NJ], rowc2[:, s:s + 1], None, ALU.is_le))
                    last = nc.vector.scalar_tensor_tensor(
                        out=Pm[:, s, :].rearrange("c (b j) -> c b j", j=NJ), in0=eb[:, :, 1:NJ + 1],
                        scalar=rowc2[:, s:s + 1], in1=a, op0=ALU.is_ge, op1=ALU.mult)
                last.then_inc(s_pm, 1)
            ve.wait_ge(s_uT, 1)
            ve.wait_ge(s_gate, 1)
            nc.vector.scalar_tensor_tensor(
                out=xT[:, :].rearrange("p (t a j) -> p t a j", a=2, j=NJ)[:, :, 0, :],
                in0=ps[3][:, :].rearrange("p (t a j) -> p t a j", a=2, j=64)[:, :, 0, 0:NJ],
                scalar=gt[:, 0:1],
                in1=xT[:, :].rearrange("p (t a j) -> p t a j", a=2, j=NJ)[:, :, 0, :],
                op0=ALU.mult, op1=ALU.add)
            link(nc.vector.scalar_tensor_tensor(
                out=xT[:, :].rearrange("p (t a j) -> p t a j", a=2, j=NJ)[:, :, 1, :],
                in0=ps[3][:, :].rearrange("p (t a j) -> p t a j", a=2, j=64)[:, :, 1, 0:NJ],
                scalar=gt[:, 0:1],
                in1=xT[:, :].rearrange("p (t a j) -> p t a j", a=2, j=NJ)[:, :, 1, :],
                op0=ALU.mult, op1=ALU.add))
            nc.vector.memset(pad0[:, :], 0.0).then_inc(s_xr, 1)
            if stage >= 2:
                memory_layer()
            if stage >= 3:
                attention_layer()
            if stage >= 4:
                expert_layer()

        @block.tensor
        def _(pe):
            pe.wait_ge(s_x, 16)
            pe.wait_ge(s_pool, 9)
            pe.wait_ge(s_const, 3)
            for t in range(4):
                last = nc.tensor.transpose(ps[0][:, t * TT:(t + 1) * TT], x_tok[:, t, :], ident[0:TT, 0:TT])
            last.then_inc(s_xT, 1)

            def layernorm_sums(k):
                nc.tensor.matmul(ps[0][:, 0:TOK], meanw[:, :], xT[:, :], start=True, stop=True
                                 ).then_inc(s_mean, 1)
                pe.wait_ge(s_cen, k + 1 + (k > 0))
                nc.tensor.matmul(ps[0][:, 0:TOK], meanw[:, :], xsq[:, :], start=True, stop=True
                                 ).then_inc(s_var, 1)

            pe.wait_ge(s_xTe, 1)
            layernorm_sums(0)
            pe.wait_ge(s_cen, 2)
            nc.tensor.matmul(ps[0][0:C, 0:TOK], ones[:, 0:C], xsq[:, :], start=True, stop=True).then_inc(s_bb, 1)

            def dots(b):
                pe.wait_ge(s_ctA, (NPIECE - 1) * (b + 1))
                pe.wait_ge(s_ctV, b + 1)
                if b >= 2:
                    pe.wait_ge(s_d2, b - 1)
                for s in range(NS):
                    bank, o = (ps[4 + 2 * (b % 2)], s) if s < 8 else (ps[5 + 2 * (b % 2)], s - 8)
                    last = nc.tensor.matmul(bank[0:C, o * NJ:(o + 1) * NJ],
                                            ctxT[:, b * NI + s * C:b * NI + (s + 1) * C],
                                            xm2[:, b * NJ:(b + 1) * NJ], start=True, stop=True)
                last.then_inc(s_dot, 1)

            for b in range(NB):
                pe.wait_ge(s_nat[b], 16)
                for n in range(NPIECE):
                    if b >= 1:
                        if n < NPIECE - 1:
                            pe.wait_ge(s_ctA, (NPIECE - 1) * (b - 1) + n + 1)
                        else:
                            pe.wait_ge(s_ctV, b)
                    for i in range(SPP):
                        last = nc.tensor.transpose(ps[1 + n][:, i * C:(i + 1) * C],
                                                   nat[:, b % RING, n * SPP + i, :], ident[0:C, 0:C])
                    last.then_inc(s_ct, 1)
                if b >= 1:
                    dots(b - 1)
            dots(NB - 1)
            pe.wait_ge(s_dist, NB)
            pe.wait_ge(s_bbe, 1)
            for q in range(STEPS // DT_STEPS):
                if q >= 2:
                    pe.wait_ge(s_dtc, q - 1)
                for i in range(DT_STEPS):
                    t = q * DT_STEPS + i
                    src = view(dist[:, :], [[JW - 1, P]], t + PADJ)
                    last = nc.tensor.transpose(ps[q % 2][:, i * C:(i + 1) * C], src, ident[0:C, 0:C])
                last.then_inc(s_dt, 1)
            for j in range(NJ - 1, 0, -1):
                pe.wait_ge(s_hit, NJ - j)
                nc.tensor.matmul(ps[4][:, j:j + 1], blk[:, :], acc[:, j:j + 1], start=True, stop=True
                                 ).then_inc(s_hop, 1)
            pe.wait_ge(s_z, 1)
            nc.tensor.matmul(ps[5][0:C, 0:NB * (NJ + 1)], ones[:, 0:C],
                             zt[:, :, :].rearrange("p b j -> p (b j)"), start=True, stop=True).then_inc(s_eb, 1)
            pe.wait_ge(s_keys, 16 * 5)
            for c in range(8):
                nc.tensor.transpose(ps[1 + c // 4][:, (c % 4) * P:(c % 4 + 1) * P], wq_sb[:, c * P:(c + 1) * P],
                                    ident[:, :])
            for c in range(8):
                last = nc.tensor.transpose(ps[7][:, c * 2 * NK:(c + 1) * 2 * NK], keyn[:, c, :],
                                           ident[0:2 * NK, 0:2 * NK])
            last.then_inc(s_foldT, 1)
            for half in range(2):
                pe.wait_ge(s_pm, half + 1)
                for i in range(NB // 2):
                    b = half * NB // 2 + i
                    pe.wait_ge(s_nat2[b], 16)
                    par, pair = b % 2, i // 2
                    for s in range(NS):
                        rows = nat[:, b, s, :] if b < RING else \
                            dist[:, ((b - RING) * NS + s) * D:((b - RING) * NS + s + 1) * D]
                        last = nc.tensor.matmul(ps[6 + half][64 * par:64 * par + NJ, pair * D:(pair + 1) * D],
                                                Pm[:, s, i * NJ:(i + 1) * NJ], rows,
                                                start=(s == 0), stop=(s == NS - 1))
                last.then_inc(s_ex, 1)
                if half == 0:
                    pe.wait_ge(s_foldc, 1)
                    for c in range(8):
                        last = nc.tensor.matmul(ps[1][:, c * 2 * NK:(c + 1) * 2 * NK], wqT[:, c * P:(c + 1) * P],
                                                keyT[:, c * 2 * NK:(c + 1) * 2 * NK], start=True, stop=True)
                    last.then_inc(s_fold, 1)
            pe.wait_ge(s_u, 4)
            for t in range(4):
                last = nc.tensor.transpose(ps[3][:, t * P:(t + 1) * P], U[:, t, :], ident[:, :])
            last.then_inc(s_uT, 1)
            pe.wait_ge(s_xr, 1)
            if stage >= 2:
                layernorm_sums(1)
                pe.wait_ge(s_xn, 2)
                for t in range(4):
                    last = nc.tensor.transpose(ps[4][0:TT, t * D:(t + 1) * D], xnT[:, t * TT:(t + 1) * TT],
                                               ident[:, :])
                last.then_inc(s_xnk, 1)
                pe.wait_ge(s_fold_sb, 1)
                for t in range(4):
                    nc.tensor.matmul(ps[t][0:TT, :], xnT[:, t * TT:(t + 1) * TT], fold[:, :],
                                     start=True, stop=True).then_inc(s_sim, 1)
                if stage >= 3:
                    pe.wait_ge(s_w, 16 * 22)
                    pe.wait_ge(s_xnc, 1)
                    for b in range(NB):
                        for i in range(NCH // 4):
                            n = b * (NCH // 4) + i
                            if n >= 2:
                                pe.wait_ge(s_vc, n - 1)
                            for k in range(4):
                                c = 4 * i + k
                                rows = min(P, NI - c * P)
                                last = nc.tensor.matmul(ps[4 + n % 2][0:rows, k * D:(k + 1) * D],
                                                        ctxT[:, b * NI + c * P:b * NI + c * P + rows], Wv_sb,
                                                        start=True, stop=True)
                            last.then_inc(s_vp, 1)
                        for i in range(NPIECE):
                            n = b * NPIECE + i
                            if n >= 2:
                                pe.wait_ge(s_kc, n - 1)
                            nc.tensor.matmul(ps[6 + n % 2][:, 0:PIECE], Wk_sb,
                                             ctxT[:, b * NI + i * PIECE:b * NI + (i + 1) * PIECE],
                                             start=True, stop=True).then_inc(s_kp, 1)
                pe.wait_ge(s_otok, 4)
                for t in range(4):
                    last = nc.tensor.transpose(ps[0][:, t * TT:(t + 1) * TT], x_tok[:, t, :], ident[0:TT, 0:TT])
                last.then_inc(s_oT, 1)
            if stage >= 3:
                pe.wait_ge(s_xr, 2)
                layernorm_sums(2)
                pe.wait_ge(s_xn, 3)
                nc.tensor.matmul(ps[1][:, 0:TOK], Wq_sb, xnT[:, :], start=True, stop=True).then_inc(s_q, 1)
                pe.wait_ge(s_kc, NPIECE * NB)
                pe.wait_ge(s_vc, NCH // 4 * NB)
                pe.wait_ge(s_qt, 1)
                pe.wait_ge(s_tabs, 34)

                def row_scores(b, u):
                    k = b * UNITS + u
                    if u == 0:
                        pe.wait_ge(s_qb, b + 1)
                    if k >= 2:
                        pe.wait_ge(s_mx, k - 1)
                    nc.tensor.matmul(ps[k % 2][0:2 * NJ, 0:PIECE],
                                     Qb[:, b % 2, (u // NPIECE) * 2 * NJ:(u // NPIECE + 1) * 2 * NJ],
                                     ctxT[:, b * NI + (u % NPIECE) * PIECE:b * NI + (u % NPIECE + 1) * PIECE],
                                     start=True, stop=True).then_inc(s_s1, 1)

                def maxima_to_rows(b):
                    pe.wait_ge(s_np, b + 1)
                    if b >= 2:
                        pe.wait_ge(s_ob, b - 1)
                    for pair in range(NH // 2):
                        half, i = pair // (NH // 4), pair % (NH // 4)
                        last = nc.tensor.matmul(ps[7][32 * half:32 * half + 3, i * 2 * NJ:(i + 1) * 2 * NJ],
                                                npart[:, pair, :], identb[0:2 * NJ, 0:2 * NJ],
                                                start=True, stop=True)
                    last.then_inc(s_nmt, 1)

                def weigh_values(g):
                    b, c = g // NCH, g % NCH
                    rows = min(P, NI - c * P)
                    pe.wait_ge(s_exp, g + 1)
                    if c == 0 and b >= 1:
                        pe.wait_ge(s_oc, b)
                    for t in range(6):
                        w = min(3, NH - 3 * t) * NJ
                        q, o = 32 * (t % 4), (t // 4) * 3 * NJ
                        v0 = (g * 6 + t) * (3 * DH + 1)
                        last = nc.tensor.matmul(ps[6][q:q + 32, o:o + w], vals[0:rows, v0:v0 + 32],
                                                Pt[0:rows, g % 2, 3 * t * NJ:3 * t * NJ + w],
                                                start=(c == 0 and t < 4), stop=(c == NCH - 1),
                                                skip_group_check=True)
                    last.then_inc(s_pv, 1)

                for u in range(UNITS):
                    row_scores(0, u)
                maxima_to_rows(0)
                for b in range(NB):
                    pe.wait_ge(s_nmc, b + 1)
                    for c in range(NCH):
                        g = b * NCH + c
                        rows = min(P, NI - c * P)
                        if g >= 2:
                            pe.wait_ge(s_exp, g - 1)
                        for half in range(2):
                            dst = ps[2 + 2 * (g % 2) + half][0:rows, 0:HQ // 2]
                            cut = slice(half * HQ // 2, (half + 1) * HQ // 2)
                            nc.tensor.matmul(dst, ctxT[:, b * NI + c * P:b * NI + c * P + rows], Qb[:, b % 2, cut],
                                             start=True, stop=False)
                            last = nc.tensor.matmul(dst, ones3[:, 0:rows], NM[:, b % 2, cut],
                                                    start=False, stop=True)
                        last.then_inc(s_s2, 1)
                        if g >= 1:
                            weigh_values(g - 1)
                        if b + 1 < NB and c < UNITS // 3:
                            for u in range(3 * c, 3 * c + 3):
                                row_scores(b + 1, u)
                        if c == 3 and b >= 1:
                            pe.wait_ge(s_oc, b)
                            pe.wait_ge(s_nmc, b + 1)
                            nc.tensor.matmul(ps[7][:, 0:6 * NJ], sel, Osb, start=True, stop=True
                                             ).then_inc(s_den, 1)
                        if c == MAXROW_AT and b + 1 < NB:
                            maxima_to_rows(b + 1)
                weigh_values(NB * NCH - 1)
                pe.wait_ge(s_oc, NB)
                pe.wait_ge(s_ob, NB - 1)
                nc.tensor.matmul(ps[7][:, 0:6 * NJ], sel, Osb, start=True, stop=True).then_inc(s_den, 1)
                pe.wait_ge(s_ob, NB)
                for half in range(2):
                    last = nc.tensor.matmul(ps[0][:, 0:TOK], WoAB[:, half, :], OAB[:, half, :],
                                            start=(half == 0), stop=(half == 1))
                last.then_inc(s_wo, 1)
            if stage >= 4:
                pe.wait_ge(s_xr, 3)
                layernorm_sums(3)
                pe.wait_ge(s_xn, 4)
                for t in range(4):
                    last = nc.tensor.matmul(ps[1][0:TT, t * NE:(t + 1) * NE], xnT[:, t * TT:(t + 1) * TT],
                                            Wr[:, :], start=True, stop=True)
                last.then_inc(s_lg, 1)
                pe.wait_ge(s_w12, 32)
                FC = F // P

                def hidden(i):
                    e, c = i // FC, i % FC
                    if i >= 2:
                        pe.wait_ge(s_hc, i - 1)
                    nc.tensor.matmul(ps[5 + i % 2][:, 0:TOK], W1s[:, e, c * P:(c + 1) * P], xnT[:, :],
                                     start=True, stop=True).then_inc(s_h, 1)

                def output(i):
                    e, c = i // FC, i % FC
                    pe.wait_ge(s_hc, i + 1)
                    if c == 0 and e >= 2:
                        pe.wait_ge(s_yc, e - 1)
                    nc.tensor.matmul(ps[7 if e % 2 else 0][:, 0:TOK], W2s[:, i, :], hT[:, i % 4, :],
                                         start=(c == 0), stop=(c == FC - 1)).then_inc(s_yu, 1)

                hidden(0)
                hidden(1)
                pe.wait_ge(s_rw, 1)
                for t in range(4):
                    last = nc.tensor.transpose(ps[2][0:NE, t * TT:(t + 1) * TT], lg[:, 4, t * NE:(t + 1) * NE],
                                               ident[0:TT, 0:TT])
                last.then_inc(s_wtT, 1)
                pe.wait_ge(s_wtc, 1)
                pe.wait_ge(s_et, 3)
                for i in range(NE * FC):
                    if i % FC == 0:
                        e = i // FC
                        if e >= 2:
                            pe.wait_ge(s_wbc, e - 1)
                        nc.tensor.matmul(ps[3 + e % 2][:, 0:TOK], sele[:, e, :], wT, start=True, stop=True
                                         ).then_inc(s_wb, 1)
                    if i + 2 < NE * FC:
                        hidden(i + 2)
                    output(i)
            pe.wait_ge(s_xr, min(stage, 4))
            for t in range(4):
                last = nc.tensor.transpose(ps[1][0:TT, t * D:(t + 1) * D], xT[:, t * TT:(t + 1) * TT],
                                           ident[:, :])
            last.then_inc(s_fT, 1)


_INS = ["x", "ctx_1024", "g_xattn", "g_ffn", "L0_ffn_w_q", "L0_ffn_keys", "w_tab",
        "L1_xattn_Wq", "L1_xattn_bq", "L1_xattn_Wk", "L1_xattn_bk", "L1_xattn_Wv", "L1_xattn_bv",
        "L1_xattn_Wo", "L1_xattn_bo", "L1_ffn_W_router", "L1_ffn_b_router", "L1_ffn_W1", "L1_ffn_b1",
        "L1_ffn_W2", "L1_ffn_b2"]


def kernel(**inputs):
    import numpy as np
    from concourse import bacc
    from concourse.bass_utils import run_bass_kernel_spmd

    nc = bacc.Bacc("TRN2", target_bir_lowering=False, num_devices=1)
    laid = dict(inputs)
    laid["w_tab"] = np.concatenate([np.asarray(inputs["L0_ffn_w_down"]), np.asarray(inputs["L0_ffn_w_up"])], axis=1)
    arrays, args = {}, []
    for name in _INS:
        a = np.ascontiguousarray(laid[name])
        arrays[f"in_{name}"] = a
        args.append(nc.dram_tensor(f"in_{name}", a.shape, mybir.dt.from_np(a.dtype), kind="ExternalInput").ap())
    shape = np.asarray(inputs["x"]).shape
    args.append(nc.dram_tensor("out_x", shape, mybir.dt.float32, kind="ExternalOutput").ap())
    build_gated_layers(nc, *args)
    r = run_bass_kernel_spmd(nc, [arrays], core_ids=[0])
    return r.results[0]["out_x"]
```

```python
from contextlib import ExitStack

import concourse.bass as bass
from concourse import mybir

ALU = mybir.AluOpType
ACT = mybir.ActivationFunctionType
AX_X = mybir.AxisListType.X
F32 = mybir.dt.float32
BF16 = mybir.dt.bfloat16
I32 = mybir.dt.int32
U32 = mybir.dt.uint32

P = 128
BIG = 1.0e20
EPS = 1.0e-5


def view(ap, dims, offset=0):
    return bass.AP(tensor=ap.tensor, offset=ap.offset + offset, ap=[list(ap.ap[0])] + dims)


def build_gated_layers(nc, x, ctx_in, g_xattn, g_ffn, w_q, keys, w_tab, Wq, bq, Wk, bk, Wv, bv, Wo, bo,
                       W_router, b_router, W1, b1, W2, b2, out, stage=9):
    NB, NJ, D = x.shape
    NI = ctx_in.shape[1]
    TOK = NB * NJ
    LB = P // NB
    C = 100
    NS = NI // C
    assert NS * C == NI and NS < LB and D == P
    BS = LB * (NJ + NS - 2)
    STEPS = NJ + NS - 1
    PADJ = NS - 1
    JW = NJ + PADJ
    SLOT = C + 1
    PIECE = 500
    NPIECE = NI // PIECE
    SPP = PIECE // C
    TB = 5
    NTB = STEPS // TB
    assert NTB * TB == STEPS
    RING = 4
    DT_STEPS = PIECE // C
    JQ = NS * D + 3 * NS * NJ
    NHK, NK = keys.shape[0], keys.shape[1]
    FOLD = w_q.shape[1]
    NH = 16
    DH = D // NH
    HQ = NH * NJ
    NCH = -(-NI // P)
    VT, VTW = NH // 2, 2 * DH + 1
    VW = VT * VTW
    UNITS = NH // 2 * NPIECE
    PRODUCTS = ((0, 0), (0, 1), (0, 2), (1, 0), (1, 1), (2, 0))
    NPR = len(PRODUCTS) * 2 * DH
    KPIECE = 375
    KPB = NI // KPIECE
    NKP = NB * KPB
    EARLY = 12
    assert KPIECE * KPB == NI and 2 * (NKP - EARLY) <= NJ - 1
    BESIDE = [3] * 8 + [2] * (NCH * NB)
    assert 3 * 8 == UNITS and 2 * NCH == UNITS
    MAXROW_AT = 10
    NE, F = W1.shape[0], W1.shape[2]
    FC = F // P
    TT = TOK // 4

    with ExitStack() as ctx:
        def sb(name, shape, dt=F32):
            return ctx.enter_context(nc.sbuf_tensor(name, shape, dt))

        def sem(name):
            return ctx.enter_context(nc.semaphore(name))

        banks = ctx.enter_context(nc.psum_tensor("banks", [P, 8, 512], F32))
        ps = [banks[:, i, :] for i in range(8)]

        ctxT = sb("ctxT", [P, NB * NI])
        N_DIST, N_NAT, N_JUMP, N_R = NB * BS + P, RING * NS * D, NJ * C, (STEPS + 1) * SLOT
        arena = sb("arena", [P, N_DIST + N_NAT + N_JUMP + N_R])
        o_nat, o_jump, o_R = N_DIST, N_DIST + N_NAT, N_DIST + N_NAT + N_JUMP
        dist = arena[0:C, 0:N_DIST]
        nat = arena[0:C, o_nat:o_jump].rearrange("c (r s d) -> c r s d", r=RING, s=NS)
        jump = arena[:, o_jump:o_R]
        R = arena[:, o_R:]
        N_B = TB * C
        work = sb("work", [P, 10 * N_B + TB * SLOT])
        mring = work[:, 0:2 * N_B]
        dts = work[:, 2 * N_B:4 * N_B]
        wk = [[work[:, (4 + 3 * a + i) * N_B:(5 + 3 * a + i) * N_B] for i in range(3)] for a in range(2)]
        gate = work[:, 10 * N_B:]
        taken = 0

        def later(rows, n, dt=F32):
            nonlocal taken
            words = n if dt == F32 else -(-n // 2)
            ap = work[0:rows, taken:taken + words]
            taken += words
            assert taken <= 10 * N_B + TB * SLOT
            return ap if dt == F32 else ap.bitcast(dt)

        twice1 = sb("twice1", [P, C])
        sq = jump[0:C, 0:NS * D]
        absum = jump[0:C, NS * D:NS * D + 2 * NS * NJ].rearrange("c (a n) -> c a n", a=2)
        dtmp = jump[0:C, NS * D + 2 * NS * NJ:NS * D + 3 * NS * NJ]
        aa = sb("aa", [C, NB, NS])
        bbB = jump[0:C, JQ:JQ + TOK]

        ident = sb("ident", [P, P])
        Wk_sb = sb("Wk_sb", [P, D])
        o_kf = (NB - RING) * NS * D
        assert o_kf + 3 * KPIECE <= N_DIST and 6 * KPIECE <= 5 * N_B
        kf = arena[:, o_kf:o_kf + 3 * KPIECE].rearrange("p (r i) -> p r i", r=3)
        kq = work[:, 2 * N_B:2 * N_B + 6 * KPIECE].bitcast(BF16).rearrange("p (r x i) -> p r x i", r=4, x=3)
        key_parts = nc.dram_tensor("key_parts", (NB, 3, P, NI), BF16, kind="Internal").ap()
        query_parts = nc.dram_tensor("query_parts", (3, P, 2 * TOK), BF16, kind="Internal").ap()
        meanw = sb("meanw", [P, P])
        ones = sb("ones", [P, P])
        blk = sb("blk", [P, P])
        first = sb("first", [P, NB])
        pidx = sb("pidx", [P, 1], I32)
        lane_i = sb("lane_i", [P, 1], I32)
        lane = sb("lane", [P, 1])
        lmask = sb("lmask", [P, 4])
        twice = sb("twice", [P, C * 2])
        rowc2 = sb("rowc2", [C, NS])
        acc = sb("acc", [P, NJ])
        e_last = sb("e_last", [P, 1])
        hops = sb("hops", [P, 2, STEPS + 1])
        shf = sb("shf", [P, STEPS + 1])
        zt = mring[:, 0:NB * (NJ + 1)].rearrange("p (b j) -> p b j", b=NB)
        EB = work[0:C, 7 * N_B:7 * N_B + NB * (NJ + 1)].rearrange("c (b j) -> c b j", b=NB)
        Pm = R[0:C, 0:2 * NS * 2 * NJ].rearrange("c (r s n) -> c r s n", r=2, s=NS)
        U = work[:, 8 * N_B:8 * N_B + NB // 2 * D].rearrange("p (t d) -> p t d", d=D)
        o_am = 8 * N_B + NB // 2 * D
        A_RING = 6
        Am = work[0:C, o_am:o_am + A_RING * 2 * NJ].rearrange("c (a n) -> c a n", a=A_RING)
        g4 = sb("g4", [P, 4])
        gt = sb("gt", [P, 4])
        x_tok = sb("x_tok", [TT, 4, D])
        xT = sb("xT", [P, TOK])
        xc = sb("xc", [P, TOK])
        xsq = sb("xsq", [P, TOK])
        rstd = sb("rstd", [P, TOK])
        xnT = sb("xnT", [P, TOK])
        xm2 = jump[:, JQ + TOK:JQ + 2 * TOK]
        epsc = sb("epsc", [P, 1])
        pad0 = sb("pad0", [P, 1])

        o_fold = N_R - 3 * FOLD
        wq_sb = R[:, o_fold:o_fold + FOLD]
        keyn = R[0:2 * NK, o_fold + FOLD:o_fold + 2 * FOLD].rearrange("k (c f) -> k c f", f=P)
        wqT = R[:, o_fold + 2 * FOLD:o_fold + 3 * FOLD]
        keyT = sb("keyT", [P, FOLD // 2])
        fold = sb("fold", [P, FOLD // 2])
        kiota = later(TT, 2 * NHK * NK)
        mxs = sb("mxs", [TT, 4, 2 * NHK])
        ixs = sb("ixs", [TT, 4, 2 * NHK])
        score = sb("score", [TT, 4, NHK])
        idxf = sb("idxf", [TT, 4, NHK])
        idx = sb("idx", [TT, 4 * NHK], U32)
        hcol = sb("hcol", [TT, 4, NHK])
        gath = arena[0:TT, 0:4 * NHK * 2 * D].rearrange("p (t h d) -> p t h d", t=4, h=NHK)
        prod = later(P, NHK * D)
        vals = arena[:, o_nat:o_nat + NCH * NB * VW + 32]
        o_att = o_nat + NCH * NB * VW + 32
        Pt = arena[:, o_att:o_att + 2 * HQ].rearrange("p (r n) -> p r n", r=2)
        KPW = NH // 2 * NI // 2
        kp_words = [ctxT[:, 0:KPW], ctxT[:, KPW:2 * KPW], arena[:, 0:KPW]]
        KP = [w.bitcast(BF16).rearrange("p (m i) -> p m i", m=NH // 2) for w in kp_words]
        assert KPW <= N_DIST
        QP = arena[:, o_att + 2 * HQ:o_att + 6 * HQ].bitcast(BF16).rearrange(
            "p (m b n) -> p m b n", m=NH // 2, b=NB)
        Qm = Pt.rearrange("p r n -> p (r n)")[:, 0:2 * TOK]
        Wq_sb, Wv_sb = later(P, D), later(P, D)
        WoAB = later(P, 2 * D).rearrange("p (a d) -> p a d", a=2)
        bvAB = sb("bvAB", [P, 2])
        cols = sb("cols", [P, 3])
        hm = sb("hm", [P, 2])
        QS = later(P, 3 * 2 * TOK, BF16).rearrange("p (x n) -> p x n", x=3)
        mx3 = sb("mx3", [2 * NJ, 2, NH // 2, NPIECE])
        nmx = sb("nmx", [2 * NJ, NH // 2])
        npart = sb("npart", [2 * NJ, NH // 2, 3], BF16)
        identb = later(P, P, BF16)
        Osb = arena[:, o_att + 6 * HQ:o_att + 6 * HQ + 4 * NJ].rearrange("p (a m q) -> p a m q", a=2, m=2)
        assert o_att + 6 * HQ + 4 * NJ <= N_DIST + N_NAT + N_JUMP + N_R
        num = later(P, 4 * NJ).rearrange("p (i a q) -> p i a q", i=2, a=2)
        OAB = QS.rearrange("p x n -> p (x n)").bitcast(F32)[:, 0:2 * TOK].rearrange("p (a n) -> p a n", a=2)
        nd = later(P, 4 * NJ).rearrange("p (a n) -> p a n", a=2)
        mk = sb("mk", [P, 2])
        mku = sb("mku", [P, 1])
        sel = later(P, P)
        mk2 = sb("mk2", [P, 1])
        l32 = sb("l32", [P, 1])
        maxrows = [ps[6 + r].bitcast(BF16)[NPR:NPR + 3, 0:HQ].rearrange("p (m n) -> p m n", m=NH // 2)
                   for r in range(2)]
        W1s = arena[:, 0:NE * F].rearrange("p (e f) -> p e f", e=NE)
        W2s = arena[:, NE * F:2 * NE * F].rearrange("p (u d) -> p u d", d=D)
        assert 2 * NE * F <= N_DIST
        Wr = sb("Wr", [P, NE])
        brB = sb("brB", [TT, NE])
        b1s = sb("b1s", [P, NE * F // P])
        b2s = sb("b2s", [P, NE])
        eiota = sb("eiota", [TT, 4, NE])
        lg = later(TT, 6 * 4 * NE).rearrange("p (i n) -> p i n", i=6)
        rs = sb("rs", [TT, 8, 4])
        wT = later(NE, TOK)
        sele = prod[0:NE, :].rearrange("p (e n) -> p e n", n=P)
        hT = arena[:, o_nat:o_nat + 4 * TOK].rearrange("p (r n) -> p r n", r=4)
        wBs = arena[:, o_nat + 4 * TOK:o_nat + 6 * TOK].rearrange("p (r n) -> p r n", r=2)

        s_x = sem("x_loaded")
        s_small = sem("small_loaded")
        s_nat = [sem(f"nat_loaded{r}") for r in range(NB)]
        s_nat2 = [sem(f"nat_again{b}") for b in range(NB)]
        s_pool = sem("pool_done")
        s_const = sem("constants_done")
        s_dve = sem("dve_done")
        s_act = sem("act_done")
        s_xT = sem("xT_transposed")
        s_xTe = sem("xT_copied")
        s_mean = sem("mean_ready")
        s_cen = sem("centred_squares_ready")
        s_var = sem("variance_ready")
        s_std = sem("deviation_ready")
        s_xn = sem("normalized_ready")
        s_bb = sem("query_norms_ready")
        s_bbe = sem("query_norms_copied")
        s_ct = sem("context_transposed")
        s_ctA = sem("context_copied_by_act")
        s_ctV = sem("context_copied_by_dve")
        s_sq = sem("context_squared")
        s_aa = sem("context_norms_ready")
        s_ab = sem("norm_sums_ready")
        s_dot = sem("dots_ready")
        s_d2 = sem("squared_distances_ready")
        s_dist = sem("distances_ready")
        s_dt = sem("distances_by_lane")
        s_dtc = sem("distances_by_lane_copied")
        s_scan = sem("column_scanned")
        s_jin = sem("jump_inputs_ready")
        s_sgn = sem("left_below_diagonal_ready")
        s_where = sem("where_to_ready")
        s_jump = sem("jumps_ready")
        s_carry = sem("carries_ready")
        s_desk = sem("last_columns_deskewed")
        s_desk2 = sem("first_columns_deskewed")
        s_hit = sem("hit_ready")
        s_hop = sem("hop_ready")
        s_z = sem("hops_placed")
        s_eb = sem("hops_spread")
        s_ebc = sem("hops_spread_copied")
        s_ex = sem("rows_summed")
        s_u = sem("sums_copied")
        s_uT = sem("sums_transposed")
        s_gate = sem("gates_ready")
        s_natfree = sem("nat_used")
        s_out = sem("out_stored")

        s_tabs = sem("attention_tables_step")
        s_lane32 = sem("row_of_quarter_ready")
        s_et = sem("expert_tables_step")
        s_wk = sem("key_weights_loaded")
        s_kr = sem("first_key_part_taken")
        s_k2 = sem("second_key_part_ready")
        s_ks = sem("keys_split")
        s_kd = [sem(f"key_parts_stored{r}") for r in range(4)]
        s_kpl = [sem(f"key_parts_loaded{r}") for r in range(3)]
        s_am = sem("path_starts_ready_by_gpsimd")
        s_amv = sem("path_starts_ready_by_dve")
        s_pm = sem("path_masks_ready")
        s_qs = sem("queries_split")
        s_qd = sem("query_parts_stored")
        s_qp = sem("query_parts_laid")
        s_one = sem("ones_rows_ready")
        s_keyz = sem("key_tiles_zeroed")
        s_keys = sem("keys_loaded")
        s_foldT = sem("fold_inputs_transposed")
        s_foldc = sem("fold_inputs_copied")
        s_fold = sem("keys_folded")
        s_fold_sb = sem("folded_keys_copied")
        s_xr = sem("hidden_state_updated")
        s_xnk = sem("tokens_transposed")
        s_xnc = sem("tokens_copied")
        s_sim = sem("similarities_ready")
        s_picked = sem("similarities_used")
        s_idx = sem("experts_chosen")
        s_gath = [sem(f"rows_gathered{t}") for t in range(4)]
        s_hcol = sem("expert_dots_ready")
        s_gelu = sem("expert_gelu_ready")
        s_otok = sem("memory_output_ready")
        s_oT = sem("memory_output_transposed")
        s_wz = sem("weight_tiles_zeroed")
        s_w = sem("attention_weights_loaded")
        s_w12 = sem("expert_weights_loaded")
        s_tab = sem("attention_tables_ready")
        s_vp = sem("values_projected")
        s_vc = sem("values_copied")
        s_kp = sem("keys_projected")
        s_kev = sem("keys_evacuated")
        s_q = sem("queries_projected")
        s_s1 = sem("row_scores_ready")
        s_mx = sem("row_scores_reduced")
        s_np = sem("negative_maxima_split")
        s_nmt = sem("negative_maxima_in_rows")
        s_nmc = sem("negative_maxima_copied")
        s_s2 = sem("column_scores_ready")
        s_exp = sem("probabilities_ready")
        s_pv = sem("values_weighted")
        s_oc = sem("head_sums_copied")
        s_den = sem("denominators_spread")
        s_ob = sem("heads_normalized")
        s_wo = sem("attention_output_ready")
        s_lg = sem("router_logits_ready")
        s_lgd = sem("logit_gap_ready")
        s_lge = sem("logit_gap_exponential")
        s_rw = sem("router_weights_ready")
        s_wtT = sem("router_weights_transposed")
        s_wtc = sem("router_weights_copied")
        s_wb = sem("router_weights_spread")
        s_wbc = sem("router_weights_spread_copied")
        s_h = sem("hidden_ready")
        s_hc = sem("hidden_copied")
        s_yu = sem("hidden_used")
        s_yc = sem("expert_output_added")
        s_fT = sem("output_transposed")
        s_fc = sem("output_copied")

        R_slot = lambda k, n, lo, cnt: view(R[:, :], [[SLOT, n], [1, cnt]], k * SLOT + lo)
        block = ctx.enter_context(nc.Block())

        @block.sync
        def _(sp):
            sp.dma_start(x_tok[:, :, :], x.rearrange("b j d -> (b j) d").rearrange("(t p) d -> p t d", t=4)
                         ).then_inc(s_x, 16)
            for b in range(NB):
                if b >= RING:
                    sp.wait_ge(s_ct, NPIECE * (b - RING + 1))
                    sp.wait_ge(s_sq, b - RING + 1)
                sp.dma_start(nat[:, b % RING, :, :], ctx_in[b].rearrange("(s c) d -> c s d", c=C)
                             ).then_inc(s_nat[b], 16)
            sp.dma_start(Wk_sb[:, :], Wk[:, :]).then_inc(s_wk, 16)
            for i, src in enumerate((bq, bk, bo)):
                sp.dma_start(cols[:, i:i + 1], src.rearrange("(d a) -> d a", a=1)).then_inc(s_wk, 16)
            for b in range(RING):
                sp.wait_ge(s_ct, NPIECE * (b + RING + 1))
                sp.wait_ge(s_sq, b + RING + 1)
                sp.dma_start(nat[:, b, :, :], ctx_in[b].rearrange("(s c) d -> c s d", c=C)
                             ).then_inc(s_nat2[b], 16)
            sp.wait_ge(s_dt, NTB * TB // DT_STEPS)
            for b in range(RING, NB):
                o = (b - RING) * NS * D
                sp.dma_start(dist[:, o:o + NS * D].rearrange("c (s d) -> c s d", d=D),
                             ctx_in[b].rearrange("(s c) d -> c s d", c=C)).then_inc(s_nat2[b], 16)
            sp.wait_ge(s_carry, 1)
            for lo, hi, s_d in ((NJ // 2, NJ, s_desk), (0, NJ // 2, s_desk2)):
                for s in range(LB):
                    sp.dma_start(view(jump[s:P - LB + s + 1:LB, :], [[1, (hi - lo) * C]], lo * C).rearrange(
                                     "p (j c) -> p j c", c=C),
                                 view(R[s:P - LB + s + 1:LB, :], [[SLOT, hi - lo], [1, C]], (lo + s) * SLOT + 1)
                                 ).then_inc(s_d, 16)
            sp.wait_ge(s_keyz, 1)
            sp.dma_start(wq_sb[:, :], w_q[:, :]).then_inc(s_keys, 16)
            kv = keys.rearrange("(m a) k p f -> a p k m f", a=2)
            for a in range(2):
                for p in range(2):
                    sp.dma_start(keyn[NK * a:NK * (a + 1), 4 * p:4 * p + 4, 64 * a:64 * a + 64], kv[a, p]
                                 ).then_inc(s_keys, 16)
            sp.wait_ge(s_wz, 1)
            for dst, src in ((Wq_sb, Wq), (Wv_sb, Wv)):
                sp.dma_start(dst, src[:, :]).then_inc(s_w, 16)
            r = G = 2 * DH
            for g in range(VT):
                q, half = 32 * (g % 4), g // 4
                sp.dma_start(WoAB[q:q + r, half, :], Wo[G * g:G * g + r, :]).then_inc(s_w, 16)
                sp.dma_start(bvAB[q:q + r, half:half + 1], bv[G * g:G * g + r].rearrange("(d a) -> d a", a=1)
                             ).then_inc(s_w, 16)
            sp.dma_start(Wr[:, :], W_router[:, :]).then_inc(s_w, 16)
            sp.dma_start(brB[:, :], bass.AP(tensor=b_router.tensor, offset=0, ap=[[0, TT], [1, NE]])
                         ).then_inc(s_w, 16)
            sp.dma_start(b2s[:, :], b2.rearrange("e d -> d e"), allow_slow_non_contiguous=True).then_inc(s_w, 16)
            sp.dma_start(b1s[:, :], b1.rearrange("e (c p) -> p (e c)", p=P), allow_slow_non_contiguous=True
                         ).then_inc(s_w, 16)
            def load_key_parts(b):
                for c, (kx, _) in enumerate(PRODUCTS):
                    sp.dma_start(KP[b % 3][2 * DH * c:2 * DH * (c + 1), :, :],
                                 key_parts[b, kx].rearrange("(m r) i -> r m i", r=2 * DH)
                                 ).then_inc(s_kpl[b % 3], 16)

            for r in range(4):
                sp.wait_ge(s_kd[r], 16 * NKP // 4)
            sp.wait_ge(s_vc, NCH // 4 * NB)
            for b in range(2):
                load_key_parts(b)
            sp.wait_ge(s_qs, 1)
            sp.dma_start(query_parts.rearrange("x p n -> p x n"), QS).then_inc(s_qd, 16)
            sp.wait_ge(s_qd, 16)
            for c, (_, qx) in enumerate(PRODUCTS):
                sp.dma_start(QP[2 * DH * c:2 * DH * (c + 1), :, :, :].rearrange("r m b n -> r m (b n)"),
                             query_parts[qx].rearrange("(m r) n -> r m n", r=2 * DH)).then_inc(s_qp, 16)
            sp.wait_ge(s_otok, 4)
            load_key_parts(2)
            for b in range(3, NB):
                sp.wait_ge(s_s2, NCH * (b - 2))
                load_key_parts(b)
            sp.wait_ge(s_s2, NCH * (NB - NB % 3))
            sp.dma_start(W1s, W1.rearrange("e d f -> d e f")).then_inc(s_w12, 16)
            sp.dma_start(W2s, W2.rearrange("e (c p) d -> p (e c) d", p=P)).then_inc(s_w12, 16)
            sp.wait_ge(s_fc, 1)
            sp.dma_start(out.rearrange("b j d -> (b j) d").rearrange("(t p) d -> p t d", t=4),
                         x_tok[:, :, :]).then_inc(s_out, 16)
            sp.wait_ge(s_out, 16)

        @block.gpsimd
        def _(pool):
            n = 0

            def done(ins):
                nonlocal n
                n += 1
                ins.then_inc(s_pool, 1)

            done(nc.gpsimd.memset(ident[:, :], 0.0))
            done(nc.gpsimd.iota(pidx[:, :], [[1, 1]], base=0, channel_multiplier=1))
            done(nc.gpsimd.memset(first[:, :], 0.0))
            done(nc.gpsimd.memset(blk[:, :], 1.0))
            done(nc.gpsimd.iota(twice[:, :], [[1, 2 * C]], base=0, channel_multiplier=0,
                                allow_small_or_imprecise_dtypes=True))
            done(nc.gpsimd.iota(rowc2[:, :], [[2 * C, NS]], base=0, channel_multiplier=2,
                                allow_small_or_imprecise_dtypes=True))
            pool.wait_ge(s_pool, n)
            done(nc.gpsimd.affine_select(out=ident[:, :], in_=ident[:, :], compare_op=ALU.not_equal, fill=1.0,
                                         base=0, pattern=[[-1, P]], channel_multiplier=1))
            done(nc.gpsimd.affine_select(out=first[:, :], in_=first[:, :], compare_op=ALU.not_equal, fill=1.0,
                                         base=0, pattern=[[-LB, NB]], channel_multiplier=1))
            bv_ = blk[:, :].rearrange("p (b s) -> p b s", s=LB)
            done(nc.gpsimd.affine_select(out=bv_, in_=bv_, compare_op=ALU.is_ge, fill=0.0,
                                         base=0, pattern=[[-LB, NB], [0, LB]], channel_multiplier=1))
            pool.wait_ge(s_pool, n)
            nc.gpsimd.affine_select(out=bv_, in_=bv_, compare_op=ALU.is_ge, fill=0.0,
                                    base=LB - 1, pattern=[[LB, NB], [0, LB]], channel_multiplier=-1
                                    ).then_inc(s_const, 1)
            pool.wait_ge(s_bbe, 1)
            for b in range(NB):
                pool.wait_ge(s_aa, b + 1)
                if b >= 2:
                    pool.wait_ge(s_d2, b - 1)
                nc.gpsimd.tensor_tensor(
                    absum[:, b % 2, :].rearrange("c (s j) -> c s j", j=NJ),
                    aa[:, b, :].unsqueeze(2).broadcast_to([C, NS, NJ]),
                    bbB[:, b * NJ:(b + 1) * NJ].unsqueeze(1).broadcast_to([C, NS, NJ]), ALU.add).then_inc(s_ab, 1)
            pool.wait_ge(s_const, 3)
            three = lambda a: a.rearrange("p (t c) -> p t c", c=C)

            def where_to(k):
                pool.wait_ge(s_sgn, k + 1)
                nc.gpsimd.tensor_tensor(three(wk[k % 2][2][:, :]), view(twice1[:, :], [[0, TB], [1, C]]),
                                        three(wk[k % 2][0][:, :]), ALU.add).then_inc(s_where, 1)

            for k in range(NTB):
                if k >= 1:
                    where_to(k - 1)
                pool.wait_ge(s_scan, TB * (k + 1))
                if k >= 2:
                    pool.wait_ge(s_jump, k - 1)
                t = k * TB
                nc.gpsimd.tensor_tensor(three(wk[k % 2][0][:, :]), R_slot(t, TB, 1, C), R_slot(t, TB, 0, C),
                                        ALU.subtract).then_inc(s_jin, 1)
                nc.gpsimd.tensor_tensor(
                    three(wk[k % 2][1][:, :]), R_slot(t + 1, TB, 0, C),
                    three(mring[:, (k % 2) * TB * C:(k % 2 + 1) * TB * C]), ALU.subtract).then_inc(s_jin, 1)
            where_to(NTB - 1)
            for n in range(NKP + 1):
                if n == EARLY + 4:
                    pool.wait_ge(s_desk, 16 * LB)
                    pool.wait_ge(s_desk2, 16 * LB)
                    nc.gpsimd.memset(keyn, 0.0).then_inc(s_keyz, 1)
                if n < NKP:
                    pool.wait_ge(s_kev, n + 1)
                    nc.gpsimd.tensor_tensor(kf[:, n % 3, :], kf[:, n % 3, :], kq[:, n % 4, 0, :], ALU.subtract
                                            ).then_inc(s_kr, 1)
                if n >= 1:
                    pool.wait_ge(s_k2, n)
                    m = n - 1
                    nc.gpsimd.tensor_tensor(kq[:, m % 4, 2, :], kf[:, m % 3, :], kq[:, m % 4, 1, :], ALU.subtract
                                            ).then_inc(s_ks, 1)
            s_t = s_tabs
            done2 = lambda ins: ins.then_inc(s_t, 1)
            pool.wait_ge(s_lane32, 1)
            done2(nc.gpsimd.tensor_scalar(mk[:, 0:1], l32[:, :], float(DH), None, ALU.is_lt))
            done2(nc.gpsimd.tensor_scalar(mk2[:, :], l32[:, :], float(2 * DH), None, ALU.is_lt))
            pool.wait_ge(s_t, 2)
            done2(nc.gpsimd.tensor_tensor(mk[:, 1:2], mk2[:, :], mk[:, 0:1], ALU.subtract))
            done2(nc.gpsimd.tensor_scalar(mku[:, :], mk2[:, :], -1.0, 1.0, ALU.mult, ALU.add))
            done2(nc.gpsimd.memset(bvAB[:, :], 0.0))
            pool.wait_ge(s_ebc, 1)
            for i in range(NB // 2 * NS):
                g, s = i // NS, i % NS
                if i % 2 == 0:
                    continue
                if i >= A_RING:
                    pool.wait_ge(s_pm, i - A_RING + 1)
                nc.gpsimd.tensor_scalar(
                    Am[:, i % A_RING, :].rearrange("c (b j) -> c b j", j=NJ), EB[:, 2 * g:2 * g + 2, 0:NJ],
                    rowc2[:, s:s + 1], None, ALU.is_le).then_inc(s_am, 1)
            pool.wait_ge(s_uT, 1)
            for r in range(4):
                pool.wait_ge(s_kd[r], 16 * NKP // 4)
            nc.gpsimd.iota(kiota, [[0, 2 * NHK], [1, NK]], base=-NK, channel_multiplier=0,
                           allow_small_or_imprecise_dtypes=True)
            pool.wait_ge(s_t, 5)
            nc.gpsimd.memset(WoAB, 0.0).then_inc(s_wz, 1)
            vt = vals[:, 0:NCH * NB * VW].rearrange("p (c g w) -> p c g w", g=VT, w=VTW)
            done2(nc.gpsimd.memset(vt[:, :, :, 2 * DH], 1.0))
            done2(nc.gpsimd.memset(vals[:, NCH * NB * VW:], 0.0))
            done2(nc.gpsimd.memset(vt[:, NCH - 1::NCH, 0, 0:32 - VTW], 0.0))
            pool.wait_ge(s_t, 8)
            done2(nc.gpsimd.memset(QP[NPR:P, :, :, :], 0.0))
            pool.wait_ge(s_t, 9)
            done2(nc.gpsimd.memset(sel, 0.0))
            done2(nc.gpsimd.memset(identb, 0.0))
            pool.wait_ge(s_t, 11)
            selv = sel.rearrange("p (t m) -> p t m", m=32)
            done2(nc.gpsimd.affine_select(out=selv, in_=selv, compare_op=ALU.not_equal, fill=1.0, base=-2 * DH,
                                          pattern=[[-32, 4], [0, 32]], channel_multiplier=1))
            done2(nc.gpsimd.affine_select(out=identb, in_=identb, compare_op=ALU.not_equal, fill=1.0, base=0,
                                          pattern=[[-1, P]], channel_multiplier=1))
            for t in range(4):
                pool.wait_ge(s_idx, t + 1)
                for h in range(NHK):
                    c = t * NHK + h
                    nc.gpsimd.indirect_dma_start(
                        out=gath[:, t, h, :], out_offset=None, in_=w_tab[:, :],
                        in_offset=bass.IndirectOffsetOnAxis(ap=idx[:, c:c + 1], axis=0)).then_inc(s_gath[t], 16)
            pool.wait_ge(s_t, 13)
            pool.wait_ge(s_vc, NCH // 4 * NB)
            nc.gpsimd.memset(ctxT[NPR:P, 0:2 * KPW], 1.0 + 0x3F80 / 2.0 ** 23).then_inc(s_one, 1)
            pool.wait_ge(s_otok, 4)
            pool.wait_ge(s_one, 1)
            nc.gpsimd.memset(kp_words[2][NPR:P, :], 1.0 + 0x3F80 / 2.0 ** 23).then_inc(s_one, 1)
            pool.wait_ge(s_one, 2)
            nc.gpsimd.iota(eiota[:, :, :], [[0, 4], [1, NE]], base=-NE, channel_multiplier=0,
                           allow_small_or_imprecise_dtypes=True).then_inc(s_et, 1)
            nc.gpsimd.memset(prod[0:NE, :], 0.0).then_inc(s_et, 1)
            pool.wait_ge(s_et, 2)
            nc.gpsimd.affine_select(out=sele, in_=sele, compare_op=ALU.not_equal, fill=1.0, base=0,
                                    pattern=[[-1, NE], [0, P]], channel_multiplier=1).then_inc(s_et, 1)

        @block.scalar
        def _(act):
            act.dma_start(g4[:, 0:2], bass.AP(tensor=g_xattn.tensor, offset=0, ap=[[0, P], [1, 2]])
                          ).then_inc(s_small, 16)
            act.dma_start(g4[:, 2:4], bass.AP(tensor=g_ffn.tensor, offset=0, ap=[[0, P], [1, 2]])
                          ).then_inc(s_small, 16)
            act.wait_ge(s_small, 32)
            nc.scalar.activation(gt[:, :], g4[:, :], ACT.Tanh).then_inc(s_gate, 1)
            act.wait_ge(s_xT, 1)
            nc.scalar.activation(xT[:, :], ps[0][:, 0:TOK], ACT.Copy).then_inc(s_xTe, 1)
            act.wait_ge(s_var, 1)
            act.wait_ge(s_const, 3)
            nc.scalar.activation(rstd[:, :], ps[0][:, 0:TOK], ACT.Sqrt, bias=epsc[:, 0:1]).then_inc(s_std, 1)

            def dist_of(b):
                act.wait_ge(s_d2, b + 1)
                nc.scalar.activation(view(dist[:, :], [[JW, NS], [1, NJ]], b * BS + PADJ),
                                     dtmp[:, :].rearrange("c (s j) -> c s j", j=NJ), ACT.Sqrt
                                     ).then_inc(s_dist, 1)

            for b in range(NB):
                act.wait_ge(s_nat[b], 16)
                if b >= 1:
                    act.wait_ge(s_aa, b)
                nc.scalar.activation(sq[:, :], nat[:, b % RING, :, :].rearrange("c s d -> c (s d)"), ACT.Square
                                     ).then_inc(s_sq, 1)
                for n in range(NPIECE - 1):
                    act.wait_ge(s_ct, NPIECE * b + n + 1)
                    nc.scalar.activation(ctxT[:, b * NI + n * PIECE:b * NI + (n + 1) * PIECE],
                                         ps[1 + n][:, 0:PIECE], ACT.Copy).then_inc(s_ctA, 1)
                if b >= 1:
                    dist_of(b - 1)
            dist_of(NB - 1)

            def lane_distances(q):
                act.wait_ge(s_dt, q + 1)
                if q >= 2:
                    act.wait_ge(s_scan, DT_STEPS * (q - 1))
                nc.scalar.activation(dts[:, (q % 2) * PIECE:(q % 2 + 1) * PIECE], ps[q % 2][:, 0:PIECE],
                                     ACT.Copy).then_inc(s_dtc, 1)

            lane_distances(0)
            lane_distances(1)
            for k in range(NTB):
                if k + 2 < NTB:
                    lane_distances(k + 2)
                h, g = wk[k % 2][0], wk[k % 2][1]
                act.wait_ge(s_jin, 2 * k + 1)
                nc.scalar.activation(h[:, :], h[:, :], ACT.Sign, scale=-1.0).then_inc(s_act, 1)
                act.wait_ge(s_act, 2 * k + 1)
                nc.scalar.activation(h[:, :], h[:, :], ACT.Relu).then_inc(s_sgn, 1)
                act.wait_ge(s_jin, 2 * k + 2)
                nc.scalar.activation(g[:, :], g[:, :], ACT.Copy, scale=1.0e14, bias=1.0).then_inc(s_act, 1)
            act.wait_ge(s_jump, NTB)
            act.wait_ge(s_wk, 16 * 4)
            for n in range(NKP + 2):
                if n < NKP:
                    act.wait_ge(s_kp, n + 1)
                    if n >= 3:
                        act.wait_ge(s_ks, n - 2)
                    if n >= 4:
                        act.wait_ge(s_kd[n % 4], 16 * (n // 4))
                    bank = ps[1 + n % 3][:, 0:KPIECE]
                    nc.scalar.activation(kf[:, n % 3, :], bank, ACT.Identity, bias=cols[:, 1:2])
                    nc.scalar.activation(kq[:, n % 4, 0, :], bank, ACT.Identity, bias=cols[:, 1:2]
                                         ).then_inc(s_kev, 1)
                if 1 <= n <= NKP:
                    m = n - 1
                    act.wait_ge(s_kr, n)
                    nc.scalar.activation(kq[:, m % 4, 1, :], kf[:, m % 3, :], ACT.Copy).then_inc(s_k2, 1)
                if n >= 2:
                    m = n - 2
                    act.wait_ge(s_ks, n - 1)
                    i = m % KPB * KPIECE
                    act.dma_start(key_parts[m // KPB, :, :, i:i + KPIECE].rearrange("x p i -> p x i"),
                                  kq[:, m % 4, :, :]).then_inc(s_kd[m % 4], 16)
            act.wait_ge(s_foldT, 1)
            nc.scalar.activation(wqT[:, 0:FOLD // 2], ps[1], ACT.Copy)
            nc.scalar.activation(wqT[:, FOLD // 2:], ps[2], ACT.Copy)
            nc.scalar.activation(keyT[:, :], ps[7], ACT.Copy).then_inc(s_foldc, 1)
            for half in range(2):
                act.wait_ge(s_ex, 2 * half + 2)
                for par in range(2):
                    nc.scalar.activation(U[64 * par:64 * par + NJ, 2 * half:2 * half + 2, :],
                                         ps[6 + half][64 * par:64 * par + NJ, 0:2 * D].rearrange(
                                             "p (t d) -> p t d", d=D), ACT.Copy).then_inc(s_u, 1)
                if half == 0:
                    act.wait_ge(s_fold, 1)
                    nc.scalar.activation(fold[:, :], ps[1], ACT.Copy).then_inc(s_fold_sb, 1)

            def deviation(k):
                act.wait_ge(s_var, k + 1)
                nc.scalar.activation(rstd[:, :], ps[0][:, 0:TOK], ACT.Sqrt, bias=epsc[:, 0:1]).then_inc(s_std, 1)

            deviation(1)
            act.wait_ge(s_xnk, 1)
            nc.scalar.activation(x_tok[:, :, :], ps[4][0:TT, :].rearrange("p (t d) -> p t d", d=D), ACT.Copy
                                 ).then_inc(s_xnc, 1)
            if stage >= 3:
                act.wait_ge(s_tabs, 13)
                for b in range(NB):
                    for i in range(NCH // 4):
                        n = b * (NCH // 4) + i
                        act.wait_ge(s_vp, n + 1)
                        tail = NI - (NCH - 1) * P if i == NCH // 4 - 1 else P
                        for r, c0, c1 in ((P, 0, 4),) if tail == P else ((P, 0, 3), (tail, 3, 4)):
                            dst = vals[0:r, (b * NCH + 4 * i + c0) * VW:(b * NCH + 4 * i + c1) * VW].rearrange(
                                "p (c g w) -> p c g w", g=VT, w=VTW)
                            last = nc.scalar.activation(
                                dst[:, :, :, 0:2 * DH],
                                ps[4 + n % 2][0:r, c0 * D:c1 * D].rearrange("p (c g w) -> p c g w", g=VT, w=2 * DH),
                                ACT.Copy)
                        last.then_inc(s_vc, 1)
            for t in range(4):
                act.wait_ge(s_hcol, t + 1)
                nc.scalar.activation(hcol[:, t, :], hcol[:, t, :], ACT.Gelu).then_inc(s_gelu, 1)
            if stage >= 3:
                deviation(2)

                def maxima_rows(b):
                    act.wait_ge(s_nmt, b + 1)
                    nc.scalar.activation(QP[NPR:NPR + 3, :, b, :], maxrows[b % 2], ACT.Copy).then_inc(s_nmc, 1)

                def head_sums(b):
                    act.wait_ge(s_pv, NCH * (b + 1))
                    if b >= 1:
                        act.wait_ge(s_ob, b)
                    nc.scalar.activation(Osb.rearrange("p a m q -> p (a m q)"), ps[6 + b % 2][:, 0:4 * NJ], ACT.Copy
                                         ).then_inc(s_oc, 1)

                maxima_rows(0)
                for b in range(NB):
                    for c in range(NCH):
                        g = b * NCH + c
                        rows = min(P, NI - c * P)
                        act.wait_ge(s_s2, g + 1)
                        if g >= 2:
                            act.wait_ge(s_pv, g - 1)
                        nc.scalar.activation(
                            Pt[0:rows, g % 2, :].rearrange("p (a n) -> p a n", a=2),
                            banks[0:rows, 2 + 2 * (g % 2):4 + 2 * (g % 2), 0:HQ // 2], ACT.Exp,
                            scale=float(DH) ** -0.5).then_inc(s_exp, 1)
                        if c == 1 and b >= 1:
                            head_sums(b - 1)
                        if c == MAXROW_AT and b + 1 < NB:
                            maxima_rows(b + 1)
                head_sums(NB - 1)
            if stage >= 4:
                deviation(3)
                def hidden(i):
                    act.wait_ge(s_h, i + 1)
                    if i >= 4:
                        act.wait_ge(s_yu, i - 3)
                    nc.scalar.activation(hT[:, i % 4, :], ps[5 + i % 2][:, 0:TOK], ACT.Relu, bias=b1s[:, i:i + 1]
                                         ).then_inc(s_hc, 1)

                hidden(0)
                hidden(1)
                act.wait_ge(s_lgd, 1)
                nc.scalar.activation(rs[:, 5, :], rs[:, 4, :], ACT.Exp).then_inc(s_lge, 1)
                hidden(2)
                hidden(3)
                act.wait_ge(s_wtT, 1)
                nc.scalar.activation(wT, ps[2][0:NE, 0:TOK], ACT.Copy).then_inc(s_wtc, 1)
                for e in range(NE):
                    if e + 1 < NE:
                        hidden(FC * (e + 1))
                    act.wait_ge(s_wb, e + 1)
                    if e >= 2:
                        act.wait_ge(s_yc, e - 1)
                    nc.scalar.activation(wBs[:, e % 2, :], ps[3 + e % 2][:, 0:TOK], ACT.Copy).then_inc(s_wbc, 1)
                    if e + 1 < NE:
                        for i in range(1, FC):
                            hidden(FC * (e + 1) + i)
            act.wait_ge(s_fT, 1)
            nc.scalar.activation(x_tok[:, :, :], ps[1][0:TT, :].rearrange("p (t d) -> p t d", d=D), ACT.Copy
                                 ).then_inc(s_fc, 1)

        @block.vector
        def _(ve):
            n = 0

            def link(ins):
                nonlocal n
                n += 1
                ins.then_inc(s_dve, 1)
                ve.wait_ge(s_dve, n)

            nc.vector.memset(meanw[:, :], 1.0 / D)
            nc.vector.memset(ones[:, :], 1.0)
            nc.vector.memset(epsc[:, :], EPS)
            nc.vector.memset(e_last[:, :], 2.0 * (NI - 1))
            nc.vector.memset(view(dist[:, :], [[BS, NB], [JW, NS], [1, PADJ]]), BIG)
            nc.vector.memset(view(dist[:, :], [[BS, NB], [1, BS - NS * JW]], NS * JW), BIG)
            nc.vector.memset(dist[:, NB * BS:NB * BS + P], BIG)
            link(nc.vector.memset(gate[:, :], 1.0))
            nc.vector.memset(pad0[:, :], 0.0).then_inc(s_const, 1)
            ve.wait_ge(s_pool, 6)
            link(nc.vector.tensor_scalar(lane_i[:, :], pidx[:, :], LB - 1, None, ALU.bitwise_and))
            link(nc.vector.tensor_copy(lane[:, :], lane_i[:, :]))
            link(nc.vector.tensor_scalar(lane_i[:, :], pidx[:, :], 31, None, ALU.bitwise_and))
            nc.vector.tensor_copy(l32[:, :], lane_i[:, :]).then_inc(s_lane32, 1)
            ve.wait_ge(s_lane32, 1)
            link(nc.vector.tensor_scalar(lane_i[:, :], pidx[:, :], DH, None, ALU.bitwise_and))
            link(nc.vector.tensor_copy(hm[:, 0:1], lane_i[:, :]))
            link(nc.vector.tensor_scalar(hm[:, 1:2], hm[:, 0:1], 0.0, None, ALU.is_gt))
            link(nc.vector.tensor_scalar(hm[:, 0:1], hm[:, 1:2], 0.0, None, ALU.is_equal))
            for i in range(4):
                nc.vector.tensor_scalar(lmask[:, i:i + 1], lane[:, :], float(1 << i), None, ALU.is_ge)
            nc.vector.memset(view(gate[:, :], [[SLOT, TB], [1, 1]]), 0.0)
            link(nc.vector.memset(R[:, 0:SLOT], BIG))
            link(nc.vector.tensor_scalar(R[:, 0:1], lane[:, :], 0.0, BIG, ALU.is_gt, ALU.mult))
            nc.vector.scalar_tensor_tensor(out=twice[:, :], in0=lane[:, 0:1].broadcast_to([P, 2 * C]),
                                           scalar=2.0 * C, in1=twice[:, :], op0=ALU.mult, op1=ALU.add
                                           ).then_inc(s_dve, 1)
            n += 1
            ve.wait_ge(s_dve, n)
            nc.vector.tensor_scalar(twice1[:, :], view(twice[:, :], [[2, C]]), -1.0, None, ALU.add
                                    ).then_inc(s_const, 1)

            def layernorm(k):
                ve.wait_ge(s_mean, k + 1)
                link(nc.vector.tensor_tensor(xc[:, :], xT[:, :], ps[0][:, 0:TOK], ALU.subtract))
                nc.vector.tensor_tensor(xsq[:, :], xc[:, :], xc[:, :], ALU.mult).then_inc(s_cen, 1)
                ve.wait_ge(s_std, k + 1)
                link(nc.vector.reciprocal(rstd[:, :], rstd[:, :]))
                nc.vector.tensor_tensor(xnT[:, :], xc[:, :], rstd[:, :], ALU.mult).then_inc(s_xn, 1)
                ve.wait_ge(s_xn, k + 1)

            layernorm(0)
            nc.vector.tensor_scalar(xm2[:, :], xnT[:, :], -2.0, None, ALU.mult)
            nc.vector.tensor_tensor(xsq[:, :], xnT[:, :], xnT[:, :], ALU.mult).then_inc(s_cen, 1)
            ve.wait_ge(s_bb, 1)
            nc.vector.tensor_copy(bbB[:, :], ps[0][0:C, 0:TOK]).then_inc(s_bbe, 1)

            def d2_of(b):
                ve.wait_ge(s_dot, b + 1)
                ve.wait_ge(s_ab, b + 1)
                if b >= 1:
                    ve.wait_ge(s_dist, b)
                for part, (lo, hi) in enumerate(((0, 8), (8, NS))):
                    bank = ps[4 + 2 * (b % 2) + part]
                    last = nc.vector.tensor_tensor(dtmp[:, lo * NJ:hi * NJ], bank[0:C, 0:(hi - lo) * NJ],
                                                   absum[:, b % 2, lo * NJ:hi * NJ], ALU.add)
                link(last)
                nc.vector.tensor_scalar(dtmp[:, :], dtmp[:, :], 0.0, None, ALU.max).then_inc(s_d2, 1)

            for b in range(NB):
                ve.wait_ge(s_sq, b + 1)
                nc.vector.tensor_reduce(aa[:, b, :], sq[:, :].rearrange("c (s d) -> c s d", d=D), AX_X, ALU.add
                                        ).then_inc(s_aa, 1)
                ve.wait_ge(s_ct, NPIECE * (b + 1))
                nc.vector.tensor_copy(ctxT[:, b * NI + 2 * PIECE:(b + 1) * NI], ps[3][:, 0:PIECE]
                                      ).then_inc(s_ctV, 1)
                if b >= 1:
                    d2_of(b - 1)
            d2_of(NB - 1)

            def memory_layer():
                layernorm(1)
                ve.wait_ge(s_wz, 1)
                for t in range(4):
                    ve.wait_ge(s_sim, t + 1)
                    sims = ps[t][0:TT, :].rearrange("p (g k) -> p g k", k=NK)
                    eq = prod[0:TT, 0:2 * NHK * NK]
                    eq3 = eq.rearrange("p (g k) -> p g k", k=NK)
                    link(nc.vector.tensor_reduce(mxs[:, t, :], sims, AX_X, ALU.max))
                    link(nc.vector.tensor_tensor(eq3, sims, mxs[:, t, :].unsqueeze(2).broadcast_to(
                        [TT, 2 * NHK, NK]), ALU.is_equal))
                    link(nc.vector.tensor_tensor(eq, eq, kiota, ALU.mult))
                    link(nc.vector.tensor_reduce(ixs[:, t, :], eq3, AX_X, ALU.min))
                    link(nc.vector.scalar_tensor_tensor(out=idxf[:, t, :], in0=ixs[:, t, 0:NHK], scalar=float(NK),
                                                        in1=ixs[:, t, NHK:], op0=ALU.mult, op1=ALU.add))
                    nc.vector.tensor_scalar(idx[:, t * NHK:(t + 1) * NHK], idxf[:, t, :], float(NK * NK + NK), None,
                                            ALU.add).then_inc(s_idx, 1)
                link(nc.vector.tensor_tensor(score[:, :, :], mxs[:, :, 0:NHK], mxs[:, :, NHK:], ALU.add))
                link(nc.vector.tensor_scalar(score[:, :, :], score[:, :, :], 0.0, None, ALU.max))
                ve.wait_ge(s_xnc, 1)
                pr = prod[0:TT, :].rearrange("p (h d) -> p h d", d=D)

                def down(t):
                    ve.wait_ge(s_gath[t], 16 * NHK)
                    link(nc.vector.tensor_tensor(pr, gath[:, t, :, 0:D], x_tok[:, t, :].unsqueeze(1).broadcast_to(
                        [TT, NHK, D]), ALU.mult))
                    nc.vector.tensor_reduce(hcol[:, t, :], pr, AX_X, ALU.add).then_inc(s_hcol, 1)
                    ve.wait_ge(s_hcol, t + 1)

                def up(t):
                    ve.wait_ge(s_gelu, t + 1)
                    link(nc.vector.tensor_tensor(hcol[:, t, :], hcol[:, t, :], score[:, t, :], ALU.mult))
                    link(nc.vector.tensor_tensor(pr, gath[:, t, :, D:], hcol[:, t, :].unsqueeze(2).broadcast_to(
                        [TT, NHK, D]), ALU.mult))
                    nc.vector.tensor_reduce(x_tok[:, t, :], view(prod[0:TT, :], [[1, D], [D, NHK]]), AX_X, ALU.add
                                            ).then_inc(s_otok, 1)
                    ve.wait_ge(s_otok, t + 1)

                down(0)
                for t in range(1, 4):
                    down(t)
                    up(t - 1)
                up(3)
                ve.wait_ge(s_oT, 1)
                nc.vector.scalar_tensor_tensor(out=xT[:, :], in0=ps[0][:, 0:TOK], scalar=gt[:, 2:3],
                                               in1=xT[:, :], op0=ALU.mult, op1=ALU.add).then_inc(s_xr, 1)
                ve.wait_ge(s_xr, 2)

            def attention_layer():
                layernorm(2)
                ve.wait_ge(s_q, 1)
                q4 = Qm.rearrange("p (b a q) -> p b a q", b=NB, a=2)
                q1 = ps[1][:, 0:TOK].rearrange("p (b q) -> p b q", q=NJ)
                nc.vector.tensor_scalar(q4[:, :, 0, :], q1, cols[:, 0:1], hm[:, 0:1], ALU.add, ALU.mult)
                link(nc.vector.tensor_scalar(q4[:, :, 1, :], q1, cols[:, 0:1], hm[:, 1:2], ALU.add, ALU.mult))
                link(nc.vector.tensor_copy(QS[:, 0, :], Qm))
                link(nc.vector.tensor_tensor(Qm, Qm, QS[:, 0, :], ALU.subtract))
                link(nc.vector.tensor_copy(QS[:, 1, :], Qm))
                nc.vector.tensor_tensor(QS[:, 2, :], Qm, QS[:, 1, :], ALU.subtract).then_inc(s_qs, 1)

                def reduce_scores(b, u):
                    k = b * UNITS + u
                    ve.wait_ge(s_s1, k + 1)
                    nc.vector.tensor_reduce(mx3[:, b % 2, u // NPIECE, u % NPIECE:u % NPIECE + 1],
                                            ps[k % (6 if b == 0 else 2)][0:2 * NJ, 0:PIECE], AX_X, ALU.max
                                            ).then_inc(s_mx, 1)

                def split_maxima(b, step):
                    if step == 0:
                        ve.wait_ge(s_mx, UNITS * (b + 1))
                        chained(nc.vector.tensor_reduce(nmx[:, :], mx3[:, b % 2, :, :], AX_X, ALU.max))
                    elif step == 1:
                        chained(nc.vector.tensor_scalar(nmx[:, :], nmx[:, :], -1.0, None, ALU.mult))
                    elif step in (2, 4, 6):
                        if step == 2 and b >= 1:
                            ve.wait_ge(s_nmt, b)
                        ins = nc.vector.tensor_copy(npart[:, :, step // 2 - 1], nmx[:, :])
                        if step == 6:
                            ins.then_inc(s_np, 1)
                        else:
                            chained(ins)
                    else:
                        chained(nc.vector.tensor_tensor(nmx[:, :], nmx[:, :], npart[:, :, step // 2 - 1],
                                                        ALU.subtract))

                def normalize(b, step):
                    den = ps[6 + b % 2][:, 256:256 + 4 * NJ].rearrange("p (a m q) -> p a m q", a=2, m=2)
                    two = lambda i: nd[:, i, :].rearrange("p (a q) -> p a q", a=2)
                    if step == 0:
                        ve.wait_ge(s_den, b + 1)
                        nc.vector.tensor_scalar(num[:, 0, :, :], Osb[:, :, 0, :], mk[:, 0:1], None, ALU.mult)
                        chained(nc.vector.tensor_scalar(num[:, 1, :, :], den[:, :, 0, :], mk[:, 0:1], mku[:, 0:1],
                                                        ALU.mult, ALU.add))
                    elif step == 1:
                        for i, src in enumerate((Osb, den)):
                            last = nc.vector.scalar_tensor_tensor(
                                out=two(i), in0=src[:, :, 1, :], scalar=mk[:, 1:2], in1=num[:, i, :, :],
                                op0=ALU.mult, op1=ALU.add)
                        chained(last)
                    elif step == 2:
                        chained(nc.vector.reciprocal(nd[:, 1, :], nd[:, 1, :]))
                    elif step == 3:
                        chained(nc.vector.tensor_tensor(two(0), two(0), two(1), ALU.mult))
                    else:
                        nc.vector.tensor_tensor(OAB[:, :, b * NJ:(b + 1) * NJ], two(0),
                                                bvAB[:, :].unsqueeze(2).broadcast_to([P, 2, NJ]), ALU.add
                                                ).then_inc(s_ob, 1)

                def chained(ins):
                    nonlocal n
                    n += 1
                    ins.then_inc(s_dve, 1)

                for u in range(UNITS):
                    reduce_scores(0, u)
                for step in range(7):
                    ve.wait_ge(s_dve, n)
                    split_maxima(0, step)
                for k in range(UNITS, NB * UNITS):
                    b, u = k // UNITS, k % UNITS
                    reduce_scores(b, u)
                    if b >= 2 and u < 4:
                        for step in range(2 * u, min(2 * u + 2, 7)):
                            ve.wait_ge(s_dve, n)
                            split_maxima(b - 1, step)
                    if b >= 2 and 18 <= u < 23:
                        ve.wait_ge(s_dve, n)
                        normalize(b - 2, u - 18)
                for step in range(7):
                    ve.wait_ge(s_dve, n)
                    split_maxima(NB - 1, step)
                for b in (NB - 2, NB - 1):
                    for step in range(5):
                        ve.wait_ge(s_dve, n)
                        normalize(b, step)
                ve.wait_ge(s_np, NB)
                ve.wait_ge(s_ob, NB)
                ve.wait_ge(s_wo, 1)
                link(nc.vector.tensor_scalar(xc[:, :], ps[0][:, 0:TOK], cols[:, 2:3], None, ALU.add))
                nc.vector.scalar_tensor_tensor(out=xT[:, :], in0=xc[:, :], scalar=gt[:, 1:2], in1=xT[:, :],
                                               op0=ALU.mult, op1=ALU.add).then_inc(s_xr, 1)
                ve.wait_ge(s_xr, 3)

            def expert_layer():
                layernorm(3)
                ve.wait_ge(s_lg, 1)
                ve.wait_ge(s_et, 1)
                e4 = lambda i: lg[:, i, :].rearrange("p (t e) -> p t e", e=NE)
                wide = lambda a: a.unsqueeze(2).broadcast_to([TT, 4, NE])
                link(nc.vector.tensor_tensor(e4(0), ps[1][0:TT, 0:4 * NE].rearrange("p (t e) -> p t e", e=NE),
                                             brB[:, :].unsqueeze(1).broadcast_to([TT, 4, NE]), ALU.add))
                for i in range(2):
                    link(nc.vector.tensor_reduce(rs[:, i, :], e4(0), AX_X, ALU.max))
                    link(nc.vector.tensor_tensor(e4(3), e4(0), wide(rs[:, i, :]), ALU.is_equal))
                    link(nc.vector.tensor_tensor(e4(3), e4(3), eiota[:, :, :], ALU.mult))
                    link(nc.vector.tensor_reduce(rs[:, 2 + i, :], e4(3), AX_X, ALU.min))
                    link(nc.vector.tensor_tensor(e4(1 + i), eiota[:, :, :], wide(rs[:, 2 + i, :]), ALU.is_equal))
                    if i == 0:
                        link(nc.vector.scalar_tensor_tensor(out=lg[:, 0, :], in0=lg[:, 1, :], scalar=-3.0e38,
                                                            in1=lg[:, 0, :], op0=ALU.mult, op1=ALU.add))
                nc.vector.tensor_tensor(rs[:, 4, :], rs[:, 1, :], rs[:, 0, :], ALU.subtract).then_inc(s_lgd, 1)
                ve.wait_ge(s_lge, 1)
                link(nc.vector.tensor_scalar(rs[:, 6, :], rs[:, 5, :], 1.0, None, ALU.add))
                link(nc.vector.reciprocal(rs[:, 7, :], rs[:, 6, :]))
                link(nc.vector.tensor_tensor(e4(2), e4(2), wide(rs[:, 5, :]), ALU.mult))
                link(nc.vector.tensor_tensor(lg[:, 1, :], lg[:, 1, :], lg[:, 2, :], ALU.add))
                nc.vector.tensor_tensor(e4(4), e4(1), wide(rs[:, 7, :]), ALU.mult).then_inc(s_rw, 1)
                for e in range(NE):
                    ve.wait_ge(s_yu, FC * (e + 1))
                    ve.wait_ge(s_wbc, e + 1)
                    dst = xsq if e == 0 else xc
                    ins = nc.vector.scalar_tensor_tensor(
                        out=dst[:, :], in0=ps[7 if e % 2 else 0][:, 0:TOK], scalar=b2s[:, e:e + 1],
                        in1=wBs[:, e % 2, :], op0=ALU.add, op1=ALU.mult)
                    ins.then_inc(s_yc, 1)
                    ve.wait_ge(s_yc, e + 1)
                    if e:
                        link(nc.vector.tensor_tensor(xsq[:, :], xsq[:, :], xc[:, :], ALU.add))
                nc.vector.scalar_tensor_tensor(out=xT[:, :], in0=xsq[:, :], scalar=gt[:, 3:4], in1=xT[:, :],
                                               op0=ALU.mult, op1=ALU.add).then_inc(s_xr, 1)

            shift = [LB - 1] + list(range(LB - 1)) + [2 * LB - 1] + list(range(LB, 2 * LB - 1))

            def jumps(k):
                t = k * TB
                h, g, w = wk[k % 2]
                ve.wait_ge(s_act, 2 * k + 2)
                link(nc.vector.tensor_tensor(g[:, :], g[:, :], h[:, :], ALU.is_gt))
                ve.wait_ge(s_where, k + 1)
                nc.vector.tensor_tensor(R_slot(t, TB, 1, C), g[:, :].rearrange("p (t c) -> p t c", c=C),
                                        w[:, :].rearrange("p (t c) -> p t c", c=C), ALU.mult).then_inc(s_jump, 1)

            for t in range(STEPS):
                if t % TB == 0 and t // TB >= 2:
                    jumps(t // TB - 2)
                m = mring[:, (t % (2 * TB)) * C:(t % (2 * TB) + 1) * C]
                if t >= 1:
                    ve.wait_ge(s_scan, t)
                nc.vector.tensor_tensor(m, R_slot(t, 1, 1, C), R_slot(t, 1, 0, C), ALU.min)
                link(nc.vector.stream_shuffle(R_slot(t + 1, 1, 0, 1), R_slot(t, 1, C, 1), shift))
                if t % DT_STEPS == 0:
                    ve.wait_ge(s_dtc, t // DT_STEPS + 1)
                d = dts[:, (t % (2 * DT_STEPS)) * C:(t % (2 * DT_STEPS) + 1) * C]
                nc.vector.tensor_tensor_scan(view(R, [[1, C]], (t + 1) * SLOT + 1), m, d,
                                             R[:, (t + 1) * SLOT:(t + 1) * SLOT + 1], ALU.min, ALU.add
                                             ).then_inc(s_scan, 1)
            jumps(NTB - 2)
            jumps(NTB - 1)
            ve.wait_ge(s_jump, NTB)
            link(nc.vector.tensor_reduce(hops[:, 0, 0:STEPS], R_slot(0, STEPS, 1, C), AX_X, ALU.max))
            for i in range(4):
                k = 1 << i
                a, b_ = hops[:, i % 2, :], hops[:, (i + 1) % 2, :]
                mask = list(range(32))
                for h in range(2):
                    for s in range(LB):
                        mask[h * LB + s] = h * LB + (s - k if s >= k else s)
                nc.vector.tensor_copy(b_[:, 0:k], a[:, 0:k])
                link(nc.vector.stream_shuffle(shf[:, 0:STEPS - k], a[:, 0:STEPS - k], mask))
                link(nc.vector.scalar_tensor_tensor(out=b_[:, k:STEPS], in0=shf[:, 0:STEPS - k],
                                                    scalar=lmask[:, i:i + 1], in1=a[:, k:STEPS],
                                                    op0=ALU.mult, op1=ALU.max))
            mask = [LB - 1] + list(range(LB - 1)) + [2 * LB - 1] + list(range(LB, 2 * LB - 1))
            nc.vector.memset(R[:, 0:1], 0.0)
            link(nc.vector.stream_shuffle(shf[:, 0:STEPS - 1], hops[:, 0, 0:STEPS - 1], mask))
            link(nc.vector.tensor_scalar(view(R[:, :], [[SLOT, STEPS - 1], [1, 1]], SLOT),
                                         shf[:, 0:STEPS - 1].unsqueeze(2), lmask[:, 0:1], None, ALU.mult))
            for k in range(NTB):
                v = R[:, k * TB * SLOT:(k + 1) * TB * SLOT]
                last = nc.vector.tensor_tensor_scan(v, gate[:, :], v, 0.0, ALU.mult, ALU.max)
            last.then_inc(s_carry, 1)

            nc.vector.memset(zt, 0.0)
            nc.vector.memset(U, 0.0)
            ve.wait_ge(s_desk, 16 * LB)
            for j in range(NJ - 1, 0, -1):
                if j < NJ - 1:
                    ve.wait_ge(s_hop, NJ - 1 - j)
                if j == NJ // 2 - 1:
                    ve.wait_ge(s_desk2, 16 * LB)
                e = e_last[:, 0:1] if j == NJ - 1 else ps[4][:, j + 1:j + 2]
                nc.vector.scalar_tensor_tensor(
                    out=mring[:, 6 * C:8 * C].rearrange("p (c k) -> p c k", k=2),
                    in0=twice[:, :].rearrange("p (c k) -> p c k", k=2), scalar=e,
                    in1=view(jump[:, :], [[1, C], [0, 2]], j * C),
                    op0=ALU.is_equal, op1=ALU.mult, accum_out=acc[:, j:j + 1]).then_inc(s_hit, 1)
            ve.wait_ge(s_hop, NJ - 1)
            nc.vector.tensor_tensor(zt[:, :, 1:NJ], ps[4][:, 1:NJ].unsqueeze(1).broadcast_to([P, NB, NJ - 1]),
                                    first[:, :].unsqueeze(2).broadcast_to([P, NB, NJ - 1]), ALU.mult)
            nc.vector.tensor_scalar(zt[:, :, NJ:NJ + 1], first[:, :].unsqueeze(2), 2.0 * (NI - 1), None, ALU.mult
                                    ).then_inc(s_z, 1)
            ve.wait_ge(s_eb, 1)
            nc.vector.tensor_copy(EB[:, :, :], ps[5][0:C, 0:NB * (NJ + 1)].rearrange(
                "c (b j) -> c b j", b=NB)).then_inc(s_ebc, 1)
            ve.wait_ge(s_ebc, 1)
            def path_starts(i):
                g, s = i // NS, i % NS
                if i >= A_RING:
                    ve.wait_ge(s_pm, i - A_RING + 1)
                nc.vector.tensor_scalar(
                    Am[:, i % A_RING, :].rearrange("c (b j) -> c b j", j=NJ), EB[:, 2 * g:2 * g + 2, 0:NJ],
                    rowc2[:, s:s + 1], None, ALU.is_le).then_inc(s_amv, 1)

            path_starts(0)
            for i in range(NB // 2 * NS):
                g, s = i // NS, i % NS
                if i % 2 == 0 and i + 2 < NB // 2 * NS:
                    path_starts(i + 2)
                if s == 0 and g >= 2:
                    ve.wait_ge(s_ex, g - 1)
                if i % 2:
                    ve.wait_ge(s_am, i // 2 + 1)
                else:
                    ve.wait_ge(s_amv, i // 2 + 1)
                nc.vector.scalar_tensor_tensor(
                    out=Pm[:, g % 2, s, :].rearrange("c (b j) -> c b j", j=NJ),
                    in0=EB[:, 2 * g:2 * g + 2, 1:NJ + 1], scalar=rowc2[:, s:s + 1],
                    in1=Am[:, i % A_RING, :].rearrange("c (b j) -> c b j", j=NJ), op0=ALU.is_ge, op1=ALU.mult
                    ).then_inc(s_pm, 1)
            ve.wait_ge(s_uT, 1)
            ve.wait_ge(s_gate, 1)
            nc.vector.scalar_tensor_tensor(
                out=xT[:, :].rearrange("p (t a j) -> p t a j", a=2, j=NJ)[:, :, 0, :],
                in0=ps[3][:, :].rearrange("p (t a j) -> p t a j", a=2, j=64)[:, :, 0, 0:NJ],
                scalar=gt[:, 0:1],
                in1=xT[:, :].rearrange("p (t a j) -> p t a j", a=2, j=NJ)[:, :, 0, :],
                op0=ALU.mult, op1=ALU.add)
            link(nc.vector.scalar_tensor_tensor(
                out=xT[:, :].rearrange("p (t a j) -> p t a j", a=2, j=NJ)[:, :, 1, :],
                in0=ps[3][:, :].rearrange("p (t a j) -> p t a j", a=2, j=64)[:, :, 1, 0:NJ],
                scalar=gt[:, 0:1],
                in1=xT[:, :].rearrange("p (t a j) -> p t a j", a=2, j=NJ)[:, :, 1, :],
                op0=ALU.mult, op1=ALU.add))
            nc.vector.memset(pad0[:, :], 0.0).then_inc(s_xr, 1)
            if stage >= 2:
                memory_layer()
            if stage >= 3:
                attention_layer()
            if stage >= 4:
                expert_layer()

        @block.tensor
        def _(pe):
            pe.wait_ge(s_x, 16)
            pe.wait_ge(s_pool, 9)
            pe.wait_ge(s_const, 3)
            for t in range(4):
                last = nc.tensor.transpose(ps[0][:, t * TT:(t + 1) * TT], x_tok[:, t, :], ident[0:TT, 0:TT])
            last.then_inc(s_xT, 1)

            def layernorm_sums(k):
                nc.tensor.matmul(ps[0][:, 0:TOK], meanw[:, :], xT[:, :], start=True, stop=True
                                 ).then_inc(s_mean, 1)
                pe.wait_ge(s_cen, k + 1 + (k > 0))
                nc.tensor.matmul(ps[0][:, 0:TOK], meanw[:, :], xsq[:, :], start=True, stop=True
                                 ).then_inc(s_var, 1)

            pe.wait_ge(s_xTe, 1)
            layernorm_sums(0)
            pe.wait_ge(s_cen, 2)
            nc.tensor.matmul(ps[0][0:C, 0:TOK], ones[:, 0:C], xsq[:, :], start=True, stop=True).then_inc(s_bb, 1)

            def dots(b):
                pe.wait_ge(s_ctA, (NPIECE - 1) * (b + 1))
                pe.wait_ge(s_ctV, b + 1)
                if b >= 2:
                    pe.wait_ge(s_d2, b - 1)
                for s in range(NS):
                    bank, o = (ps[4 + 2 * (b % 2)], s) if s < 8 else (ps[5 + 2 * (b % 2)], s - 8)
                    last = nc.tensor.matmul(bank[0:C, o * NJ:(o + 1) * NJ],
                                            ctxT[:, b * NI + s * C:b * NI + (s + 1) * C],
                                            xm2[:, b * NJ:(b + 1) * NJ], start=True, stop=True)
                last.then_inc(s_dot, 1)

            for b in range(NB):
                pe.wait_ge(s_nat[b], 16)
                for n in range(NPIECE):
                    if b >= 1:
                        if n < NPIECE - 1:
                            pe.wait_ge(s_ctA, (NPIECE - 1) * (b - 1) + n + 1)
                        else:
                            pe.wait_ge(s_ctV, b)
                    for i in range(SPP):
                        last = nc.tensor.transpose(ps[1 + n][:, i * C:(i + 1) * C],
                                                   nat[:, b % RING, n * SPP + i, :], ident[0:C, 0:C])
                    last.then_inc(s_ct, 1)
                if b >= 1:
                    dots(b - 1)
            dots(NB - 1)
            pe.wait_ge(s_dist, NB)
            pe.wait_ge(s_bbe, 1)
            for q in range(STEPS // DT_STEPS):
                if q >= 2:
                    pe.wait_ge(s_dtc, q - 1)
                for i in range(DT_STEPS):
                    t = q * DT_STEPS + i
                    src = view(dist[:, :], [[JW - 1, P]], t + PADJ)
                    last = nc.tensor.transpose(ps[q % 2][:, i * C:(i + 1) * C], src, ident[0:C, 0:C])
                last.then_inc(s_dt, 1)
            pe.wait_ge(s_wk, 16 * 4)

            def keys_of(n, part):
                if n >= 3 and part == 0:
                    pe.wait_ge(s_kev, n - 2)
                lo, hi = (0, KPIECE // 2) if part == 0 else (KPIECE // 2, KPIECE)
                ins = nc.tensor.matmul(ps[1 + n % 3][:, lo:hi], Wk_sb[:, :],
                                       ctxT[:, n * KPIECE + lo:n * KPIECE + hi], start=True, stop=True)
                if part == 1:
                    ins.then_inc(s_kp, 1)

            pe.wait_ge(s_dtc, NTB)
            for n in range(EARLY):
                keys_of(n, 0)
                keys_of(n, 1)
            for j in range(NJ - 1, 0, -1):
                pe.wait_ge(s_hit, NJ - j)
                nc.tensor.matmul(ps[4][:, j:j + 1], blk[:, :], acc[:, j:j + 1], start=True, stop=True
                                 ).then_inc(s_hop, 1)
                i = NJ - 1 - j
                if i < 2 * (NKP - EARLY):
                    keys_of(EARLY + i // 2, i % 2)
            pe.wait_ge(s_z, 1)
            nc.tensor.matmul(ps[5][0:C, 0:NB * (NJ + 1)], ones[:, 0:C],
                             zt[:, :, :].rearrange("p b j -> p (b j)"), start=True, stop=True).then_inc(s_eb, 1)
            pe.wait_ge(s_keys, 16 * 5)
            pe.wait_ge(s_kev, NKP)
            for c in range(8):
                nc.tensor.transpose(ps[1 + c // 4][:, (c % 4) * P:(c % 4 + 1) * P], wq_sb[:, c * P:(c + 1) * P],
                                    ident[:, :])
            for c in range(8):
                last = nc.tensor.transpose(ps[7][:, c * 2 * NK:(c + 1) * 2 * NK], keyn[:, c, :],
                                           ident[0:2 * NK, 0:2 * NK])
            last.then_inc(s_foldT, 1)
            for g in range(NB // 2):
                pe.wait_ge(s_pm, NS * (g + 1))
                for par in range(2):
                    b = 2 * g + par
                    pe.wait_ge(s_nat2[b], 16)
                    for s in range(NS):
                        rows = nat[:, b, s, :] if b < RING else \
                            dist[:, ((b - RING) * NS + s) * D:((b - RING) * NS + s + 1) * D]
                        last = nc.tensor.matmul(ps[6 + g // 2][64 * par:64 * par + NJ, g % 2 * D:(g % 2 + 1) * D],
                                                Pm[:, g % 2, s, par * NJ:(par + 1) * NJ], rows,
                                                start=(s == 0), stop=(s == NS - 1))
                last.then_inc(s_ex, 1)
                if g == 1:
                    pe.wait_ge(s_foldc, 1)
                    for c in range(8):
                        last = nc.tensor.matmul(ps[1][:, c * 2 * NK:(c + 1) * 2 * NK], wqT[:, c * P:(c + 1) * P],
                                                keyT[:, c * 2 * NK:(c + 1) * 2 * NK], start=True, stop=True)
                    last.then_inc(s_fold, 1)
            pe.wait_ge(s_u, 4)
            for t in range(4):
                last = nc.tensor.transpose(ps[3][:, t * P:(t + 1) * P], U[:, t, :], ident[:, :])
            last.then_inc(s_uT, 1)
            pe.wait_ge(s_xr, 1)
            if stage >= 2:
                layernorm_sums(1)
                pe.wait_ge(s_xn, 2)
                for t in range(4):
                    last = nc.tensor.transpose(ps[4][0:TT, t * D:(t + 1) * D], xnT[:, t * TT:(t + 1) * TT],
                                               ident[:, :])
                last.then_inc(s_xnk, 1)
                pe.wait_ge(s_fold_sb, 1)
                for t in range(4):
                    nc.tensor.matmul(ps[t][0:TT, :], xnT[:, t * TT:(t + 1) * TT], fold[:, :],
                                     start=True, stop=True).then_inc(s_sim, 1)
                if stage >= 3:
                    pe.wait_ge(s_w, 16 * 22)
                    pe.wait_ge(s_xnc, 1)
                    for b in range(NB):
                        for i in range(NCH // 4):
                            n = b * (NCH // 4) + i
                            if n >= 2:
                                pe.wait_ge(s_vc, n - 1)
                            for k in range(4):
                                c = 4 * i + k
                                rows = min(P, NI - c * P)
                                last = nc.tensor.matmul(ps[4 + n % 2][0:rows, k * D:(k + 1) * D],
                                                        ctxT[:, b * NI + c * P:b * NI + c * P + rows], Wv_sb,
                                                        start=True, stop=True)
                            last.then_inc(s_vp, 1)
                pe.wait_ge(s_otok, 4)
                for t in range(4):
                    last = nc.tensor.transpose(ps[0][:, t * TT:(t + 1) * TT], x_tok[:, t, :], ident[0:TT, 0:TT])
                last.then_inc(s_oT, 1)
            if stage >= 3:
                pe.wait_ge(s_xr, 2)
                layernorm_sums(2)
                pe.wait_ge(s_xn, 3)
                nc.tensor.matmul(ps[1][:, 0:TOK], Wq_sb, xnT[:, :], start=True, stop=True).then_inc(s_q, 1)
                pe.wait_ge(s_qp, 16 * len(PRODUCTS))
                pe.wait_ge(s_one, 1)
                pe.wait_ge(s_tabs, 13)

                def row_scores(b, u):
                    k = b * UNITS + u
                    if u == 0:
                        pe.wait_ge(s_kpl[b % 3], 16 * len(PRODUCTS) * (b // 3 + 1))
                        if b == 2:
                            pe.wait_ge(s_one, 2)
                    ring = 6 if b == 0 else 2
                    if k >= ring:
                        pe.wait_ge(s_mx, k - ring + 1)
                    nc.tensor.matmul(ps[k % ring][0:2 * NJ, 0:PIECE],
                                     QP[:, u // NPIECE, b, :],
                                     KP[b % 3][:, u // NPIECE, (u % NPIECE) * PIECE:(u % NPIECE + 1) * PIECE],
                                     start=True, stop=True).then_inc(s_s1, 1)

                def maxima_to_rows(b):
                    pe.wait_ge(s_np, b + 1)
                    if b >= 2:
                        pe.wait_ge(s_ob, b - 1)
                    for pair in range(NH // 2):
                        last = nc.tensor.transpose(maxrows[b % 2][:, pair, :], npart[:, pair, :],
                                                   identb[0:2 * NJ, 0:2 * NJ])
                    last.then_inc(s_nmt, 1)

                def weigh_values(g):
                    b, c = g // NCH, g % NCH
                    rows = min(P, NI - c * P)
                    pe.wait_ge(s_exp, g + 1)
                    if c == 0 and b >= 2:
                        pe.wait_ge(s_ob, b - 1)
                    for t in range(VT):
                        q, o = 32 * (t % 4), (t // 4) * 2 * NJ
                        v0 = (g * VT + t) * VTW
                        last = nc.tensor.matmul(ps[6 + b % 2][q:q + 32, o:o + 2 * NJ], vals[0:rows, v0:v0 + 32],
                                                Pt[0:rows, g % 2, 2 * t * NJ:2 * (t + 1) * NJ],
                                                start=(c == 0 and t < 4), stop=(c == NCH - 1),
                                                skip_group_check=True)
                    last.then_inc(s_pv, 1)

                for u in range(UNITS):
                    row_scores(0, u)
                maxima_to_rows(0)
                for b in range(NB):
                    pe.wait_ge(s_nmc, b + 1)
                    for c in range(NCH):
                        g = b * NCH + c
                        rows = min(P, NI - c * P)
                        if g >= 2:
                            pe.wait_ge(s_exp, g - 1)
                        ahead = UNITS + sum(BESIDE[:g])
                        units = [divmod(k, UNITS) for k in range(ahead, min(ahead + BESIDE[g], NB * UNITS))]
                        for m in range(NH // 2):
                            if m % 4 == 0 and len(units) > 1:
                                row_scores(*units.pop(0))
                            bank = ps[2 + 2 * (g % 2) + m // (NH // 4)]
                            o = m % (NH // 4) * 2 * NJ
                            last = nc.tensor.matmul(bank[0:rows, o:o + 2 * NJ],
                                                    KP[b % 3][:, m, c * P:c * P + rows],
                                                    QP[:, m, b, :], start=True, stop=True)
                        last.then_inc(s_s2, 1)
                        if g >= 1:
                            weigh_values(g - 1)
                        for unit in units:
                            row_scores(*unit)
                        if c == 3 and b >= 1:
                            pe.wait_ge(s_oc, b)
                            nc.tensor.matmul(ps[6 + (b - 1) % 2][:, 256:256 + 4 * NJ], sel, Osb.rearrange("p a m q -> p (a m q)"), start=True, stop=True
                                             ).then_inc(s_den, 1)
                        if c == MAXROW_AT and b + 1 < NB:
                            maxima_to_rows(b + 1)
                weigh_values(NB * NCH - 1)
                pe.wait_ge(s_oc, NB)
                nc.tensor.matmul(ps[6 + (NB - 1) % 2][:, 256:256 + 4 * NJ], sel, Osb.rearrange("p a m q -> p (a m q)"), start=True, stop=True).then_inc(s_den, 1)
                pe.wait_ge(s_ob, NB)
                for half in range(2):
                    last = nc.tensor.matmul(ps[0][:, 0:TOK], WoAB[:, half, :], OAB[:, half, :],
                                            start=(half == 0), stop=(half == 1))
                last.then_inc(s_wo, 1)
            if stage >= 4:
                pe.wait_ge(s_xr, 3)
                layernorm_sums(3)
                pe.wait_ge(s_xn, 4)
                for t in range(4):
                    last = nc.tensor.matmul(ps[1][0:TT, t * NE:(t + 1) * NE], xnT[:, t * TT:(t + 1) * TT],
                                            Wr[:, :], start=True, stop=True)
                last.then_inc(s_lg, 1)
                pe.wait_ge(s_w12, 32)
                def hidden(i):
                    e, c = i // FC, i % FC
                    if i >= 2:
                        pe.wait_ge(s_hc, i - 1)
                    nc.tensor.matmul(ps[5 + i % 2][:, 0:TOK], W1s[:, e, c * P:(c + 1) * P], xnT[:, :],
                                     start=True, stop=True).then_inc(s_h, 1)

                def output(i):
                    e, c = i // FC, i % FC
                    pe.wait_ge(s_hc, i + 1)
                    if c == 0 and e >= 2:
                        pe.wait_ge(s_yc, e - 1)
                    nc.tensor.matmul(ps[7 if e % 2 else 0][:, 0:TOK], W2s[:, i, :], hT[:, i % 4, :],
                                         start=(c == 0), stop=(c == FC - 1)).then_inc(s_yu, 1)

                hidden(0)
                hidden(1)
                for i in range(NE * FC):
                    if i == FC - 2:
                        pe.wait_ge(s_rw, 1)
                        for t in range(4):
                            last = nc.tensor.transpose(ps[2][0:NE, t * TT:(t + 1) * TT],
                                                       lg[:, 4, t * NE:(t + 1) * NE], ident[0:TT, 0:TT])
                        last.then_inc(s_wtT, 1)
                    if i % FC == FC - 1:
                        e = i // FC
                        if e == 0:
                            pe.wait_ge(s_wtc, 1)
                            pe.wait_ge(s_et, 3)
                        if e >= 2:
                            pe.wait_ge(s_wbc, e - 1)
                        nc.tensor.matmul(ps[3 + e % 2][:, 0:TOK], sele[:, e, :], wT, start=True, stop=True
                                         ).then_inc(s_wb, 1)
                    if i + 2 < NE * FC:
                        hidden(i + 2)
                    output(i)
            pe.wait_ge(s_xr, min(stage, 4))
            for t in range(4):
                last = nc.tensor.transpose(ps[1][0:TT, t * D:(t + 1) * D], xT[:, t * TT:(t + 1) * TT],
                                           ident[:, :])
            last.then_inc(s_fT, 1)


_INS = ["x", "ctx_1024", "g_xattn", "g_ffn", "L0_ffn_w_q", "L0_ffn_keys", "w_tab",
        "L1_xattn_Wq", "L1_xattn_bq", "L1_xattn_Wk", "L1_xattn_bk", "L1_xattn_Wv", "L1_xattn_bv",
        "L1_xattn_Wo", "L1_xattn_bo", "L1_ffn_W_router", "L1_ffn_b_router", "L1_ffn_W1", "L1_ffn_b1",
        "L1_ffn_W2", "L1_ffn_b2"]


def kernel(**inputs):
    import numpy as np
    from concourse import bacc
    from concourse.bass_utils import run_bass_kernel_spmd

    nc = bacc.Bacc("TRN2", target_bir_lowering=False, num_devices=1)
    laid = dict(inputs)
    laid["w_tab"] = np.concatenate([np.asarray(inputs["L0_ffn_w_down"]), np.asarray(inputs["L0_ffn_w_up"])], axis=1)
    arrays, args = {}, []
    for name in _INS:
        a = np.ascontiguousarray(laid[name])
        arrays[f"in_{name}"] = a
        args.append(nc.dram_tensor(f"in_{name}", a.shape, mybir.dt.from_np(a.dtype), kind="ExternalInput").ap())
    shape = np.asarray(inputs["x"]).shape
    args.append(nc.dram_tensor("out_x", shape, mybir.dt.float32, kind="ExternalOutput").ap())
    build_gated_layers(nc, *args)
    r = run_bass_kernel_spmd(nc, [arrays], core_ids=[0])
    return r.results[0]["out_x"]
```

```python
from contextlib import ExitStack

import concourse.bass as bass
from concourse import mybir

ALU = mybir.AluOpType
ACT = mybir.ActivationFunctionType
AX_X = mybir.AxisListType.X
F32 = mybir.dt.float32
BF16 = mybir.dt.bfloat16
F16 = mybir.dt.float16
I32 = mybir.dt.int32
U32 = mybir.dt.uint32

P = 128
BIG = 1.0e20
EPS = 1.0e-5


def view(ap, dims, offset=0):
    return bass.AP(tensor=ap.tensor, offset=ap.offset + offset, ap=[list(ap.ap[0])] + dims)


def build_gated_layers(nc, x, ctx_in, g_xattn, g_ffn, w_q, keys, w_tab, Wq, bq, Wk, bk, Wv, bv, Wo, bo,
                       W_router, b_router, W1, b1, W2, b2, out):
    NB, NJ, D = x.shape
    NI = ctx_in.shape[1]
    TOK = NB * NJ
    LB = P // NB
    C = 100
    NS = NI // C
    assert NS * C == NI and NS < LB and D == P
    BS = LB * (NJ + NS - 2)
    assert NI <= 2048
    OFF = float(NI)
    STEPS = NJ + NS - 1
    PADJ = NS - 1
    JW = NJ + PADJ
    SLOT = C + 1
    PIECE = 500
    NPIECE = NI // PIECE
    SPP = PIECE // C
    TB = 5
    NTB = STEPS // TB
    assert NTB * TB == STEPS
    RING = 4
    AHEAD = 3
    DT_STEPS = PIECE // C
    JQ = NS * D + 3 * NS * NJ
    NHK, NK = keys.shape[0], keys.shape[1]
    FOLD = w_q.shape[1]
    NH = 16
    DH = D // NH
    HQ = NH * NJ
    NCH = -(-NI // P)
    VT, VTW = NH // 2, 2 * DH + 1
    VW = VT * VTW
    UNITS = NH // 2 * NPIECE
    PRODUCTS = ((0, 0), (0, 1), (0, 2), (1, 0), (1, 1), (2, 0))
    NPR = len(PRODUCTS) * 2 * DH
    KPIECE = 375
    KPB = NI // KPIECE
    NKP = NB * KPB
    KBANKS = (0, 1, 2, 3, 5, 6, 7)
    THIRD = KPIECE // 3
    EARLY = 14
    assert KPIECE * KPB == NI and 3 * (NKP - EARLY) <= NJ - 1 and KPIECE % 3 == 0
    BESIDE = [3] * 8 + [2] * (NCH * NB)
    assert 3 * 8 == UNITS and 2 * NCH == UNITS
    MAXROW_AT = 10
    NE, F = W1.shape[0], W1.shape[2]
    FC = F // P
    TT = TOK // 4
    CUT = 3 * TT
    LN_COLS = ((0, TOK),) + 3 * ((0, CUT), (CUT, TOK))
    LN_BANK = (0, 0, 7, 0, 3, 0, 3)
    TILES = (range(3), range(3, 4))
    assert CUT % NJ == 0

    with ExitStack() as ctx:
        def sb(name, shape, dt=F32):
            return ctx.enter_context(nc.sbuf_tensor(name, shape, dt))

        def sem(name):
            return ctx.enter_context(nc.semaphore(name))

        banks = ctx.enter_context(nc.psum_tensor("banks", [P, 8, 512], F32))
        ps = [banks[:, i, :] for i in range(8)]

        ctxT = sb("ctxT", [P, NB * NI])
        N_DIST, N_NAT, N_JUMP, N_R = NB * BS + P, RING * NS * D, NJ * C, (STEPS + 1) * SLOT
        arena = sb("arena", [P, N_DIST + N_NAT + N_JUMP + N_R])
        o_nat, o_jump, o_R = N_DIST, N_DIST + N_NAT, N_DIST + N_NAT + N_JUMP
        dist = arena[0:C, 0:N_DIST]
        nat = arena[0:C, o_nat:o_jump].rearrange("c (r s d) -> c r s d", r=RING, s=NS)
        jump = arena[:, o_jump:o_R]
        jslot = arena[:, o_jump:o_jump + STEPS * C // 2].bitcast(F16)
        o_jcol = o_jump + STEPS * C // 2
        jcol = arena[:, o_jcol:o_jcol + NJ * C // 2].bitcast(F16)
        R = arena[:, o_R:]
        N_B = TB * C
        work = sb("work", [P, 10 * N_B + TB * SLOT])
        mring = work[:, 0:2 * N_B]
        dts = work[:, 2 * N_B:4 * N_B]
        wk = [[work[:, (4 + 3 * a + i) * N_B:(5 + 3 * a + i) * N_B] for i in range(3)] for a in range(2)]
        gate = work[:, 10 * N_B:]
        taken = 0

        def later(rows, n, dt=F32):
            nonlocal taken
            words = n if dt == F32 else -(-n // 2)
            ap = work[0:rows, taken:taken + words]
            taken += words
            assert taken <= 10 * N_B + TB * SLOT
            return ap if dt == F32 else ap.bitcast(dt)

        twice1 = sb("twice1", [P, C])
        sq = jump[0:C, 0:NS * D]
        absum = jump[0:C, NS * D:NS * D + 2 * NS * NJ].rearrange("c (a n) -> c a n", a=2)
        dtmp = jump[0:C, NS * D + 2 * NS * NJ:NS * D + 3 * NS * NJ]
        aa = sb("aa", [C, NB, NS])
        bbB = jump[0:C, JQ:JQ + TOK]

        ident = sb("ident", [P, P])
        Wk_sb = sb("Wk_sb", [P, D])
        o_kf = (NB - RING) * NS * D
        assert o_kf + 3 * KPIECE <= N_DIST and 6 * KPIECE <= 5 * N_B
        kf = arena[:, o_kf:o_kf + 3 * KPIECE].rearrange("p (r i) -> p r i", r=3)
        kq = work[:, 2 * N_B:2 * N_B + 6 * KPIECE].bitcast(BF16).rearrange("p (r x i) -> p r x i", r=4, x=3)
        key_parts = nc.dram_tensor("key_parts", (NB, 3, P, NI), BF16, kind="Internal").ap()
        query_parts = nc.dram_tensor("query_parts", (3, P, 2 * TOK), BF16, kind="Internal").ap()
        meanw = sb("meanw", [P, P])
        ones = sb("ones", [P, P])
        blk = sb("blk", [P, P])
        first = sb("first", [P, NB])
        pidx = sb("pidx", [P, 1], I32)
        lane_i = sb("lane_i", [P, 1], I32)
        lane = sb("lane", [P, 1])
        lmask = sb("lmask", [P, 4])
        twice = sb("twice", [P, C * 2])
        rowc2 = sb("rowc2", [C, NS])
        rowc21 = sb("rowc21", [C, NS])
        acc = sb("acc", [P, NJ], F16)
        blk16 = sb("blk16", [P, P], F16)
        e_last = sb("e_last", [P, 1])
        hops = sb("hops", [P, 2, STEPS + 1])
        shf = sb("shf", [P, STEPS + 1])
        zt = mring[:, 0:NB * (NJ + 1)].rearrange("p (b j) -> p b j", b=NB)
        EB = work[0:C, 7 * N_B:7 * N_B + NB * (NJ + 1)].rearrange("c (b j) -> c b j", b=NB)
        Pm = R[0:C, 0:2 * NS * 2 * NJ].rearrange("c (r s n) -> c r s n", r=2, s=NS)
        U = work[:, 8 * N_B:8 * N_B + NB // 2 * D].rearrange("p (t d) -> p t d", d=D)
        o_am = 8 * N_B + NB // 2 * D
        A_RING = 6
        Am = work[0:C, o_am:o_am + A_RING * 2 * NJ].rearrange("c (a n) -> c a n", a=A_RING)
        g4 = sb("g4", [P, 4])
        gt = sb("gt", [P, 4])
        x_tok = sb("x_tok", [TT, 4, D])
        xT = sb("xT", [P, TOK])
        xc = sb("xc", [P, TOK])
        xsq = sb("xsq", [P, TOK])
        rstd = sb("rstd", [P, TOK])
        xnT = sb("xnT", [P, TOK])
        xm2 = jump[:, JQ + TOK:JQ + 2 * TOK]
        epsc = sb("epsc", [P, 1])
        pad0 = sb("pad0", [P, 1])

        SUM_BANK = (6, 7, 5, 4)
        o_fold = N_R - 3 * FOLD
        wq_sb = R[:, o_fold:o_fold + FOLD]
        keyn = R[0:2 * NK, o_fold + FOLD:o_fold + 2 * FOLD].rearrange("k (c f) -> k c f", f=P)
        wqT = R[:, o_fold + 2 * FOLD:o_fold + 3 * FOLD]
        keyT = sb("keyT", [P, FOLD // 2])
        fold = sb("fold", [P, FOLD // 2])
        kiota = later(TT, 2 * NHK * NK)
        mxs = sb("mxs", [TT, 4, 2 * NHK])
        ixs = sb("ixs", [TT, 4, 2 * NHK])
        score = sb("score", [TT, 4, NHK])
        idxf = sb("idxf", [TT, 4, NHK])
        idx = sb("idx", [TT, 4 * NHK], U32)
        hcol = sb("hcol", [TT, 4, NHK])
        gath = arena[0:TT, 0:4 * NHK * 2 * D].rearrange("p (t h d) -> p t h d", t=4, h=NHK)
        prod = later(P, NHK * D)
        vals = arena[:, o_nat:o_nat + NCH * NB * VW + 32]
        o_att = o_nat + NCH * NB * VW + 32
        Pt = arena[:, o_att:o_att + 2 * HQ].rearrange("p (r n) -> p r n", r=2)
        KPW = NH // 2 * NI // 2
        kp_words = [ctxT[:, 0:KPW], ctxT[:, KPW:2 * KPW], arena[:, 0:KPW]]
        KP = [w.bitcast(BF16).rearrange("p (m i) -> p m i", m=NH // 2) for w in kp_words]
        assert KPW <= N_DIST
        QP = arena[:, o_att + 2 * HQ:o_att + 6 * HQ].bitcast(BF16).rearrange(
            "p (m b n) -> p m b n", m=NH // 2, b=NB)
        Qm = Pt.rearrange("p r n -> p (r n)")[:, 0:2 * TOK]
        Wq_sb, Wv_sb = later(P, D), later(P, D)
        WoAB = later(P, 2 * D).rearrange("p (a d) -> p a d", a=2)
        bvAB = sb("bvAB", [P, 2])
        cols = sb("cols", [P, 3])
        hm = sb("hm", [P, 2])
        QS = later(P, 3 * 2 * TOK, BF16).rearrange("p (x n) -> p x n", x=3)
        mx3 = sb("mx3", [2 * NJ, 2, NH // 2, NPIECE])
        nmx = sb("nmx", [2 * NJ, NH // 2])
        npart = sb("npart", [2 * NJ, NH // 2, 3], BF16)
        identb = later(P, P, BF16)
        Osb = arena[:, o_att + 6 * HQ:o_att + 6 * HQ + 4 * NJ].rearrange("p (a m q) -> p a m q", a=2, m=2)
        both = arena[:, o_att + 6 * HQ:o_att + 6 * HQ + 8 * NJ]
        assert o_att + 6 * HQ + 8 * NJ <= N_DIST + N_NAT + N_JUMP + N_R
        masked = later(P, 8 * NJ)
        num = masked[:, 0:4 * NJ].rearrange("p (i a q) -> p i a q", i=2, a=2)
        OAB = QS.rearrange("p x n -> p (x n)").bitcast(F32)[:, 0:2 * TOK].rearrange("p (a n) -> p a n", a=2)
        nd = later(P, 4 * NJ).rearrange("p (a n) -> p a n", a=2)
        mk = sb("mk", [P, 2])
        mku = sb("mku", [P, 1])
        sel = later(P, P)
        mk2 = sb("mk2", [P, 1])
        l32 = sb("l32", [P, 1])
        maxrows = [ps[6 + r].bitcast(BF16)[NPR:NPR + 3, 0:HQ].rearrange("p (m n) -> p m n", m=NH // 2)
                   for r in range(2)]
        W1s = arena[:, 0:NE * F].rearrange("p (e f) -> p e f", e=NE)
        W2s = arena[:, NE * F:2 * NE * F].rearrange("p (u d) -> p u d", d=D)
        assert 2 * NE * F <= N_DIST
        Wr = sb("Wr", [P, NE])
        brB = sb("brB", [TT, NE])
        b1s = sb("b1s", [P, NE * F // P])
        b2s = sb("b2s", [P, NE])
        eiota = sb("eiota", [TT, 4, NE])
        lg = later(TT, 6 * 4 * NE).rearrange("p (i n) -> p i n", i=6)
        rs = sb("rs", [TT, 8, 4])
        wparts = sb("wparts", [TT, 4, 3 * NE], BF16)
        wT = later(3 * NE, TOK, BF16)
        sele = prod[0:3 * NE, :].bitcast(BF16)[:, 0:NE * P].rearrange("p (e n) -> p e n", n=P)
        hT = arena[:, o_nat:o_nat + 4 * TOK].rearrange("p (r n) -> p r n", r=4)
        wBs = arena[:, o_nat + 4 * TOK:o_nat + 6 * TOK].rearrange("p (r n) -> p r n", r=2)

        s_x = sem("x_loaded")
        s_small = sem("small_loaded")
        s_nat = [sem(f"nat_loaded{r}") for r in range(NB)]
        s_nat2 = [sem(f"nat_again{b}") for b in range(NB)]
        s_pool = sem("pool_done")
        s_const = sem("constants_done")
        s_blk = sem("lanes_of_a_batch_in_float16")
        s_dve = sem("dve_done")
        s_act = sem("act_done")
        s_xT = sem("xT_transposed")
        s_xTe = sem("xT_copied")
        s_mean = sem("mean_ready")
        s_cen = sem("centred_squares_ready")
        s_var = sem("variance_ready")
        s_std = sem("deviation_ready")
        s_xn = sem("normalized_ready")
        s_xm = sem("queries_scaled")
        s_bb = sem("query_norms_ready")
        s_bbe = sem("query_norms_copied")
        s_ct = sem("context_transposed")
        s_ctA = sem("context_copied_by_act")
        s_ctV = sem("context_copied_by_dve")
        s_sq = sem("context_squared")
        s_aa = sem("context_norms_ready")
        s_ab = sem("norm_sums_ready")
        s_dot = sem("dots_ready")
        s_d2 = sem("squared_distances_ready")
        s_dist = sem("distances_ready")
        s_dt = sem("distances_by_lane")
        s_dtc = sem("distances_by_lane_copied")
        s_scan = sem("column_scanned")
        s_jin = sem("jump_inputs_ready")
        s_sgn = sem("left_below_diagonal_ready")
        s_where = sem("where_to_ready")
        s_jump = sem("jumps_ready")
        s_leave = sem("leaving_rows_ready")
        s_carry = sem("carries_ready")
        s_j16 = sem("jumps_in_float16")
        s_desk = sem("jumps_deskewed")
        s_hit = sem("hit_ready")
        s_hop = sem("hop_ready")
        s_z = sem("hops_placed")
        s_eb = sem("hops_spread")
        s_ebc = sem("hops_spread_copied")
        s_ex = sem("rows_summed")
        s_u = sem("sums_copied")
        s_uT = sem("sums_transposed")
        s_gate = sem("gates_ready")
        s_natfree = sem("nat_used")
        s_out = sem("out_stored")

        s_tabs = sem("attention_tables_step")
        s_lane32 = sem("row_of_quarter_ready")
        s_et = sem("expert_tables_step")
        s_wk = sem("key_weights_loaded")
        s_kr = sem("first_key_part_taken")
        s_k2 = sem("second_key_part_ready")
        s_ks = sem("keys_split")
        s_kd = [sem(f"key_parts_stored{r}") for r in range(4)]
        s_kpl = [sem(f"key_parts_loaded{r}") for r in range(3)]
        s_am = sem("path_starts_ready")
        s_pm = sem("path_masks_ready")
        s_qs = sem("queries_split")
        s_qd = [sem(f"query_part_stored{x}") for x in range(3)]
        s_qp = sem("query_parts_laid")
        s_one = sem("ones_rows_ready")
        s_keyz = sem("key_tiles_zeroed")
        s_keys = sem("keys_loaded")
        s_foldT = sem("fold_inputs_transposed")
        s_foldc = sem("fold_inputs_copied")
        s_fold = sem("keys_folded")
        s_fold_sb = sem("folded_keys_copied")
        s_xr = sem("hidden_state_updated")
        s_xnk = sem("tokens_transposed")
        s_xnc = sem("tokens_copied")
        s_sim = sem("similarities_ready")
        s_picked = sem("similarities_used")
        s_idx = sem("experts_chosen")
        s_gath = [sem(f"rows_gathered{t}") for t in range(4)]
        s_hcol = sem("expert_dots_ready")
        s_gelu = sem("expert_gelu_ready")
        s_otok = sem("memory_output_ready")
        s_oT = sem("memory_output_transposed")
        s_wz = sem("weight_tiles_zeroed")
        s_w = sem("attention_weights_loaded")
        s_w12 = sem("expert_weights_loaded")
        s_tab = sem("attention_tables_ready")
        s_vp = sem("values_projected")
        s_vc = sem("values_copied")
        s_kp = sem("keys_projected")
        s_kev = sem("keys_evacuated")
        s_q = sem("queries_projected")
        s_s1 = sem("row_scores_ready")
        s_mx = sem("row_scores_reduced")
        s_np = sem("negative_maxima_split")
        s_nmt = sem("negative_maxima_in_rows")
        s_nmc = sem("negative_maxima_copied")
        s_s2 = sem("column_scores_ready")
        s_exp = sem("probabilities_ready")
        s_pv = sem("values_weighted")
        s_oc = sem("head_sums_copied")
        s_den = sem("denominators_spread")
        s_dnc = sem("denominators_copied")
        s_nst = sem("normalizing_step")
        s_ndm = sem("denominators_masked")
        s_rcp = sem("denominators_inverted")
        s_ob = sem("heads_normalized")
        s_wo = sem("attention_output_ready")
        s_lg = sem("router_logits_ready")
        s_lgd = sem("logit_gap_ready")
        s_lge = sem("logit_gap_exponential")
        s_rw = sem("router_weights_ready")
        s_wtT = sem("router_weights_transposed")
        s_wtc = sem("router_weights_copied")
        s_wb = sem("router_weights_spread")
        s_wbc = sem("router_weights_spread_copied")
        s_h = sem("hidden_ready")
        s_hc = sem("hidden_copied")
        s_yu = sem("hidden_used")
        s_yc = sem("expert_output_added")
        s_fT = sem("output_transposed")
        s_fc = sem("output_copied")

        R_slot = lambda k, n, lo, cnt: view(R[:, :], [[SLOT, n], [1, cnt]], k * SLOT + lo)
        block = ctx.enter_context(nc.Block())

        @block.sync
        def _(sp):
            sp.dma_start(x_tok[:, :, :], x.rearrange("b j d -> (b j) d").rearrange("(t p) d -> p t d", t=4)
                         ).then_inc(s_x, 16)
            for b in range(NB):
                if b >= RING:
                    sp.wait_ge(s_ct, NPIECE * (b - RING + 1))
                    sp.wait_ge(s_sq, b - RING + 1)
                sp.dma_start(nat[:, b % RING, :, :], ctx_in[b].rearrange("(s c) d -> c s d", c=C)
                             ).then_inc(s_nat[b], 16)
            sp.dma_start(Wk_sb[:, :], Wk[:, :]).then_inc(s_wk, 16)
            for i, src in enumerate((bq, bk, bo)):
                sp.dma_start(cols[:, i:i + 1], src.rearrange("(d a) -> d a", a=1)).then_inc(s_wk, 16)
            for b in range(RING):
                sp.wait_ge(s_ct, NPIECE * (b + RING + 1))
                sp.wait_ge(s_sq, b + RING + 1)
                sp.dma_start(nat[:, b, :, :], ctx_in[b].rearrange("(s c) d -> c s d", c=C)
                             ).then_inc(s_nat2[b], 16)
            sp.wait_ge(s_dt, NTB * TB // DT_STEPS)
            for b in range(RING, NB):
                o = (b - RING) * NS * D
                sp.dma_start(dist[:, o:o + NS * D].rearrange("c (s d) -> c s d", d=D),
                             ctx_in[b].rearrange("(s c) d -> c s d", c=C)).then_inc(s_nat2[b], 16)
            sp.wait_ge(s_j16, NTB)
            for s in range(LB):
                lanes, slot = slice(s, P - LB + s + 1, LB), min(s, NS - 1)
                sp.dma_start(jcol[lanes, :], jslot[lanes, slot * C:(slot + NJ) * C]).then_inc(s_desk, 16)
            sp.wait_ge(s_keyz, 1)
            sp.dma_start(wq_sb[:, :], w_q[:, :]).then_inc(s_keys, 16)
            kv = keys.rearrange("(m a) k p f -> a p k m f", a=2)
            for a in range(2):
                for p in range(2):
                    sp.dma_start(keyn[NK * a:NK * (a + 1), 4 * p:4 * p + 4, 64 * a:64 * a + 64], kv[a, p]
                                 ).then_inc(s_keys, 16)
            sp.wait_ge(s_wz, 1)
            for dst, src in ((Wq_sb, Wq), (Wv_sb, Wv)):
                sp.dma_start(dst, src[:, :]).then_inc(s_w, 16)
            r = G = 2 * DH
            for g in range(VT):
                q, half = 32 * (g % 4), g // 4
                sp.dma_start(WoAB[q:q + r, half, :], Wo[G * g:G * g + r, :]).then_inc(s_w, 16)
                sp.dma_start(bvAB[q:q + r, half:half + 1], bv[G * g:G * g + r].rearrange("(d a) -> d a", a=1)
                             ).then_inc(s_w, 16)
            sp.dma_start(Wr[:, :], W_router[:, :]).then_inc(s_w, 16)
            sp.dma_start(brB[:, :], bass.AP(tensor=b_router.tensor, offset=0, ap=[[0, TT], [1, NE]])
                         ).then_inc(s_w, 16)
            sp.dma_start(b2s[:, :], b2.rearrange("e d -> d e"), allow_slow_non_contiguous=True).then_inc(s_w, 16)
            sp.dma_start(b1s[:, :], b1.rearrange("e (c p) -> p (e c)", p=P), allow_slow_non_contiguous=True
                         ).then_inc(s_w, 16)
            def load_key_parts(b):
                for c, (kx, _) in enumerate(PRODUCTS):
                    sp.dma_start(KP[b % 3][2 * DH * c:2 * DH * (c + 1), :, :],
                                 key_parts[b, kx].rearrange("(m r) i -> r m i", r=2 * DH)
                                 ).then_inc(s_kpl[b % 3], 16)

            for r in range(4):
                sp.wait_ge(s_kd[r], 16 * NKP // 4)
            sp.wait_ge(s_vc, NCH // 4 * NB)
            for t in range(4):
                sp.wait_ge(s_gath[t], 16 * NHK)
            for b in range(2):
                load_key_parts(b)
            for part in range(3):
                sp.wait_ge(s_qs, part + 1)
                sp.dma_start(query_parts[part], QS[:, part, :]).then_inc(s_qd[part], 16)
            for c, (_, qx) in sorted(enumerate(PRODUCTS), key=lambda product: product[1][1]):
                sp.wait_ge(s_qd[qx], 16)
                sp.dma_start(QP[2 * DH * c:2 * DH * (c + 1), :, :, :].rearrange("r m b n -> r m (b n)"),
                             query_parts[qx].rearrange("(m r) n -> r m n", r=2 * DH)).then_inc(s_qp, 16)
            sp.wait_ge(s_otok, 4)
            load_key_parts(2)
            for b in range(3, NB):
                sp.wait_ge(s_s2, NCH * (b - 2))
                load_key_parts(b)
            sp.wait_ge(s_s2, NCH * (NB - NB % 3))
            sp.dma_start(W1s, W1.rearrange("e d f -> d e f")).then_inc(s_w12, 16)
            sp.dma_start(W2s, W2.rearrange("e (c p) d -> p (e c) d", p=P)).then_inc(s_w12, 16)
            sp.wait_ge(s_fc, 1)
            sp.dma_start(out.rearrange("b j d -> (b j) d").rearrange("(t p) d -> p t d", t=4),
                         x_tok[:, :, :]).then_inc(s_out, 16)
            sp.wait_ge(s_out, 16)

        @block.gpsimd
        def _(pool):
            n = 0

            def done(ins):
                nonlocal n
                n += 1
                ins.then_inc(s_pool, 1)

            done(nc.gpsimd.memset(ident[:, :], 0.0))
            done(nc.gpsimd.iota(pidx[:, :], [[1, 1]], base=0, channel_multiplier=1))
            done(nc.gpsimd.memset(first[:, :], 0.0))
            done(nc.gpsimd.memset(blk[:, :], 1.0))
            done(nc.gpsimd.iota(twice[:, :], [[1, 2 * C]], base=0, channel_multiplier=0,
                                allow_small_or_imprecise_dtypes=True))
            done(nc.gpsimd.iota(rowc2[:, :], [[2 * C, NS]], base=0, channel_multiplier=2,
                                allow_small_or_imprecise_dtypes=True))
            pool.wait_ge(s_pool, n)
            done(nc.gpsimd.affine_select(out=ident[:, :], in_=ident[:, :], compare_op=ALU.not_equal, fill=1.0,
                                         base=0, pattern=[[-1, P]], channel_multiplier=1))
            done(nc.gpsimd.affine_select(out=first[:, :], in_=first[:, :], compare_op=ALU.not_equal, fill=1.0,
                                         base=0, pattern=[[-LB, NB]], channel_multiplier=1))
            bv_ = blk[:, :].rearrange("p (b s) -> p b s", s=LB)
            done(nc.gpsimd.affine_select(out=bv_, in_=bv_, compare_op=ALU.is_ge, fill=0.0,
                                         base=0, pattern=[[-LB, NB], [0, LB]], channel_multiplier=1))
            pool.wait_ge(s_pool, n)
            nc.gpsimd.affine_select(out=bv_, in_=bv_, compare_op=ALU.is_ge, fill=0.0,
                                    base=LB - 1, pattern=[[LB, NB], [0, LB]], channel_multiplier=-1
                                    ).then_inc(s_const, 1)
            pool.wait_ge(s_bbe, 1)
            for b in range(NB):
                pool.wait_ge(s_aa, b + 1)
                if b >= 2:
                    pool.wait_ge(s_d2, b - 1)
                nc.gpsimd.tensor_tensor(
                    absum[:, b % 2, :].rearrange("c (s j) -> c s j", j=NJ),
                    aa[:, b, :].unsqueeze(2).broadcast_to([C, NS, NJ]),
                    bbB[:, b * NJ:(b + 1) * NJ].unsqueeze(1).broadcast_to([C, NS, NJ]), ALU.add).then_inc(s_ab, 1)
            pool.wait_ge(s_const, 3)
            three = lambda a: a.rearrange("p (t c) -> p t c", c=C)

            def where_to(k):
                pool.wait_ge(s_sgn, k + 1)
                nc.gpsimd.tensor_tensor(three(wk[k % 2][2][:, :]), view(twice1[:, :], [[0, TB], [1, C]]),
                                        three(wk[k % 2][0][:, :]), ALU.add).then_inc(s_where, 1)

            for k in range(NTB):
                if k >= 1:
                    where_to(k - 1)
                pool.wait_ge(s_scan, TB * (k + 1))
                if k >= 2:
                    pool.wait_ge(s_jump, TB * (k - 1))
                t = k * TB
                nc.gpsimd.tensor_tensor(three(wk[k % 2][0][:, :]), R_slot(t, TB, 1, C), R_slot(t, TB, 0, C),
                                        ALU.subtract).then_inc(s_jin, 1)
                nc.gpsimd.tensor_tensor(
                    three(wk[k % 2][1][:, :]), R_slot(t + 1, TB, 0, C),
                    three(mring[:, (k % 2) * TB * C:(k % 2 + 1) * TB * C]), ALU.subtract).then_inc(s_jin, 1)
            where_to(NTB - 1)
            for n in range(NKP + 1):
                if n == EARLY + 4:
                    pool.wait_ge(s_desk, 16 * LB)
                    nc.gpsimd.memset(keyn, 0.0).then_inc(s_keyz, 1)
                if n < NKP:
                    pool.wait_ge(s_kev, n + 1)
                    nc.gpsimd.tensor_tensor(kf[:, n % 3, :], kf[:, n % 3, :], kq[:, n % 4, 0, :], ALU.subtract
                                            ).then_inc(s_kr, 1)
                if n >= 1:
                    pool.wait_ge(s_k2, n)
                    m = n - 1
                    nc.gpsimd.tensor_tensor(kq[:, m % 4, 2, :], kf[:, m % 3, :], kq[:, m % 4, 1, :], ALU.subtract
                                            ).then_inc(s_ks, 1)
            s_t = s_tabs
            done2 = lambda ins: ins.then_inc(s_t, 1)
            pool.wait_ge(s_lane32, 1)
            done2(nc.gpsimd.tensor_scalar(mk[:, 0:1], l32[:, :], float(DH), None, ALU.is_lt))
            done2(nc.gpsimd.tensor_scalar(mk2[:, :], l32[:, :], float(2 * DH), None, ALU.is_lt))
            pool.wait_ge(s_t, 2)
            done2(nc.gpsimd.tensor_tensor(mk[:, 1:2], mk2[:, :], mk[:, 0:1], ALU.subtract))
            done2(nc.gpsimd.tensor_scalar(mku[:, :], mk2[:, :], -1.0, 1.0, ALU.mult, ALU.add))
            done2(nc.gpsimd.memset(bvAB[:, :], 0.0))
            pool.wait_ge(s_uT, 2)
            for r in range(4):
                pool.wait_ge(s_kd[r], 16 * NKP // 4)
            nc.gpsimd.iota(kiota, [[0, 2 * NHK], [1, NK]], base=-NK, channel_multiplier=0,
                           allow_small_or_imprecise_dtypes=True)
            pool.wait_ge(s_t, 5)
            nc.gpsimd.memset(WoAB, 0.0).then_inc(s_wz, 1)
            vt = vals[:, 0:NCH * NB * VW].rearrange("p (c g w) -> p c g w", g=VT, w=VTW)
            done2(nc.gpsimd.memset(vt[:, :, :, 2 * DH], 1.0))
            done2(nc.gpsimd.memset(vals[:, NCH * NB * VW:], 0.0))
            done2(nc.gpsimd.memset(vt[:, NCH - 1::NCH, 0, 0:32 - VTW], 0.0))
            pool.wait_ge(s_t, 8)
            done2(nc.gpsimd.memset(QP[NPR:P, :, :, :], 0.0))
            pool.wait_ge(s_t, 9)
            done2(nc.gpsimd.memset(sel, 0.0))
            done2(nc.gpsimd.memset(identb, 0.0))
            pool.wait_ge(s_t, 11)
            selv = sel.rearrange("p (t m) -> p t m", m=32)
            done2(nc.gpsimd.affine_select(out=selv, in_=selv, compare_op=ALU.not_equal, fill=1.0, base=-2 * DH,
                                          pattern=[[-32, 4], [0, 32]], channel_multiplier=1))
            done2(nc.gpsimd.affine_select(out=identb, in_=identb, compare_op=ALU.not_equal, fill=1.0, base=0,
                                          pattern=[[-1, P]], channel_multiplier=1))
            for t in range(4):
                pool.wait_ge(s_idx, t + 1)
                for h in range(NHK):
                    c = t * NHK + h
                    nc.gpsimd.indirect_dma_start(
                        out=gath[:, t, h, :], out_offset=None, in_=w_tab[:, :],
                        in_offset=bass.IndirectOffsetOnAxis(ap=idx[:, c:c + 1], axis=0)).then_inc(s_gath[t], 16)
            pool.wait_ge(s_t, 13)
            pool.wait_ge(s_vc, NCH // 4 * NB)
            nc.gpsimd.memset(ctxT[NPR:P, 0:2 * KPW], 1.0 + 0x3F80 / 2.0 ** 23).then_inc(s_one, 1)
            pool.wait_ge(s_otok, 4)
            pool.wait_ge(s_one, 1)
            nc.gpsimd.memset(kp_words[2][NPR:P, :], 1.0 + 0x3F80 / 2.0 ** 23).then_inc(s_one, 1)
            pool.wait_ge(s_one, 2)
            nc.gpsimd.iota(eiota[:, :, :], [[0, 4], [1, NE]], base=-NE, channel_multiplier=0,
                           allow_small_or_imprecise_dtypes=True).then_inc(s_et, 1)
            nc.gpsimd.memset(sele, 0.0).then_inc(s_et, 1)
            for part in range(3):
                pool.wait_ge(s_et, 2 + part)
                nc.gpsimd.affine_select(out=sele, in_=sele, compare_op=ALU.not_equal, fill=1.0, base=-part * NE,
                                        pattern=[[-1, NE], [0, P]], channel_multiplier=1).then_inc(s_et, 1)
            pool.wait_ge(s_t, 13)
            steps = 0

            def step(ins):
                nonlocal steps
                steps += 1
                ins.then_inc(s_nst, 1)
                pool.wait_ge(s_nst, steps)

            half = lambda i: nd[:, i, :]
            for b in range(NB - 1):
                pool.wait_ge(s_dnc, b + 1)
                step(nc.gpsimd.tensor_tensor(
                    masked[:, :].rearrange("p (x m q) -> p x m q", m=2, q=NJ),
                    both.rearrange("p (x m q) -> p x m q", m=2, q=NJ),
                    mk[:, :].unsqueeze(1).unsqueeze(3).broadcast_to([P, 4, 2, NJ]), ALU.mult))
                m4 = masked[:, :].rearrange("p (x m q) -> p x m q", m=2, q=NJ)
                step(nc.gpsimd.tensor_tensor(nd[:, :, :].rearrange("p i (a q) -> p (i a) q", a=2),
                                             m4[:, :, 0, :], m4[:, :, 1, :], ALU.add))
                nc.gpsimd.tensor_tensor(half(1), half(1), mku[:, 0:1].broadcast_to([P, 2 * NJ]), ALU.add
                                        ).then_inc(s_ndm, 1)
                pool.wait_ge(s_rcp, b + 1)
                step(nc.gpsimd.tensor_tensor(half(0), half(0), half(1), ALU.mult))
                nc.gpsimd.tensor_tensor(OAB[:, :, b * NJ:(b + 1) * NJ], half(0).rearrange("p (a q) -> p a q", a=2),
                                        bvAB[:, :].unsqueeze(2).broadcast_to([P, 2, NJ]), ALU.add
                                        ).then_inc(s_ob, 1)

        @block.scalar
        def _(act):
            act.dma_start(g4[:, 0:2], bass.AP(tensor=g_xattn.tensor, offset=0, ap=[[0, P], [1, 2]])
                          ).then_inc(s_small, 16)
            act.dma_start(g4[:, 2:4], bass.AP(tensor=g_ffn.tensor, offset=0, ap=[[0, P], [1, 2]])
                          ).then_inc(s_small, 16)
            act.wait_ge(s_small, 32)
            nc.scalar.activation(gt[:, :], g4[:, :], ACT.Tanh).then_inc(s_gate, 1)
            act.wait_ge(s_xT, 1)
            nc.scalar.activation(xT[:, :], ps[0][:, 0:TOK], ACT.Copy).then_inc(s_xTe, 1)

            def first_pieces(b):
                for n in range(NPIECE - 1):
                    act.wait_ge(s_ct, NPIECE * b + n + 1)
                    nc.scalar.activation(ctxT[:, b * NI + n * PIECE:b * NI + (n + 1) * PIECE],
                                         ps[1 + n][:, 0:PIECE], ACT.Copy).then_inc(s_ctA, 1)

            def squares(b):
                act.wait_ge(s_nat[b], 16)
                if b >= 1:
                    act.wait_ge(s_aa, b)
                nc.scalar.activation(sq[:, :], nat[:, b % RING, :, :].rearrange("c s d -> c (s d)"), ACT.Square
                                     ).then_inc(s_sq, 1)

            def dist_of(b):
                act.wait_ge(s_d2, b + 1)
                nc.scalar.activation(view(dist[:, :], [[JW, NS], [1, NJ]], b * BS + PADJ),
                                     dtmp[:, :].rearrange("c (s j) -> c s j", j=NJ), ACT.Sqrt
                                     ).then_inc(s_dist, 1)

            first_pieces(0)
            squares(0)
            first_pieces(1)
            act.wait_ge(s_var, 1)
            act.wait_ge(s_const, 3)
            nc.scalar.activation(rstd[:, :], ps[0][:, 0:TOK], ACT.Sqrt, bias=epsc[:, 0:1]).then_inc(s_std, 1)
            squares(1)
            for b in range(2, AHEAD):
                first_pieces(b)
                squares(b)
            for b in range(NB):
                dist_of(b)
                if b + AHEAD < NB:
                    first_pieces(b + AHEAD)
                    squares(b + AHEAD)

            def lane_distances(q):
                act.wait_ge(s_dt, q + 1)
                if q >= 2:
                    act.wait_ge(s_scan, DT_STEPS * (q - 1))
                nc.scalar.activation(dts[:, (q % 2) * PIECE:(q % 2 + 1) * PIECE], ps[q % 2][:, 0:PIECE],
                                     ACT.Copy).then_inc(s_dtc, 1)

            lane_distances(0)
            lane_distances(1)
            for k in range(NTB):
                if k + 2 < NTB:
                    lane_distances(k + 2)
                h, g = wk[k % 2][0], wk[k % 2][1]
                act.wait_ge(s_jin, 2 * k + 1)
                nc.scalar.activation(h[:, :], h[:, :], ACT.Sign, scale=-1.0).then_inc(s_act, 1)
                act.wait_ge(s_act, 2 * k + 1)
                nc.scalar.activation(h[:, :], h[:, :], ACT.Relu).then_inc(s_sgn, 1)
                act.wait_ge(s_jin, 2 * k + 2)
                nc.scalar.activation(g[:, :], g[:, :], ACT.Copy, scale=1.0e14, bias=1.0).then_inc(s_act, 1)
            act.wait_ge(s_jump, STEPS)
            act.wait_ge(s_wk, 16 * 4)

            def key_step(n):
                if n < NKP:
                    act.wait_ge(s_kp, n + 1)
                    if n >= 3:
                        act.wait_ge(s_ks, n - 2)
                    if n >= 4:
                        act.wait_ge(s_kd[n % 4], 16 * (n // 4))
                    bank = ps[KBANKS[n % 7]][:, 0:KPIECE]
                    nc.scalar.activation(kf[:, n % 3, :], bank, ACT.Identity, bias=cols[:, 1:2])
                    nc.scalar.activation(kq[:, n % 4, 0, :], bank, ACT.Identity, bias=cols[:, 1:2]
                                         ).then_inc(s_kev, 1)
                if 1 <= n <= NKP:
                    m = n - 1
                    act.wait_ge(s_kr, n)
                    nc.scalar.activation(kq[:, m % 4, 1, :], kf[:, m % 3, :], ACT.Copy).then_inc(s_k2, 1)
                if n >= 2:
                    m = n - 2
                    act.wait_ge(s_ks, n - 1)
                    i = m % KPB * KPIECE
                    act.dma_start(key_parts[m // KPB, :, :, i:i + KPIECE].rearrange("x p i -> p x i"),
                                  kq[:, m % 4, :, :]).then_inc(s_kd[m % 4], 16)

            BEFORE = 7
            for i in range(BEFORE):
                key_step(i)
            for k in range(NTB):
                act.wait_ge(s_carry, k + 1)
                nc.scalar.activation(jslot[:, k * TB * C:(k + 1) * TB * C].rearrange("p (t c) -> p t c", c=C),
                                     R_slot(k * TB, TB, 1, C), ACT.Copy, bias=-OFF).then_inc(s_j16, 1)
            for i in range(BEFORE, NKP + 2):
                key_step(i)

            def path_starts(g):
                for s in range(NS):
                    i = g * NS + s
                    if i >= A_RING:
                        act.wait_ge(s_pm, i - A_RING + 1)
                    nc.scalar.activation(Am[:, i % A_RING, :].rearrange("c (b j) -> c b j", j=NJ),
                                         EB[:, 2 * g:2 * g + 2, 0:NJ], ACT.Relu, scale=-1.0,
                                         bias=rowc21[:, s:s + 1]).then_inc(s_am, 1)

            def path_sums(g):
                act.wait_ge(s_ex, g + 1)
                for par in range(2):
                    nc.scalar.activation(U[64 * par:64 * par + NJ, g, :], ps[SUM_BANK[g]][64 * par:64 * par + NJ, 0:D],
                                         ACT.Copy).then_inc(s_u, 1)

            act.wait_ge(s_ebc, 1)
            path_starts(0)
            act.wait_ge(s_foldT, 1)
            nc.scalar.activation(wqT[:, 0:FOLD // 2], ps[1], ACT.Copy)
            nc.scalar.activation(wqT[:, FOLD // 2:], ps[2], ACT.Copy)
            nc.scalar.activation(keyT[:, :], ps[7], ACT.Copy).then_inc(s_foldc, 1)
            for g in range(1, NB // 2):
                path_starts(g)
            path_sums(0)
            path_sums(1)
            act.wait_ge(s_fold, 1)
            nc.scalar.activation(fold[:, :], ps[1], ACT.Copy).then_inc(s_fold_sb, 1)
            path_sums(2)
            path_sums(3)

            def deviation(k):
                lo, hi = LN_COLS[k]
                act.wait_ge(s_var, k + 1)
                nc.scalar.activation(rstd[:, lo:hi], ps[LN_BANK[k]][:, lo:hi], ACT.Sqrt, bias=epsc[:, 0:1]
                                     ).then_inc(s_std, 1)

            for part, tiles in enumerate(TILES):
                deviation(1 + part)
                act.wait_ge(s_xnk, part + 1)
                t0, t1 = tiles[0], tiles[-1] + 1
                nc.scalar.activation(x_tok[:, t0:t1, :], ps[4 + part][0:TT, t0 * D:t1 * D].rearrange(
                    "p (t d) -> p t d", d=D), ACT.Copy).then_inc(s_xnc, 1)
            act.wait_ge(s_tabs, 13)

            GELU_AT = (8, 15)

            def gelu(t):
                act.wait_ge(s_hcol, t + 1)
                nc.scalar.activation(hcol[:, t, :], hcol[:, t, :], ACT.Gelu).then_inc(s_gelu, 1)

            for b in range(NB):
                for i in range(NCH // 4):
                    n = b * (NCH // 4) + i
                    act.wait_ge(s_vp, n + 1)
                    tail = NI - (NCH - 1) * P if i == NCH // 4 - 1 else P
                    for r, c0, c1 in ((P, 0, 4),) if tail == P else ((P, 0, 3), (tail, 3, 4)):
                        dst = vals[0:r, (b * NCH + 4 * i + c0) * VW:(b * NCH + 4 * i + c1) * VW].rearrange(
                            "p (c g w) -> p c g w", g=VT, w=VTW)
                        last = nc.scalar.activation(
                            dst[:, :, :, 0:2 * DH],
                            ps[4 + n % 2][0:r, c0 * D:c1 * D].rearrange("p (c g w) -> p c g w", g=VT, w=2 * DH),
                            ACT.Copy)
                    last.then_inc(s_vc, 1)
                    if n in GELU_AT:
                        gelu(GELU_AT.index(n))
            gelu(2)
            gelu(3)
            deviation(3)
            deviation(4)

            def maxima_rows(b):
                act.wait_ge(s_nmt, b + 1)
                nc.scalar.activation(QP[NPR:NPR + 3, :, b, :], maxrows[b % 2], ACT.Copy).then_inc(s_nmc, 1)

            def head_sums(b):
                act.wait_ge(s_pv, NCH * (b + 1))
                if b >= 1:
                    act.wait_ge(s_ob, b)
                nc.scalar.activation(Osb.rearrange("p a m q -> p (a m q)"), ps[6 + b % 2][:, 0:4 * NJ], ACT.Copy
                                     ).then_inc(s_oc, 1)

            def denominators(b):
                act.wait_ge(s_den, b + 1)
                nc.scalar.activation(both[:, 4 * NJ:8 * NJ], ps[6 + b % 2][:, 256:256 + 4 * NJ], ACT.Copy
                                     ).then_inc(s_dnc, 1)

            maxima_rows(0)
            for b in range(NB):
                for c in range(NCH):
                    if c == 4 and b >= 1:
                        denominators(b - 1)
                    g = b * NCH + c
                    rows = min(P, NI - c * P)
                    act.wait_ge(s_s2, g + 1)
                    if g >= 2:
                        act.wait_ge(s_pv, g - 1)
                    nc.scalar.activation(
                        Pt[0:rows, g % 2, :].rearrange("p (a n) -> p a n", a=2),
                        banks[0:rows, 2 + 2 * (g % 2):4 + 2 * (g % 2), 0:HQ // 2], ACT.Exp,
                        scale=float(DH) ** -0.5).then_inc(s_exp, 1)
                    if c == 1 and b >= 1:
                        head_sums(b - 1)
                    if c == MAXROW_AT and b + 1 < NB:
                        maxima_rows(b + 1)
            head_sums(NB - 1)
            deviation(5)
            deviation(6)
            def hidden(i):
                act.wait_ge(s_h, i + 1)
                if i >= 4:
                    act.wait_ge(s_yu, i - 3)
                nc.scalar.activation(hT[:, i % 4, :], ps[5 + i % 2][:, 0:TOK], ACT.Relu, bias=b1s[:, i:i + 1]
                                     ).then_inc(s_hc, 1)

            hidden(0)
            hidden(1)
            act.wait_ge(s_lgd, 1)
            nc.scalar.activation(rs[:, 5, :], rs[:, 4, :], ACT.Exp).then_inc(s_lge, 1)
            hidden(2)
            hidden(3)
            act.wait_ge(s_wtT, 1)
            nc.scalar.activation(wT, ps[2].bitcast(BF16)[0:3 * NE, 0:TOK], ACT.Copy).then_inc(s_wtc, 1)
            for e in range(NE):
                if e + 1 < NE:
                    hidden(FC * (e + 1))
                act.wait_ge(s_wb, e + 1)
                if e >= 2:
                    act.wait_ge(s_yc, e - 1)
                nc.scalar.activation(wBs[:, e % 2, :], ps[3 + e % 2][:, 0:TOK], ACT.Copy).then_inc(s_wbc, 1)
                if e + 1 < NE:
                    for i in range(1, FC):
                        hidden(FC * (e + 1) + i)
            act.wait_ge(s_fT, 1)
            nc.scalar.activation(x_tok[:, :, :], ps[1][0:TT, :].rearrange("p (t d) -> p t d", d=D), ACT.Copy
                                 ).then_inc(s_fc, 1)

        @block.vector
        def _(ve):
            n = 0

            def link(ins):
                nonlocal n
                n += 1
                ins.then_inc(s_dve, 1)
                ve.wait_ge(s_dve, n)

            nc.vector.memset(meanw[:, :], 1.0 / D)
            nc.vector.memset(ones[:, :], 1.0)
            nc.vector.memset(epsc[:, :], EPS)
            nc.vector.memset(e_last[:, :], 2.0 * (NI - 1) - OFF)
            nc.vector.memset(view(dist[:, :], [[BS, NB], [JW, NS], [1, PADJ]]), BIG)
            nc.vector.memset(view(dist[:, :], [[BS, NB], [1, BS - NS * JW]], NS * JW), BIG)
            nc.vector.memset(dist[:, NB * BS:NB * BS + P], BIG)
            link(nc.vector.memset(gate[:, :], 1.0))
            nc.vector.memset(pad0[:, :], 0.0).then_inc(s_const, 1)
            ve.wait_ge(s_pool, 6)
            link(nc.vector.tensor_scalar(lane_i[:, :], pidx[:, :], LB - 1, None, ALU.bitwise_and))
            nc.vector.tensor_scalar(rowc21[:, :], rowc2[:, :], 1.0, None, ALU.add)
            link(nc.vector.tensor_copy(lane[:, :], lane_i[:, :]))
            link(nc.vector.tensor_scalar(lane_i[:, :], pidx[:, :], 31, None, ALU.bitwise_and))
            nc.vector.tensor_copy(l32[:, :], lane_i[:, :]).then_inc(s_lane32, 1)
            ve.wait_ge(s_lane32, 1)
            link(nc.vector.tensor_scalar(lane_i[:, :], pidx[:, :], DH, None, ALU.bitwise_and))
            link(nc.vector.tensor_copy(hm[:, 0:1], lane_i[:, :]))
            link(nc.vector.tensor_scalar(hm[:, 1:2], hm[:, 0:1], 0.0, None, ALU.is_gt))
            link(nc.vector.tensor_scalar(hm[:, 0:1], hm[:, 1:2], 0.0, None, ALU.is_equal))
            for i in range(4):
                nc.vector.tensor_scalar(lmask[:, i:i + 1], lane[:, :], float(1 << i), None, ALU.is_ge)
            nc.vector.memset(view(gate[:, :], [[SLOT, TB], [1, 1]]), 0.0)
            link(nc.vector.memset(R[:, 0:SLOT], BIG))
            link(nc.vector.tensor_scalar(R[:, 0:1], lane[:, :], 0.0, BIG, ALU.is_gt, ALU.mult))
            nc.vector.scalar_tensor_tensor(out=twice[:, :], in0=lane[:, 0:1].broadcast_to([P, 2 * C]),
                                           scalar=2.0 * C, in1=twice[:, :], op0=ALU.mult, op1=ALU.add
                                           ).then_inc(s_dve, 1)
            n += 1
            ve.wait_ge(s_dve, n)
            nc.vector.tensor_scalar(twice1[:, :], view(twice[:, :], [[2, C]]), -1.0, None, ALU.add
                                    ).then_inc(s_const, 1)
            ve.wait_ge(s_const, 3)
            nc.vector.tensor_scalar(twice[:, :], twice[:, :], -OFF, None, ALU.add)
            nc.vector.tensor_copy(blk16[:, :], blk[:, :]).then_inc(s_blk, 1)

            def centre(k):
                lo, hi = LN_COLS[k]
                ve.wait_ge(s_mean, k + 1)
                link(nc.vector.tensor_tensor(xc[:, lo:hi], xT[:, lo:hi], ps[LN_BANK[k]][:, lo:hi], ALU.subtract))
                nc.vector.tensor_tensor(xsq[:, lo:hi], xc[:, lo:hi], xc[:, lo:hi], ALU.mult).then_inc(s_cen, 1)

            def scale(k):
                lo, hi = LN_COLS[k]
                ve.wait_ge(s_std, k + 1)
                link(nc.vector.reciprocal(rstd[:, lo:hi], rstd[:, lo:hi]))
                nc.vector.tensor_tensor(xnT[:, lo:hi], xc[:, lo:hi], rstd[:, lo:hi], ALU.mult).then_inc(s_xn, 1)

            def row_squares(b):
                ve.wait_ge(s_sq, b + 1)
                nc.vector.tensor_reduce(aa[:, b, :], sq[:, :].rearrange("c (s d) -> c s d", d=D), AX_X, ALU.add
                                        ).then_inc(s_aa, 1)

            def last_piece(b):
                ve.wait_ge(s_ct, NPIECE * (b + 1))
                nc.vector.tensor_copy(ctxT[:, b * NI + 2 * PIECE:(b + 1) * NI], ps[3][:, 0:PIECE]
                                      ).then_inc(s_ctV, 1)

            last_piece(0)
            centre(0)
            last_piece(1)
            row_squares(0)
            ve.wait_ge(s_std, 1)
            for k, (lo, hi) in enumerate(((0, NJ), (NJ, TOK))):
                link(nc.vector.reciprocal(rstd[:, lo:hi], rstd[:, lo:hi]))
                link(nc.vector.tensor_tensor(xnT[:, lo:hi], xc[:, lo:hi], rstd[:, lo:hi], ALU.mult))
                nc.vector.tensor_scalar(xm2[:, lo:hi], xnT[:, lo:hi], -2.0, None, ALU.mult).then_inc(s_xm, 1)
            nc.vector.tensor_tensor(xsq[:, :], xnT[:, :], xnT[:, :], ALU.mult).then_inc(s_cen, 1)
            last_piece(2)
            row_squares(1)
            ve.wait_ge(s_bb, 1)
            nc.vector.tensor_copy(bbB[:, :], ps[0][0:C, 0:TOK]).then_inc(s_bbe, 1)

            def d2_of(b):
                ve.wait_ge(s_dot, b + 1)
                ve.wait_ge(s_ab, b + 1)
                if b >= 1:
                    ve.wait_ge(s_dist, b)
                for part, (lo, hi) in enumerate(((0, 8), (8, NS))):
                    bank = ps[4 + 2 * (b % 2) + part]
                    last = nc.vector.tensor_tensor(dtmp[:, lo * NJ:hi * NJ], bank[0:C, 0:(hi - lo) * NJ],
                                                   absum[:, b % 2, lo * NJ:hi * NJ], ALU.add)
                link(last)
                nc.vector.tensor_scalar(dtmp[:, :], dtmp[:, :], 0.0, None, ALU.max).then_inc(s_d2, 1)

            for b in range(NB):
                d2_of(b)
                if b + AHEAD < NB:
                    last_piece(b + AHEAD)
                if b + AHEAD <= NB:
                    row_squares(b + AHEAD - 1)

            def memory_layer():
                def add_alignment(part):
                    t0, t1 = TILES[part][0], TILES[part][-1] + 1
                    ve.wait_ge(s_uT, part + 1)
                    x4 = xT[:, :].rearrange("p (t a j) -> p t a j", a=2, j=NJ)[:, t0:t1, :, :]
                    nc.vector.scalar_tensor_tensor(
                        out=x4, in0=ps[(3, 6)[part]][:, :].rearrange("p (t a j) -> p t a j", a=2, j=64)[
                            :, t0:t1, :, 0:NJ], scalar=gt[:, 0:1], in1=x4, op0=ALU.mult, op1=ALU.add
                        ).then_inc(s_xr, 1)
                    ve.wait_ge(s_xr, part + 1)

                def choose(t):
                    ve.wait_ge(s_sim, t + 1)
                    sims = ps[t][0:TT, :].rearrange("p (g k) -> p g k", k=NK)
                    eq = prod[0:TT, 0:2 * NHK * NK]
                    eq3 = eq.rearrange("p (g k) -> p g k", k=NK)
                    link(nc.vector.tensor_reduce(mxs[:, t, :], sims, AX_X, ALU.max))
                    link(nc.vector.tensor_tensor(eq3, sims, mxs[:, t, :].unsqueeze(2).broadcast_to(
                        [TT, 2 * NHK, NK]), ALU.is_equal))
                    link(nc.vector.tensor_tensor(eq, eq, kiota, ALU.mult))
                    link(nc.vector.tensor_reduce(ixs[:, t, :], eq3, AX_X, ALU.min))
                    link(nc.vector.scalar_tensor_tensor(out=idxf[:, t, :], in0=ixs[:, t, 0:NHK], scalar=float(NK),
                                                        in1=ixs[:, t, NHK:], op0=ALU.mult, op1=ALU.add))
                    nc.vector.tensor_scalar(idx[:, t * NHK:(t + 1) * NHK], idxf[:, t, :], float(NK * NK + NK), None,
                                            ALU.add).then_inc(s_idx, 1)

                add_alignment(0)
                centre(1)
                add_alignment(1)
                scale(1)
                ve.wait_ge(s_wz, 1)
                choose(0)
                centre(2)
                scale(2)
                for t in range(1, 4):
                    choose(t)
                link(nc.vector.tensor_tensor(score[:, :, :], mxs[:, :, 0:NHK], mxs[:, :, NHK:], ALU.add))
                link(nc.vector.tensor_scalar(score[:, :, :], score[:, :, :], 0.0, None, ALU.max))
                ve.wait_ge(s_xnc, 2)
                pr = prod[0:TT, :].rearrange("p (h d) -> p h d", d=D)

                def down(t):
                    ve.wait_ge(s_gath[t], 16 * NHK)
                    link(nc.vector.tensor_tensor(pr, gath[:, t, :, 0:D], x_tok[:, t, :].unsqueeze(1).broadcast_to(
                        [TT, NHK, D]), ALU.mult))
                    nc.vector.tensor_reduce(hcol[:, t, :], pr, AX_X, ALU.add).then_inc(s_hcol, 1)
                    ve.wait_ge(s_hcol, t + 1)

                def up(t):
                    ve.wait_ge(s_gelu, t + 1)
                    link(nc.vector.tensor_tensor(hcol[:, t, :], hcol[:, t, :], score[:, t, :], ALU.mult))
                    link(nc.vector.tensor_tensor(pr, gath[:, t, :, D:], hcol[:, t, :].unsqueeze(2).broadcast_to(
                        [TT, NHK, D]), ALU.mult))
                    nc.vector.tensor_reduce(x_tok[:, t, :], view(prod[0:TT, :], [[1, D], [D, NHK]]), AX_X, ALU.add
                                            ).then_inc(s_otok, 1)
                    ve.wait_ge(s_otok, t + 1)

                def add_memory(part):
                    lo, hi = LN_COLS[3 + part]
                    ve.wait_ge(s_oT, part + 1)
                    nc.vector.scalar_tensor_tensor(out=xT[:, lo:hi], in0=ps[(1, 6)[part]][:, lo:hi], scalar=gt[:, 2:3],
                                                   in1=xT[:, lo:hi], op0=ALU.mult, op1=ALU.add).then_inc(s_xr, 1)
                    ve.wait_ge(s_xr, 3 + part)

                for t in range(3):
                    down(t)
                    up(t)
                add_memory(0)
                down(3)
                centre(3)
                up(3)
                add_memory(1)
                centre(4)
                scale(3)
                scale(4)

            def attention_layer():
                ve.wait_ge(s_q, 2)
                q4 = Qm.rearrange("p (b a q) -> p b a q", b=NB, a=2)
                q1 = ps[2][:, 0:TOK].rearrange("p (b q) -> p b q", q=NJ)
                nc.vector.tensor_scalar(q4[:, :, 0, :], q1, cols[:, 0:1], hm[:, 0:1], ALU.add, ALU.mult)
                link(nc.vector.tensor_scalar(q4[:, :, 1, :], q1, cols[:, 0:1], hm[:, 1:2], ALU.add, ALU.mult))
                nc.vector.tensor_copy(QS[:, 0, :], Qm).then_inc(s_qs, 1)
                ve.wait_ge(s_qs, 1)
                link(nc.vector.tensor_tensor(Qm, Qm, QS[:, 0, :], ALU.subtract))
                nc.vector.tensor_copy(QS[:, 1, :], Qm).then_inc(s_qs, 1)
                ve.wait_ge(s_qs, 2)
                nc.vector.tensor_tensor(QS[:, 2, :], Qm, QS[:, 1, :], ALU.subtract).then_inc(s_qs, 1)

                def reduce_scores(b, u):
                    k = b * UNITS + u
                    ve.wait_ge(s_s1, k + 1)
                    nc.vector.tensor_reduce(mx3[:, b % 2, u // NPIECE, u % NPIECE:u % NPIECE + 1],
                                            ps[k % (6 if b == 0 else 2)][0:2 * NJ, 0:PIECE], AX_X, ALU.max
                                            ).then_inc(s_mx, 1)

                def split_maxima(b, step):
                    if step == 0:
                        ve.wait_ge(s_mx, UNITS * (b + 1))
                        chained(nc.vector.tensor_reduce(nmx[:, :], mx3[:, b % 2, :, :], AX_X, ALU.max))
                    elif step == 1:
                        chained(nc.vector.tensor_scalar(nmx[:, :], nmx[:, :], -1.0, None, ALU.mult))
                    elif step in (2, 4, 6):
                        if step == 2 and b >= 1:
                            ve.wait_ge(s_nmt, b)
                        ins = nc.vector.tensor_copy(npart[:, :, step // 2 - 1], nmx[:, :])
                        if step == 6:
                            ins.then_inc(s_np, 1)
                        else:
                            chained(ins)
                    else:
                        chained(nc.vector.tensor_tensor(nmx[:, :], nmx[:, :], npart[:, :, step // 2 - 1],
                                                        ALU.subtract))

                def invert(b):
                    ve.wait_ge(s_ndm, b + 1)
                    nc.vector.reciprocal(nd[:, 1, :], nd[:, 1, :]).then_inc(s_rcp, 1)

                def normalize(b, step):
                    den = ps[6 + b % 2][:, 256:256 + 4 * NJ].rearrange("p (a m q) -> p a m q", a=2, m=2)
                    two = lambda i: nd[:, i, :].rearrange("p (a q) -> p a q", a=2)
                    if step == 0:
                        ve.wait_ge(s_den, b + 1)
                        nc.vector.tensor_scalar(num[:, 0, :, :], Osb[:, :, 0, :], mk[:, 0:1], None, ALU.mult)
                        chained(nc.vector.tensor_scalar(num[:, 1, :, :], den[:, :, 0, :], mk[:, 0:1], mku[:, 0:1],
                                                        ALU.mult, ALU.add))
                    elif step == 1:
                        for i, src in enumerate((Osb, den)):
                            last = nc.vector.scalar_tensor_tensor(
                                out=two(i), in0=src[:, :, 1, :], scalar=mk[:, 1:2], in1=num[:, i, :, :],
                                op0=ALU.mult, op1=ALU.add)
                        chained(last)
                    elif step == 2:
                        chained(nc.vector.reciprocal(nd[:, 1, :], nd[:, 1, :]))
                    elif step == 3:
                        chained(nc.vector.tensor_tensor(two(0), two(0), two(1), ALU.mult))
                    else:
                        nc.vector.tensor_tensor(OAB[:, :, b * NJ:(b + 1) * NJ], two(0),
                                                bvAB[:, :].unsqueeze(2).broadcast_to([P, 2, NJ]), ALU.add
                                                ).then_inc(s_ob, 1)

                def chained(ins):
                    nonlocal n
                    n += 1
                    ins.then_inc(s_dve, 1)

                for u in range(UNITS):
                    reduce_scores(0, u)
                for step in range(7):
                    ve.wait_ge(s_dve, n)
                    split_maxima(0, step)
                for k in range(UNITS, NB * UNITS):
                    b, u = k // UNITS, k % UNITS
                    reduce_scores(b, u)
                    if b >= 2 and u < 4:
                        for step in range(2 * u, min(2 * u + 2, 7)):
                            ve.wait_ge(s_dve, n)
                            split_maxima(b - 1, step)
                    if b >= 2 and u == 22:
                        invert(b - 2)
                for step in range(7):
                    ve.wait_ge(s_dve, n)
                    split_maxima(NB - 1, step)
                def add_attention(part):
                    lo, hi = LN_COLS[5 + part]
                    ve.wait_ge(s_wo, part + 1)
                    link(nc.vector.tensor_scalar(xc[:, lo:hi], ps[1][:, lo:hi], cols[:, 2:3], None, ALU.add))
                    nc.vector.scalar_tensor_tensor(out=xT[:, lo:hi], in0=xc[:, lo:hi], scalar=gt[:, 1:2],
                                                   in1=xT[:, lo:hi], op0=ALU.mult, op1=ALU.add).then_inc(s_xr, 1)
                    ve.wait_ge(s_xr, 5 + part)

                invert(NB - 2)
                add_attention(0)
                centre(5)
                ve.wait_ge(s_np, NB)
                ve.wait_ge(s_ob, NB - 1)
                for step in range(5):
                    ve.wait_ge(s_dve, n)
                    normalize(NB - 1, step)
                add_attention(1)
                centre(6)
                scale(5)
                scale(6)

            def expert_layer():
                ve.wait_ge(s_lg, 1)
                ve.wait_ge(s_et, 1)
                e4 = lambda i: lg[:, i, :].rearrange("p (t e) -> p t e", e=NE)
                wide = lambda a: a.unsqueeze(2).broadcast_to([TT, 4, NE])
                link(nc.vector.tensor_tensor(e4(0), ps[1][0:TT, TOK:TOK + 4 * NE].rearrange("p (t e) -> p t e", e=NE),
                                             brB[:, :].unsqueeze(1).broadcast_to([TT, 4, NE]), ALU.add))
                for i in range(2):
                    link(nc.vector.tensor_reduce(rs[:, i, :], e4(0), AX_X, ALU.max))
                    link(nc.vector.tensor_tensor(e4(3), e4(0), wide(rs[:, i, :]), ALU.is_equal))
                    link(nc.vector.tensor_tensor(e4(3), e4(3), eiota[:, :, :], ALU.mult))
                    link(nc.vector.tensor_reduce(rs[:, 2 + i, :], e4(3), AX_X, ALU.min))
                    link(nc.vector.tensor_tensor(e4(1 + i), eiota[:, :, :], wide(rs[:, 2 + i, :]), ALU.is_equal))
                    if i == 0:
                        link(nc.vector.scalar_tensor_tensor(out=lg[:, 0, :], in0=lg[:, 1, :], scalar=-3.0e38,
                                                            in1=lg[:, 0, :], op0=ALU.mult, op1=ALU.add))
                nc.vector.tensor_tensor(rs[:, 4, :], rs[:, 1, :], rs[:, 0, :], ALU.subtract).then_inc(s_lgd, 1)
                ve.wait_ge(s_lge, 1)
                link(nc.vector.tensor_scalar(rs[:, 6, :], rs[:, 5, :], 1.0, None, ALU.add))
                link(nc.vector.reciprocal(rs[:, 7, :], rs[:, 6, :]))
                link(nc.vector.tensor_tensor(e4(2), e4(2), wide(rs[:, 5, :]), ALU.mult))
                link(nc.vector.tensor_tensor(lg[:, 1, :], lg[:, 1, :], lg[:, 2, :], ALU.add))
                link(nc.vector.tensor_tensor(e4(4), e4(1), wide(rs[:, 7, :]), ALU.mult))
                for part in range(3):
                    piece = wparts[:, :, part * NE:(part + 1) * NE]
                    ins = nc.vector.tensor_copy(piece, e4(4))
                    if part == 2:
                        ins.then_inc(s_rw, 1)
                    else:
                        link(ins)
                        link(nc.vector.tensor_tensor(e4(4), e4(4), piece, ALU.subtract))
                for e in range(NE):
                    ve.wait_ge(s_yu, FC * (e + 1))
                    ve.wait_ge(s_wbc, e + 1)
                    dst = xsq if e == 0 else xc
                    ins = nc.vector.scalar_tensor_tensor(
                        out=dst[:, :], in0=ps[7 if e % 2 else 0][:, 0:TOK], scalar=b2s[:, e:e + 1],
                        in1=wBs[:, e % 2, :], op0=ALU.add, op1=ALU.mult)
                    ins.then_inc(s_yc, 1)
                    ve.wait_ge(s_yc, e + 1)
                    if e:
                        link(nc.vector.tensor_tensor(xsq[:, :], xsq[:, :], xc[:, :], ALU.add))
                nc.vector.scalar_tensor_tensor(out=xT[:, :], in0=xsq[:, :], scalar=gt[:, 3:4], in1=xT[:, :],
                                               op0=ALU.mult, op1=ALU.add).then_inc(s_xr, 1)

            shift = [LB - 1] + list(range(LB - 1)) + [2 * LB - 1] + list(range(LB, 2 * LB - 1))

            def leaves_column(i):
                h, g, _ = wk[i // TB % 2]
                o = i % TB * C
                nc.vector.tensor_tensor(g[:, o:o + C], g[:, o:o + C], h[:, o:o + C], ALU.is_gt).then_inc(s_leave, 1)

            def jump_of(i):
                _, g, w = wk[i // TB % 2]
                o = i % TB * C
                if i % TB == 0:
                    ve.wait_ge(s_where, i // TB + 1)
                ve.wait_ge(s_leave, i + 1)
                nc.vector.tensor_tensor(R_slot(i, 1, 1, C), g[:, o:o + C], w[:, o:o + C], ALU.mult).then_inc(s_jump, 1)

            def jumps(k):
                t = k * TB
                h, g, w = wk[k % 2]
                ve.wait_ge(s_act, 2 * k + 2)
                link(nc.vector.tensor_tensor(g[:, :], g[:, :], h[:, :], ALU.is_gt))
                ve.wait_ge(s_where, k + 1)
                nc.vector.tensor_tensor(R_slot(t, TB, 1, C), g[:, :].rearrange("p (t c) -> p t c", c=C),
                                        w[:, :].rearrange("p (t c) -> p t c", c=C), ALU.mult).then_inc(s_jump, TB)

            for t in range(STEPS):
                late = t - 2 * TB
                if late >= 0 and late % TB == 0:
                    ve.wait_ge(s_act, 2 * (late // TB) + 2)
                if late >= 1:
                    jump_of(late - 1)
                m = mring[:, (t % (2 * TB)) * C:(t % (2 * TB) + 1) * C]
                if t >= 1:
                    ve.wait_ge(s_scan, t)
                nc.vector.tensor_tensor(m, R_slot(t, 1, 1, C), R_slot(t, 1, 0, C), ALU.min)
                nc.vector.stream_shuffle(R_slot(t + 1, 1, 0, 1), R_slot(t, 1, C, 1), shift).then_inc(s_dve, 1)
                n += 1
                if late >= 0:
                    leaves_column(late)
                ve.wait_ge(s_dve, n)
                if t % DT_STEPS == 0:
                    ve.wait_ge(s_dtc, t // DT_STEPS + 1)
                d = dts[:, (t % (2 * DT_STEPS)) * C:(t % (2 * DT_STEPS) + 1) * C]
                nc.vector.tensor_tensor_scan(view(R, [[1, C]], (t + 1) * SLOT + 1), m, d,
                                             R[:, (t + 1) * SLOT:(t + 1) * SLOT + 1], ALU.min, ALU.add
                                             ).then_inc(s_scan, 1)
            jump_of(STEPS - 2 * TB - 1)
            jumps(NTB - 2)
            jumps(NTB - 1)
            ve.wait_ge(s_jump, STEPS)
            link(nc.vector.tensor_reduce(hops[:, 0, 0:STEPS], R_slot(0, STEPS, 1, C), AX_X, ALU.max))
            for i in range(4):
                k = 1 << i
                a, b_ = hops[:, i % 2, :], hops[:, (i + 1) % 2, :]
                mask = list(range(32))
                for h in range(2):
                    for s in range(LB):
                        mask[h * LB + s] = h * LB + (s - k if s >= k else s)
                nc.vector.tensor_copy(b_[:, 0:k], a[:, 0:k])
                link(nc.vector.stream_shuffle(shf[:, 0:STEPS - k], a[:, 0:STEPS - k], mask))
                link(nc.vector.scalar_tensor_tensor(out=b_[:, k:STEPS], in0=shf[:, 0:STEPS - k],
                                                    scalar=lmask[:, i:i + 1], in1=a[:, k:STEPS],
                                                    op0=ALU.mult, op1=ALU.max))
            mask = [LB - 1] + list(range(LB - 1)) + [2 * LB - 1] + list(range(LB, 2 * LB - 1))
            nc.vector.memset(R[:, 0:1], 0.0)
            link(nc.vector.stream_shuffle(shf[:, 0:STEPS - 1], hops[:, 0, 0:STEPS - 1], mask))
            link(nc.vector.tensor_scalar(view(R[:, :], [[SLOT, STEPS - 1], [1, 1]], SLOT),
                                         shf[:, 0:STEPS - 1].unsqueeze(2), lmask[:, 0:1], None, ALU.mult))
            for k in range(NTB):
                v = R[:, k * TB * SLOT:(k + 1) * TB * SLOT]
                nc.vector.tensor_tensor_scan(v, gate[:, :], v, 0.0, ALU.mult, ALU.max).then_inc(s_carry, 1)

            nc.vector.memset(zt, 0.0)
            nc.vector.memset(U, 0.0)
            ve.wait_ge(s_desk, 16 * LB)
            for j in range(NJ - 1, 0, -1):
                if j < NJ - 1:
                    ve.wait_ge(s_hop, NJ - 1 - j)
                e = e_last[:, 0:1] if j == NJ - 1 else ps[4][:, j + 1:j + 2]
                nc.vector.scalar_tensor_tensor(
                    out=mring[:, 6 * C:8 * C].rearrange("p (c k) -> p c k", k=2),
                    in0=twice[:, :].rearrange("p (c k) -> p c k", k=2), scalar=e,
                    in1=view(jcol, [[1, C], [0, 2]], j * C),
                    op0=ALU.is_equal, op1=ALU.mult, accum_out=acc[:, j:j + 1]).then_inc(s_hit, 1)
            ve.wait_ge(s_hop, NJ - 1)
            nc.vector.scalar_tensor_tensor(
                out=zt[:, :, 1:NJ], in0=ps[4][:, 1:NJ].unsqueeze(1).broadcast_to([P, NB, NJ - 1]), scalar=OFF,
                in1=first[:, :].unsqueeze(2).broadcast_to([P, NB, NJ - 1]), op0=ALU.add, op1=ALU.mult)
            nc.vector.tensor_scalar(zt[:, :, NJ:NJ + 1], first[:, :].unsqueeze(2), 2.0 * (NI - 1), None, ALU.mult
                                    ).then_inc(s_z, 1)
            ve.wait_ge(s_eb, 1)
            nc.vector.tensor_copy(EB[:, :, :], ps[4][0:C, NJ:NJ + NB * (NJ + 1)].rearrange(
                "c (b j) -> c b j", b=NB)).then_inc(s_ebc, 1)
            ve.wait_ge(s_ebc, 1)
            for i in range(NB // 2 * NS):
                g, s = i // NS, i % NS
                if s == 0 and g >= 2:
                    ve.wait_ge(s_ex, g - 1)
                ve.wait_ge(s_am, i + 1)
                nc.vector.scalar_tensor_tensor(
                    out=Pm[:, g % 2, s, :].rearrange("c (b j) -> c b j", j=NJ),
                    in0=EB[:, 2 * g:2 * g + 2, 1:NJ + 1], scalar=rowc2[:, s:s + 1],
                    in1=Am[:, i % A_RING, :].rearrange("c (b j) -> c b j", j=NJ), op0=ALU.is_ge, op1=ALU.min
                    ).then_inc(s_pm, 1)
            ve.wait_ge(s_gate, 1)
            memory_layer()
            attention_layer()
            expert_layer()

        @block.tensor
        def _(pe):
            pe.wait_ge(s_x, 16)
            pe.wait_ge(s_pool, 9)
            pe.wait_ge(s_const, 3)
            for t in range(4):
                last = nc.tensor.transpose(ps[0][:, t * TT:(t + 1) * TT], x_tok[:, t, :], ident[0:TT, 0:TT])
            last.then_inc(s_xT, 1)

            def mean_of(k):
                lo, hi = LN_COLS[k]
                nc.tensor.matmul(ps[LN_BANK[k]][:, lo:hi], meanw[:, :], xT[:, lo:hi], start=True, stop=True
                                 ).then_inc(s_mean, 1)

            def variance_of(k):
                lo, hi = LN_COLS[k]
                pe.wait_ge(s_cen, k + 1 + (k > 0))
                nc.tensor.matmul(ps[LN_BANK[k]][:, lo:hi], meanw[:, :], xsq[:, lo:hi], start=True, stop=True
                                 ).then_inc(s_var, 1)

            def dots(b):
                pe.wait_ge(s_ctA, (NPIECE - 1) * (b + 1))
                pe.wait_ge(s_ctV, b + 1)
                if b >= 2:
                    pe.wait_ge(s_d2, b - 1)
                for s in range(NS):
                    bank, o = (ps[4 + 2 * (b % 2)], s) if s < 8 else (ps[5 + 2 * (b % 2)], s - 8)
                    last = nc.tensor.matmul(bank[0:C, o * NJ:(o + 1) * NJ],
                                            ctxT[:, b * NI + s * C:b * NI + (s + 1) * C],
                                            xm2[:, b * NJ:(b + 1) * NJ], start=True, stop=True)
                last.then_inc(s_dot, 1)

            def context_rows(b):
                pe.wait_ge(s_nat[b], 16)
                for n in range(NPIECE):
                    if b >= 1:
                        if n < NPIECE - 1:
                            pe.wait_ge(s_ctA, (NPIECE - 1) * (b - 1) + n + 1)
                        else:
                            pe.wait_ge(s_ctV, b)
                    for i in range(SPP):
                        last = nc.tensor.transpose(ps[1 + n][:, i * C:(i + 1) * C],
                                                   nat[:, b % RING, n * SPP + i, :], ident[0:C, 0:C])
                    last.then_inc(s_ct, 1)

            pe.wait_ge(s_xTe, 1)
            mean_of(0)
            context_rows(0)
            context_rows(1)
            variance_of(0)
            context_rows(2)
            for b in range(NB):
                if b < 2:
                    pe.wait_ge(s_xm, b + 1)
                dots(b)
                if b == 0:
                    pe.wait_ge(s_cen, 2)
                    nc.tensor.matmul(ps[0][0:C, 0:TOK], ones[:, 0:C], xsq[:, :], start=True, stop=True
                                     ).then_inc(s_bb, 1)
                if b + AHEAD < NB:
                    context_rows(b + AHEAD)
            pe.wait_ge(s_dist, NB)
            pe.wait_ge(s_bbe, 1)
            for q in range(STEPS // DT_STEPS):
                if q >= 2:
                    pe.wait_ge(s_dtc, q - 1)
                for i in range(DT_STEPS):
                    t = q * DT_STEPS + i
                    src = view(dist[:, :], [[JW - 1, P]], t + PADJ)
                    last = nc.tensor.transpose(ps[q % 2][:, i * C:(i + 1) * C], src, ident[0:C, 0:C])
                last.then_inc(s_dt, 1)
            pe.wait_ge(s_wk, 16 * 4)

            def keys_of(n, lo, hi):
                if n >= 7 and lo == 0:
                    pe.wait_ge(s_kev, n - 6)
                ins = nc.tensor.matmul(ps[KBANKS[n % 7]][:, lo:hi], Wk_sb[:, :],
                                       ctxT[:, n * KPIECE + lo:n * KPIECE + hi], start=True, stop=True)
                if hi == KPIECE:
                    ins.then_inc(s_kp, 1)

            pe.wait_ge(s_dtc, NTB)
            pe.wait_ge(s_blk, 1)
            for n in range(EARLY):
                keys_of(n, 0, KPIECE)
            for j in range(NJ - 1, 0, -1):
                pe.wait_ge(s_hit, NJ - j)
                nc.tensor.matmul(ps[4][:, j:j + 1], blk16[:, :], acc[:, j:j + 1], start=True, stop=True
                                 ).then_inc(s_hop, 1)
                i = NJ - 1 - j
                if i < 3 * (NKP - EARLY):
                    keys_of(EARLY + i // 3, i % 3 * THIRD, (i % 3 + 1) * THIRD)
            pe.wait_ge(s_z, 1)
            nc.tensor.matmul(ps[4][0:C, NJ:NJ + NB * (NJ + 1)], ones[:, 0:C],
                             zt[:, :, :].rearrange("p b j -> p (b j)"), start=True, stop=True).then_inc(s_eb, 1)
            pe.wait_ge(s_keys, 16 * 5)
            pe.wait_ge(s_kev, NKP)
            for c in range(8):
                nc.tensor.transpose(ps[1 + c // 4][:, (c % 4) * P:(c % 4 + 1) * P], wq_sb[:, c * P:(c + 1) * P],
                                    ident[:, :])
            for c in range(8):
                last = nc.tensor.transpose(ps[7][:, c * 2 * NK:(c + 1) * 2 * NK], keyn[:, c, :],
                                           ident[0:2 * NK, 0:2 * NK])
            last.then_inc(s_foldT, 1)
            def sums(g, par):
                b = 2 * g + par
                if par == 0:
                    pe.wait_ge(s_pm, NS * (g + 1))
                pe.wait_ge(s_nat2[b], 16)
                for s in range(NS):
                    rows = nat[:, b, s, :] if b < RING else \
                        dist[:, ((b - RING) * NS + s) * D:((b - RING) * NS + s + 1) * D]
                    last = nc.tensor.matmul(ps[SUM_BANK[g]][64 * par:64 * par + NJ, 0:D],
                                            Pm[:, g % 2, s, par * NJ:(par + 1) * NJ], rows,
                                            start=(s == 0), stop=(s == NS - 1))
                if par == 1:
                    last.then_inc(s_ex, 1)

            def sums_transposed(part):
                pe.wait_ge(s_u, 2 * (TILES[part][-1] + 1))
                for t in TILES[part]:
                    last = nc.tensor.transpose(ps[(3, 6)[part]][:, t * P:(t + 1) * P], U[:, t, :], ident[:, :])
                last.then_inc(s_uT, 1)

            def tokens(part):
                pe.wait_ge(s_xn, 1 + part)
                for t in TILES[part]:
                    nc.tensor.matmul(ps[t][0:TT, :], xnT[:, t * TT:(t + 1) * TT], fold[:, :],
                                     start=True, stop=True).then_inc(s_sim, 1)
                for t in TILES[part]:
                    last = nc.tensor.transpose(ps[4 + part][0:TT, t * D:(t + 1) * D], xnT[:, t * TT:(t + 1) * TT],
                                               ident[:, :])
                last.then_inc(s_xnk, 1)

            sums(0, 0)
            sums(0, 1)
            sums(1, 0)
            sums(1, 1)
            pe.wait_ge(s_foldc, 1)
            for c in range(8):
                last = nc.tensor.matmul(ps[1][:, c * 2 * NK:(c + 1) * 2 * NK], wqT[:, c * P:(c + 1) * P],
                                        keyT[:, c * 2 * NK:(c + 1) * 2 * NK], start=True, stop=True)
            last.then_inc(s_fold, 1)
            sums(2, 0)
            sums(2, 1)
            sums(3, 0)
            sums_transposed(0)
            sums(3, 1)
            pe.wait_ge(s_xr, 1)
            mean_of(1)
            sums_transposed(1)
            variance_of(1)
            pe.wait_ge(s_xr, 2)
            mean_of(2)
            pe.wait_ge(s_fold_sb, 1)
            tokens(0)
            variance_of(2)
            tokens(1)
            pe.wait_ge(s_w, 16 * 22)
            pe.wait_ge(s_xnc, 2)
            for b in range(NB):
                for i in range(NCH // 4):
                    n = b * (NCH // 4) + i
                    if n >= 2:
                        pe.wait_ge(s_vc, n - 1)
                    for k in range(4):
                        c = 4 * i + k
                        rows = min(P, NI - c * P)
                        last = nc.tensor.matmul(ps[4 + n % 2][0:rows, k * D:(k + 1) * D],
                                                ctxT[:, b * NI + c * P:b * NI + c * P + rows], Wv_sb,
                                                start=True, stop=True)
                    last.then_inc(s_vp, 1)
            for part, tiles in enumerate(TILES):
                pe.wait_ge(s_otok, tiles[-1] + 1)
                for t in tiles:
                    last = nc.tensor.transpose(ps[(1, 6)[part]][:, t * TT:(t + 1) * TT], x_tok[:, t, :],
                                               ident[0:TT, 0:TT])
                last.then_inc(s_oT, 1)
                pe.wait_ge(s_xr, 3 + part)
                mean_of(3 + part)
                variance_of(3 + part)
            for part in range(2):
                lo, hi = LN_COLS[3 + part]
                pe.wait_ge(s_xn, 3 + part)
                nc.tensor.matmul(ps[2][:, lo:hi], Wq_sb, xnT[:, lo:hi], start=True, stop=True).then_inc(s_q, 1)
            pe.wait_ge(s_qp, 16 * len(PRODUCTS))
            pe.wait_ge(s_one, 1)
            pe.wait_ge(s_tabs, 13)

            def project_output(part):
                lo, hi = LN_COLS[5 + part]
                pe.wait_ge(s_ob, hi // NJ)
                for half in range(2):
                    last = nc.tensor.matmul(ps[1][:, lo:hi], WoAB[:, half, :], OAB[:, half, lo:hi],
                                            start=(half == 0), stop=(half == 1))
                last.then_inc(s_wo, 1)

            def row_scores(b, u):
                k = b * UNITS + u
                if u == 0:
                    pe.wait_ge(s_kpl[b % 3], 16 * len(PRODUCTS) * (b // 3 + 1))
                    if b == 2:
                        pe.wait_ge(s_one, 2)
                ring = 6 if b == 0 else 2
                if k >= ring:
                    pe.wait_ge(s_mx, k - ring + 1)
                nc.tensor.matmul(ps[k % ring][0:2 * NJ, 0:PIECE],
                                 QP[:, u // NPIECE, b, :],
                                 KP[b % 3][:, u // NPIECE, (u % NPIECE) * PIECE:(u % NPIECE + 1) * PIECE],
                                 start=True, stop=True).then_inc(s_s1, 1)

            def maxima_to_rows(b):
                pe.wait_ge(s_np, b + 1)
                if b >= 2:
                    pe.wait_ge(s_ob, b - 1)
                for pair in range(NH // 2):
                    last = nc.tensor.transpose(maxrows[b % 2][:, pair, :], npart[:, pair, :],
                                               identb[0:2 * NJ, 0:2 * NJ])
                last.then_inc(s_nmt, 1)

            def weigh_values(g):
                b, c = g // NCH, g % NCH
                rows = min(P, NI - c * P)
                pe.wait_ge(s_exp, g + 1)
                if c == 0 and b >= 2:
                    pe.wait_ge(s_ob, b - 1)
                for t in range(VT):
                    q, o = 32 * (t % 4), (t // 4) * 2 * NJ
                    v0 = (g * VT + t) * VTW
                    last = nc.tensor.matmul(ps[6 + b % 2][q:q + 32, o:o + 2 * NJ], vals[0:rows, v0:v0 + 32],
                                            Pt[0:rows, g % 2, 2 * t * NJ:2 * (t + 1) * NJ],
                                            start=(c == 0 and t < 4), stop=(c == NCH - 1),
                                            skip_group_check=True)
                last.then_inc(s_pv, 1)

            for u in range(UNITS):
                row_scores(0, u)
            maxima_to_rows(0)
            for b in range(NB):
                pe.wait_ge(s_nmc, b + 1)
                for c in range(NCH):
                    g = b * NCH + c
                    rows = min(P, NI - c * P)
                    if g >= 2:
                        pe.wait_ge(s_exp, g - 1)
                    ahead = UNITS + sum(BESIDE[:g])
                    units = [divmod(k, UNITS) for k in range(ahead, min(ahead + BESIDE[g], NB * UNITS))]
                    for m in range(NH // 2):
                        if m % 4 == 0 and len(units) > 1:
                            row_scores(*units.pop(0))
                        bank = ps[2 + 2 * (g % 2) + m // (NH // 4)]
                        o = m % (NH // 4) * 2 * NJ
                        last = nc.tensor.matmul(bank[0:rows, o:o + 2 * NJ],
                                                KP[b % 3][:, m, c * P:c * P + rows],
                                                QP[:, m, b, :], start=True, stop=True)
                    last.then_inc(s_s2, 1)
                    for unit in units:
                        row_scores(*unit)
                    if g >= 1:
                        weigh_values(g - 1)
                    if c == 3 and b >= 1:
                        pe.wait_ge(s_oc, b)
                        nc.tensor.matmul(ps[6 + (b - 1) % 2][:, 256:256 + 4 * NJ], sel,
                                         Osb.rearrange("p a m q -> p (a m q)"), start=True, stop=True
                                         ).then_inc(s_den, 1)
                    if c == MAXROW_AT and b + 1 < NB:
                        maxima_to_rows(b + 1)
                    if b == NB - 1 and c == 4:
                        pe.wait_ge(s_mx, NB * UNITS)
                        project_output(0)
                    if b == NB - 1 and c == 8:
                        pe.wait_ge(s_xr, 5)
                        mean_of(5)
                    if b == NB - 1 and c == 10:
                        variance_of(5)
            weigh_values(NB * NCH - 1)
            pe.wait_ge(s_oc, NB)
            nc.tensor.matmul(ps[6 + (NB - 1) % 2][:, 256:256 + 4 * NJ], sel,
                             Osb.rearrange("p a m q -> p (a m q)"), start=True, stop=True).then_inc(s_den, 1)
            project_output(1)
            pe.wait_ge(s_xr, 6)
            mean_of(6)
            variance_of(6)
            for t in range(4):
                pe.wait_ge(s_xn, 5 + t // 3)
                last = nc.tensor.matmul(ps[1][0:TT, TOK + t * NE:TOK + (t + 1) * NE], xnT[:, t * TT:(t + 1) * TT],
                                        Wr[:, :], start=True, stop=True)
            last.then_inc(s_lg, 1)
            pe.wait_ge(s_w12, 32)
            def hidden(i):
                e, c = i // FC, i % FC
                if i >= 2:
                    pe.wait_ge(s_hc, i - 1)
                nc.tensor.matmul(ps[5 + i % 2][:, 0:TOK], W1s[:, e, c * P:(c + 1) * P], xnT[:, :],
                                 start=True, stop=True).then_inc(s_h, 1)

            def output(i):
                e, c = i // FC, i % FC
                pe.wait_ge(s_hc, i + 1)
                if c == 0 and e >= 2:
                    pe.wait_ge(s_yc, e - 1)
                nc.tensor.matmul(ps[7 if e % 2 else 0][:, 0:TOK], W2s[:, i, :], hT[:, i % 4, :],
                                     start=(c == 0), stop=(c == FC - 1)).then_inc(s_yu, 1)

            hidden(0)
            hidden(1)
            for i in range(NE * FC):
                if i == FC - 2:
                    pe.wait_ge(s_rw, 1)
                    for t in range(4):
                        last = nc.tensor.transpose(ps[2].bitcast(BF16)[0:3 * NE, t * TT:(t + 1) * TT],
                                                   wparts[:, t, :], identb[0:TT, 0:TT])
                    last.then_inc(s_wtT, 1)
                if i % FC == FC - 1:
                    e = i // FC
                    if e == 0:
                        pe.wait_ge(s_wtc, 1)
                        pe.wait_ge(s_et, 5)
                    if e >= 2:
                        pe.wait_ge(s_wbc, e - 1)
                    nc.tensor.matmul(ps[3 + e % 2][:, 0:TOK], sele[:, e, :], wT, start=True, stop=True
                                     ).then_inc(s_wb, 1)
                if i + 2 < NE * FC:
                    hidden(i + 2)
                output(i)
            pe.wait_ge(s_xr, 7)
            for t in range(4):
                last = nc.tensor.transpose(ps[1][0:TT, t * D:(t + 1) * D], xT[:, t * TT:(t + 1) * TT],
                                           ident[:, :])
            last.then_inc(s_fT, 1)


_INS = ["x", "ctx_1024", "g_xattn", "g_ffn", "L0_ffn_w_q", "L0_ffn_keys", "w_tab",
        "L1_xattn_Wq", "L1_xattn_bq", "L1_xattn_Wk", "L1_xattn_bk", "L1_xattn_Wv", "L1_xattn_bv",
        "L1_xattn_Wo", "L1_xattn_bo", "L1_ffn_W_router", "L1_ffn_b_router", "L1_ffn_W1", "L1_ffn_b1",
        "L1_ffn_W2", "L1_ffn_b2"]


def kernel(**inputs):
    import numpy as np
    from concourse import bacc
    from concourse.bass_utils import run_bass_kernel_spmd

    nc = bacc.Bacc("TRN2", target_bir_lowering=False, num_devices=1)
    laid = dict(inputs)
    laid["w_tab"] = np.concatenate([np.asarray(inputs["L0_ffn_w_down"]), np.asarray(inputs["L0_ffn_w_up"])], axis=1)
    arrays, args = {}, []
    for name in _INS:
        a = np.ascontiguousarray(laid[name])
        arrays[f"in_{name}"] = a
        args.append(nc.dram_tensor(f"in_{name}", a.shape, mybir.dt.from_np(a.dtype), kind="ExternalInput").ap())
    shape = np.asarray(inputs["x"]).shape
    args.append(nc.dram_tensor("out_x", shape, mybir.dt.float32, kind="ExternalOutput").ap())
    build_gated_layers(nc, *args)
    r = run_bass_kernel_spmd(nc, [arrays], core_ids=[0])
    return r.results[0]["out_x"]
```
